# Optimizing a Trainium2 kernel written in Bass

```python
import numpy as np
import jax
import jax.numpy as jnp

def _softmax(x, axis=-1):
    return jax.nn.softmax(x, axis=axis)

def _gelu(x):
    return jax.nn.gelu(x, approximate=True)

def _silu(x):
    return jax.nn.silu(x)

def _sigmoid(x):
    return jax.nn.sigmoid(x)

def _layernorm(x, axis=-1, eps=1e-05):
    m = jnp.mean(x, axis=axis, keepdims=True)
    v = jnp.var(x, axis=axis, keepdims=True)
    return (x - m) / jnp.sqrt(v + eps)

def _scatter_add(tgt, idx, src, axis=0):
    return tgt.at[idx].add(src)

def _segment_sum(src, seg, n):
    return jax.ops.segment_sum(src, seg, n)
kernel_name = 'mk_decoder_postln_d1_seqx_r4_2f5556'

def setup_inputs(seed: int=0):
    np.random.seed(seed)
    _w = jnp.asarray

    def _rec_inputs():
        import jax
        import jax.numpy as jnp
        _rk = jax.random.key(seed)
        x = 7.22e-05 + 1 * jax.random.normal(jax.random.fold_in(_rk, 1), (8, 256, 512), jnp.float32)
        _lenS = 256 - jax.random.randint(jax.random.fold_in(_rk, 7), (8,), 0, max(1, 256 // 4) + 1, jnp.int32)
        _lenS2 = 256 - jax.random.randint(jax.random.fold_in(_rk, 8), (8,), 0, max(1, 256 // 4) + 1, jnp.int32)
        _ctx_1024P = jax.random.normal(jax.random.fold_in(_rk, 11), (8, 16, 256), jnp.float32)
        _ctx_1024c = jax.random.dirichlet(jax.random.fold_in(_rk, 511), 0.3 * jnp.ones((16,), jnp.float32), (8, 256))
        _ctx_1024t = jnp.einsum('bsk,bkd->bsd', _ctx_1024c, _ctx_1024P)
        _ctx_1024t = _ctx_1024t * jax.lax.rsqrt(jnp.mean(jnp.square(_ctx_1024t)) + 1e-12) * 0.953939
        ctx_1024 = -1.39393e-06 + 0.999914 * (_ctx_1024t + 0.3 * jax.random.normal(jax.random.fold_in(_rk, 611), (8, 256, 256), jnp.float32))
        fside_BxSx2_0 = jax.random.uniform(jax.random.fold_in(_rk, 12), (8, 256, 2), jnp.float32, 0.0, 0.999707)
        return (x, ctx_1024, fside_BxSx2_0)
    x, ctx_1024, fside_BxSx2_0 = _rec_inputs()

    def _L0_attn_setup():
        import jax, jax.numpy as jnp
        import numpy as np
        H = 16
        KVH = 4
        D = 128
        HID = 512
        EPS = 1e-06
        GROUPS = H // KVH

        def elu_plus_one(x):
            return jax.nn.elu(x) + 1.0

        def _repeat_kv(x, b, s):
            x = x.reshape(b, s, KVH, 1, D)
            x = jnp.broadcast_to(x, (b, s, KVH, GROUPS, D))
            return x.reshape(b, s, H * D)

        def _split_heads(x, b, s, nh):
            return x.reshape(b, s, nh, D).transpose(0, 2, 1, 3)
        key = jax.random.key(seed)
        ks = jax.random.split(key, 8)
        s = 0.02
        return {'hidden_states': jax.random.normal(ks[0], (2, 1024, HID), jnp.float32), 'Wq': jax.random.normal(ks[1], (H * D, HID), jnp.float32) * s, 'bq': jnp.zeros((H * D,), jnp.float32), 'Wk': jax.random.normal(ks[2], (KVH * D, HID), jnp.float32) * s, 'bk': jnp.zeros((KVH * D,), jnp.float32), 'Wv': jax.random.normal(ks[3], (KVH * D, HID), jnp.float32) * s, 'bv': jnp.zeros((KVH * D,), jnp.float32), 'Wo': jax.random.normal(ks[4], (HID, H * D), jnp.float32) * s}
    _L0_attn_all = _L0_attn_setup()
    _L0_attn_in = {k: v for k, v in _L0_attn_all.items() if k in ('Wq', 'bq', 'Wk', 'bk', 'Wv', 'bv', 'Wo')}
    del _L0_attn_all

    def _L0_xattn_setup():
        import jax, jax.numpy as jnp
        import numpy as np
        DIM = 512
        CTX_DIM = 256
        N_HEADS = 32
        HEAD_DIM = DIM // N_HEADS
        POS_DIM = 2
        B, N, CTXN = (2, 512, 512)
        ROPE_BASE = 10000.0

        def apply_axial_rope(x, pos):
            b, n, h, d = x.shape
            p = pos.shape[-1]
            dpa = d // p
            half = dpa // 2
            freqs = ROPE_BASE ** (-jnp.arange(half, dtype=x.dtype) / half)
            ang = pos[..., :, None] * freqs
            cos = jnp.cos(ang)[:, :, None, :, :]
            sin = jnp.sin(ang)[:, :, None, :, :]
            xr = x.reshape(b, n, h, p, half, 2)
            x1, x2 = (xr[..., 0], xr[..., 1])
            out = jnp.stack([x1 * cos - x2 * sin, x1 * sin + x2 * cos], axis=-1)
            return out.reshape(b, n, h, d)
        key = jax.random.key(seed)
        ks = jax.random.split(key, 8)
        x = jax.random.normal(ks[0], (B, N, DIM), jnp.float32)
        ctx = jax.random.normal(ks[1], (B, CTXN, CTX_DIM), jnp.float32)
        pos_map = jax.random.uniform(ks[2], (B, N, POS_DIM), jnp.float32)
        ctx_pos_map = jax.random.uniform(ks[3], (B, CTXN, POS_DIM), jnp.float32)
        Wq = jax.random.normal(ks[4], (DIM, DIM), jnp.float32) / np.sqrt(DIM)
        Wkv = jax.random.normal(ks[5], (CTX_DIM, 2 * DIM), jnp.float32) / np.sqrt(CTX_DIM)
        Wout = jax.random.normal(ks[6], (DIM, DIM), jnp.float32) / np.sqrt(DIM)
        bout = jnp.zeros((DIM,), jnp.float32)
        return {'x': x, 'ctx': ctx, 'pos_map': pos_map, 'ctx_pos_map': ctx_pos_map, 'Wq': Wq, 'Wkv': Wkv, 'Wout': Wout, 'bout': bout}
    _L0_xattn_all = _L0_xattn_setup()
    _L0_xattn_in = {k: v for k, v in _L0_xattn_all.items() if k in ('Wq', 'Wkv', 'Wout', 'bout')}
    del _L0_xattn_all

    def _L0_ffn_setup():
        import jax, jax.numpy as jnp
        import numpy as np
        from jax import lax
        TOP_K = 4
        ROUTED_SCALING = 1.0
        RENORMALIZE = True

        def _swiglu_ffn(x, wg, wu, wd):
            return jax.nn.silu(x @ wg.T) * (x @ wu.T) @ wd.T
        key = jax.random.key(seed)
        ks = jax.random.split(key, 9)
        H, I, E = (512, 256, 16)
        s = 0.02
        return {'hidden_states': jax.random.normal(ks[0], (2, 256, H), jnp.float32), 'gate_w': jax.random.normal(ks[1], (E, H), jnp.float32) * s, 'expert_bias': jax.random.normal(ks[2], (E,), jnp.float32) * s, 'w_gate': jax.random.normal(ks[3], (E, I, H), jnp.float32) * s, 'w_up': jax.random.normal(ks[4], (E, I, H), jnp.float32) * s, 'w_down': jax.random.normal(ks[5], (E, H, I), jnp.float32) * s, 'sw_gate': jax.random.normal(ks[6], (I, H), jnp.float32) * s, 'sw_up': jax.random.normal(ks[7], (I, H), jnp.float32) * s, 'sw_down': jax.random.normal(ks[8], (H, I), jnp.float32) * s}
    _L0_ffn_all = _L0_ffn_setup()
    _L0_ffn_in = {k: v for k, v in _L0_ffn_all.items() if k in ('gate_w', 'expert_bias', 'w_gate', 'w_up', 'w_down', 'sw_gate', 'sw_up', 'sw_down')}
    del _L0_ffn_all
    return {'x': x, 'ctx_1024': ctx_1024, 'fside_BxSx2_0': fside_BxSx2_0, 'L0_attn_Wq': _L0_attn_in['Wq'], 'L0_attn_bq': _L0_attn_in['bq'], 'L0_attn_Wk': _L0_attn_in['Wk'], 'L0_attn_bk': _L0_attn_in['bk'], 'L0_attn_Wv': _L0_attn_in['Wv'], 'L0_attn_bv': _L0_attn_in['bv'], 'L0_attn_Wo': _L0_attn_in['Wo'], 'L0_xattn_Wq': _L0_xattn_in['Wq'], 'L0_xattn_Wkv': _L0_xattn_in['Wkv'], 'L0_xattn_Wout': _L0_xattn_in['Wout'], 'L0_xattn_bout': _L0_xattn_in['bout'], 'L0_ffn_gate_w': _L0_ffn_in['gate_w'], 'L0_ffn_expert_bias': _L0_ffn_in['expert_bias'], 'L0_ffn_w_gate': _L0_ffn_in['w_gate'], 'L0_ffn_w_up': _L0_ffn_in['w_up'], 'L0_ffn_w_down': _L0_ffn_in['w_down'], 'L0_ffn_sw_gate': _L0_ffn_in['sw_gate'], 'L0_ffn_sw_up': _L0_ffn_in['sw_up'], 'L0_ffn_sw_down': _L0_ffn_in['sw_down']}

def reference(x, ctx_1024, fside_BxSx2_0, L0_attn_Wq, L0_attn_bq, L0_attn_Wk, L0_attn_bk, L0_attn_Wv, L0_attn_bv, L0_attn_Wo, L0_xattn_Wq, L0_xattn_Wkv, L0_xattn_Wout, L0_xattn_bout, L0_ffn_gate_w, L0_ffn_expert_bias, L0_ffn_w_gate, L0_ffn_w_up, L0_ffn_w_down, L0_ffn_sw_gate, L0_ffn_sw_up, L0_ffn_sw_down):
    import jax
    import jax.numpy as jnp

    def _L0_attn_ref(hidden_states, Wq, bq, Wk, bk, Wv, bv, Wo):
        import jax, jax.numpy as jnp
        import numpy as np
        H = 16
        KVH = 4
        D = 128
        HID = 512
        EPS = 1e-06
        GROUPS = H // KVH

        def elu_plus_one(x):
            return jax.nn.elu(x) + 1.0

        def _repeat_kv(x, b, s):
            x = x.reshape(b, s, KVH, 1, D)
            x = jnp.broadcast_to(x, (b, s, KVH, GROUPS, D))
            return x.reshape(b, s, H * D)

        def _split_heads(x, b, s, nh):
            return x.reshape(b, s, nh, D).transpose(0, 2, 1, 3)
        b, s, _ = hidden_states.shape
        q = hidden_states @ Wq.T + bq
        k = hidden_states @ Wk.T + bk
        v = hidden_states @ Wv.T + bv
        k = _repeat_kv(k, b, s)
        v = _repeat_kv(v, b, s)
        q = _split_heads(q, b, s, H)
        k = _split_heads(k, b, s, H)
        v = _split_heads(v, b, s, H)
        sq = elu_plus_one(q)
        sk = elu_plus_one(k)
        kv = jnp.einsum('bhsd,bhse->bhde', sk, v)
        qkv = jnp.einsum('bhsd,bhde->bhse', sq, kv)
        k_sum = sk.sum(axis=2)
        norm = jnp.einsum('bhsd,bhd->bhs', sq, k_sum)
        attn = qkv / (norm[..., None] + EPS)
        attn = attn.transpose(0, 2, 1, 3).reshape(b, s, H * D)
        return attn @ Wo.T

    def _L0_xattn_ref(x, ctx, pos_map, ctx_pos_map, Wq, Wkv, Wout, bout):
        import jax, jax.numpy as jnp
        import numpy as np
        DIM = 512
        CTX_DIM = 256
        N_HEADS = 32
        HEAD_DIM = DIM // N_HEADS
        POS_DIM = 2
        B, N, CTXN = (2, 512, 512)
        ROPE_BASE = 10000.0

        def apply_axial_rope(x, pos):
            b, n, h, d = x.shape
            p = pos.shape[-1]
            dpa = d // p
            half = dpa // 2
            freqs = ROPE_BASE ** (-jnp.arange(half, dtype=x.dtype) / half)
            ang = pos[..., :, None] * freqs
            cos = jnp.cos(ang)[:, :, None, :, :]
            sin = jnp.sin(ang)[:, :, None, :, :]
            xr = x.reshape(b, n, h, p, half, 2)
            x1, x2 = (xr[..., 0], xr[..., 1])
            out = jnp.stack([x1 * cos - x2 * sin, x1 * sin + x2 * cos], axis=-1)
            return out.reshape(b, n, h, d)
        b, n, _ = x.shape
        ctx_n = ctx.shape[1]
        q = (x @ Wq).reshape(b, n, N_HEADS, HEAD_DIM)
        k, v = jnp.split(ctx @ Wkv, 2, axis=-1)
        k = k.reshape(b, ctx_n, N_HEADS, HEAD_DIM)
        v = v.reshape(b, ctx_n, N_HEADS, HEAD_DIM)
        q = apply_axial_rope(q, pos_map)
        k = apply_axial_rope(k, ctx_pos_map)
        scale = 1.0 / np.sqrt(HEAD_DIM).astype(np.float32)
        logits = jnp.einsum('bqhd,bkhd->bhqk', q, k) * scale
        w = jax.nn.softmax(logits, axis=-1)
        attn = jnp.einsum('bhqk,bkhd->bqhd', w, v)
        attn = attn.reshape(b, n, N_HEADS * HEAD_DIM)
        return attn @ Wout + bout

    def _L0_ffn_ref(hidden_states, gate_w, expert_bias, w_gate, w_up, w_down, sw_gate, sw_up, sw_down):
        import jax, jax.numpy as jnp
        import numpy as np
        from jax import lax
        TOP_K = 4
        ROUTED_SCALING = 1.0
        RENORMALIZE = True

        def _swiglu_ffn(x, wg, wu, wd):
            return jax.nn.silu(x @ wg.T) * (x @ wu.T) @ wd.T
        orig_shape = hidden_states.shape
        H = orig_shape[-1]
        x = hidden_states.reshape(-1, H)
        T = x.shape[0]
        logits = x.astype(jnp.float32) @ gate_w.T
        scores = jax.nn.sigmoid(logits)
        _, topk_idx = lax.top_k(scores + expert_bias[None, :], TOP_K)
        topk_w = jnp.take_along_axis(scores, topk_idx, axis=-1)
        if RENORMALIZE:
            topk_w = topk_w / jnp.sum(topk_w, axis=-1, keepdims=True)
        topk_w = topk_w * ROUTED_SCALING
        E = gate_w.shape[0]
        combine = jnp.zeros((T, E), dtype=x.dtype).at[jnp.arange(T)[:, None], topk_idx].set(topk_w.astype(x.dtype))

        def step(acc, ws):
            wg, wu, wd, cw = ws
            return (acc + cw[:, None] * _swiglu_ffn(x, wg, wu, wd), None)
        routed, _ = lax.scan(step, jnp.zeros_like(x), (w_gate, w_up, w_down, combine.T))
        shared = _swiglu_ffn(x, sw_gate, sw_up, sw_down)
        return (routed + shared).reshape(orig_shape)
    x = _layernorm(x + _L0_attn_ref(x, L0_attn_Wq, L0_attn_bq, L0_attn_Wk, L0_attn_bk, L0_attn_Wv, L0_attn_bv, L0_attn_Wo), axis=-1)
    x = _layernorm(x + _L0_xattn_ref(x, ctx_1024, fside_BxSx2_0, fside_BxSx2_0, L0_xattn_Wq, L0_xattn_Wkv, L0_xattn_Wout, L0_xattn_bout), axis=-1)
    x = _layernorm(x + _L0_ffn_ref(x, L0_ffn_gate_w, L0_ffn_expert_bias, L0_ffn_w_gate, L0_ffn_w_up, L0_ffn_w_down, L0_ffn_sw_gate, L0_ffn_sw_up, L0_ffn_sw_down), axis=-1)
    return x

_drawn_inputs = setup_inputs


def setup_inputs(seed=0):
    import zlib

    import numpy as np

    out = dict(_drawn_inputs(seed))
    spreads = {'L0_attn_bq': (0.0, 2.0),
     'L0_attn_bk': (0.0, 2.0),
     'L0_attn_bv': (0.0, 0.1),
     'L0_xattn_bout': (0.0, 0.1)}
    factors = {'L0_attn_Wq': 8.0,
     'L0_attn_Wk': 8.0,
     'L0_ffn_gate_w': 3.802,
     'L0_ffn_expert_bias': 8.0,
     'L0_ffn_w_gate': 3.318,
     'L0_ffn_w_up': 3.245,
     'L0_ffn_w_down': 3.252}
    for name, (base, spread) in spreads.items():
        noise = np.random.default_rng([zlib.crc32(name.encode()), seed]).standard_normal(out[name].shape)
        drawn = base * np.exp(spread * noise) if base else spread * noise
        out[name] = jnp.asarray(drawn.astype(out[name].dtype))
    for name, factor in factors.items():
        out[name] = (out[name] * factor).astype(out[name].dtype)
    return out
```

```python
from contextlib import ExitStack

import numpy as np
import concourse.bass as bass
from concourse import mybir

ALU = mybir.AluOpType
ACT = mybir.ActivationFunctionType
AX = mybir.AxisListType
F32 = mybir.dt.float32
F32R = mybir.dt.float32r

P = 128
B, S, HID = 8, 256, 512
T = B * S
NT = T // P
HK = HID // P
KVG, GROUP, DH = 4, 4, 128
NORM_EPS = 1e-6
LN_EPS = 1e-5
XH, XD = 32, 16
CTX = 256
CK = CTX // P
E, TOPK, FF = 16, 4, 256
TB = S // P


def wait(eng, sem, value):
    if not isinstance(value, int) or value > 0:
        eng.wait_ge(sem, value)


def wait_apart(eng, sem, value, met, count):
    if not isinstance(value, int):
        value = eng.to_reg(value)
    eng.wait_ge(met, count)
    eng.wait_ge(sem, value)


def linear_attention(nc, X, x_cols, x_tok, w_qkv, b_qkv, w_out):
    NB = GROUP + 2
    SC = DH + 2
    with ExitStack() as ctx:
        def sb(name, shape, dt=F32):
            return ctx.enter_context(nc.sbuf_tensor(name, shape, dt))

        def sem(name):
            return ctx.enter_context(nc.semaphore(name))

        xh = sb("xh", [P, HK, T], F32R)
        xl = sb("xl", [P, HK, T], F32R)
        x_raw = sb("x_raw", [P, 2, HK, S])
        w_raw = sb("w_raw", [P, HK, NB * DH])
        wo_raw = sb("wo_raw", [P, GROUP, HID])
        wh = sb("wh", [P, HK, NB * DH], F32R)
        wl = sb("wl", [P, HK, NB * DH], F32R)
        woh = sb("woh", [P, GROUP, HID], F32R)
        wol = sb("wol", [P, GROUP, HID], F32R)
        bias = sb("bias", [P, KVG, NB])
        bias1 = sb("bias1", [P, KVG, NB])
        ident = sb("ident", [P, P])
        ones = sb("ones", [P, 2])
        ex = sb("ex", [P, GROUP + 1, S])
        feat = sb("feat", [P, NB, S])
        qh = sb("qh", [P, GROUP, S], F32R)
        ql = sb("ql", [P, GROUP, S], F32R)
        ksum = sb("ksum", [P, 1])
        th = sb("th", [P, 2 * TB, P], F32R)
        tl = sb("tl", [P, 2 * TB, P], F32R)
        kvh = sb("kvh", [P, SC], F32R)
        kvl = sb("kvl", [P, SC], F32R)
        norm = sb("norm", [P, 2 * GROUP])
        at = sb("at", [P, TB, GROUP, P])
        ah = sb("ah", [P, GROUP, S], F32R)
        al = sb("al", [P, GROUP, S], F32R)

        banks = ctx.enter_context(nc.psum_tensor("banks", [P, 8, 512], F32))
        p_kv = banks[:, 0].rearrange("p (i s) -> p i s", i=2)
        p_q = [banks[:, 1 + i].rearrange("p (i s) -> p i s", i=2) for i in range(2)]
        p_num = banks[:, 3:7, 0:2 * SC].rearrange("p c (j x) -> p c j x", x=SC)
        p_at = [banks[:, 3 + i].rearrange("p (i s) -> p i s", i=2) for i in range(2)]
        p_out = [banks[:, 5], banks[:, 6]]
        p_tr = banks[:, 7].rearrange("p (i s) -> p i s", i=2 * TB)
        p_state = banks[:, 0, 0:P]

        x_landed = [sem("x_landed0"), sem("x_landed1")]
        xtok_landed, bias_landed = sem("xtok_landed"), sem("bias_landed")
        w_landed, wo_landed = sem("w_landed"), sem("wo_landed")
        x_hi, x_lo = sem("x_hi"), sem("x_lo")
        w_hi, w_lo, wo_hi, wo_lo = sem("w_hi"), sem("w_lo"), sem("wo_hi"), sem("wo_lo")
        consts = sem("consts")
        projected = sem("projected")
        exped, v_ready = sem("exped"), sem("v_ready")
        clipped, bias1_ready, feat_k, feat_q = sem("clipped"), sem("bias1_ready"), sem("feat_k"), sem("feat_q")
        q_hi, q_lo = sem("q_hi"), sem("q_lo")
        turned, turned_hi, turned_lo = sem("turned"), sem("turned_hi"), sem("turned_lo")
        state, state_hi, state_lo = sem("state"), sem("state_hi"), sem("state_lo")
        applied, norm_read, inverted, normalised = sem("applied"), sem("norm_read"), sem("inverted"), sem("normalised")
        at_turned = sem("at_turned")
        a_hi, a_lo = sem("a_hi"), sem("a_lo")
        out_done, added = sem("out_done"), sem("added")

        block = ctx.enter_context(nc.Block())

        def steps(eng, body, before=None, after_first=None):
            for g in range(KVG):
                if before:
                    before(g)
                body(g, B * g, 0)
                if after_first:
                    after_first(g)
                with eng.Fori(1, B) as b:
                    body(g, b + B * g, b)

        @block.sync
        def _(sp):
            sp.dma_start(x_raw[:, 0], x_cols[:, :, 0:S]).then_inc(x_landed[0], 16)
            sp.dma_start(bias[:, :, :], b_qkv).then_inc(bias_landed, 16)
            sp.dma_start(w_raw[:, :, :], w_qkv[0]).then_inc(w_landed, 16)
            sp.dma_start(x_raw[:, 1], x_cols[:, :, S:2 * S]).then_inc(x_landed[1], 16)
            sp.dma_start(wo_raw[:, :, :], w_out[0]).then_inc(wo_landed, 16)
            sp.dma_start(X[:, :, :], x_tok).then_inc(xtok_landed, 16)
            for b in range(2, B):
                sp.wait_ge(x_hi, b - 1)
                sp.wait_ge(x_lo, b - 1)
                sp.dma_start(x_raw[:, b % 2], x_cols[:, :, b * S:(b + 1) * S]).then_inc(x_landed[b % 2], 16)
            for g in range(1, KVG):
                sp.wait_ge(w_hi, g)
                sp.wait_ge(w_lo, g)
                sp.dma_start(w_raw[:, :, :], w_qkv[g]).then_inc(w_landed, 16)
                sp.wait_ge(wo_hi, g)
                sp.wait_ge(wo_lo, g)
                sp.dma_start(wo_raw[:, :, :], w_out[g]).then_inc(wo_landed, 16)

        @block.gpsimd
        def _(pool):
            pool.memset(ident[:, :], 0.0).then_inc(consts, 1)
            pool.memset(ones[:, :], 1.0).then_inc(consts, 1)
            pool.wait_ge(consts, 2)
            pool.affine_select(out=ident[:, :], in_=ident[:, :], compare_op=ALU.not_equal, fill=1.0,
                               base=0, pattern=[[-1, P]], channel_multiplier=1).then_inc(consts, 1)

            def split_x(b):
                pool.wait_ge(x_hi, b + 1)
                pool.tensor_tensor(xl[:, :, b * S:(b + 1) * S], x_raw[:, b % 2],
                                   xh[:, :, b * S:(b + 1) * S].bitcast(F32), ALU.subtract).then_inc(x_lo, 1)

            def split_w(g):
                pool.wait_ge(w_hi, g + 1)
                pool.tensor_tensor(wl[:, :, :], w_raw[:, :, :], wh[:, :, :].bitcast(F32), ALU.subtract).then_inc(w_lo, 1)
                if g == 0:
                    for b in range(B):
                        split_x(b)

            def split_wo(g):
                pool.wait_ge(wo_hi, g + 1)
                pool.tensor_tensor(wol[:, :, :], wo_raw[:, :, :], woh[:, :, :].bitcast(F32), ALU.subtract).then_inc(wo_lo, 1)

            def body(g, n, b):
                for i in range(2):
                    pool.wait_ge(q_hi, 2 * n + i + 1)
                    pool.tensor_tensor(ql[:, 2 * i:2 * i + 2], feat[:, 2 * i:2 * i + 2],
                                       qh[:, 2 * i:2 * i + 2].bitcast(F32), ALU.subtract).then_inc(q_lo, 1)

            steps(pool, body, split_w, split_wo)

        @block.scalar
        def _(act):
            def split_w(g):
                act.wait_ge(w_landed, 16 * (g + 1))
                wait(act, projected, NB * B * g)
                act.copy(wh[:, :, :], w_raw[:, :, :]).then_inc(w_hi, 1)
                if g == 0:
                    for b in range(B):
                        act.wait_ge(x_landed[b % 2], 16 * (b // 2 + 1))
                        act.copy(xh[:, :, b * S:(b + 1) * S], x_raw[:, b % 2]).then_inc(x_hi, 1)
                    act.wait_ge(bias_landed, 16)

            def split_wo(g):
                act.wait_ge(wo_landed, 16 * (g + 1))
                wait(act, out_done, 2 * B * g)
                act.copy(woh[:, :, :], wo_raw[:, :, :]).then_inc(wo_hi, 1)

            def attn_hi(m):
                act.wait_ge(at_turned, m + 1)
                wait(act, out_done, 2 * m)
                for i in range(2):
                    act.copy(ah[:, 2 * i:2 * i + 2], p_at[i]).then_inc(a_hi, 1)

            def q_pair(n, i):
                act.wait_ge(clipped, 3 * n + 2 + i)
                act.activation(ex[:, 2 * i:2 * i + 2], ex[:, 2 * i:2 * i + 2], ACT.Exp).then_inc(exped, 1)
                act.wait_ge(feat_q, 2 * n + i + 1)
                wait(act, applied, n)
                act.copy(qh[:, 2 * i:2 * i + 2], feat[:, 2 * i:2 * i + 2]).then_inc(q_hi, 1)

            def body(g, n, b):
                wait(act, turned, n)
                act.wait_ge(projected, NB * n + 2)
                act.activation(feat[:, GROUP + 1], p_kv[:, 1], ACT.Identity, bias=bias[:, g, GROUP + 1:GROUP + 2]).then_inc(v_ready, 1)
                act.wait_ge(clipped, 3 * n + 1)
                act.activation(ex[:, GROUP], ex[:, GROUP], ACT.Exp).then_inc(exped, 1)
                q_pair(n, 0)
                act.wait_ge(turned, n + 1)
                wait(act, state, n)
                act.copy(th[:, :, :], p_tr).then_inc(turned_hi, 1)
                if not (isinstance(n, int) and n == 0):
                    attn_hi(n - 1)
                q_pair(n, 1)

            steps(act, body, split_w, split_wo)
            attn_hi(KVG * B - 1)

        @block.vector
        def _(dve):
            def normalise(m):
                dve.wait_ge(applied, m + 1)
                dve.tensor_scalar(norm[:, :].rearrange("p (c j) -> p c j", j=2), p_num[:, :, :, DH], NORM_EPS, None,
                                  ALU.add).then_inc(norm_read, 1)
                dve.wait_ge(norm_read, m + 1)
                dve.reciprocal(norm[:, :], norm[:, :]).then_inc(inverted, 1)
                dve.wait_ge(inverted, m + 1)
                wait(dve, at_turned, m)
                for t in range(TB):
                    by = norm[:, GROUP * t:GROUP * (t + 1)].rearrange("p (c j) -> p c j", j=2).unsqueeze(3).to_broadcast([P, 2, 2, DH])
                    dve.tensor_tensor(at[:, t].rearrange("p (c j) e -> p c j e", j=2), p_num[:, 2 * t:2 * t + 2, :, 0:DH], by,
                                      ALU.mult).then_inc(normalised, 1)

            def attn_lo(m):
                dve.wait_ge(a_hi, 2 * m + 2)
                for i in range(2):
                    dve.tensor_tensor(al[:, 2 * i:2 * i + 2], p_at[i], ah[:, 2 * i:2 * i + 2].bitcast(F32),
                                      ALU.subtract).then_inc(a_lo, 1)

            def add_out(m, b):
                for t in range(TB):
                    dve.wait_ge(out_done, 2 * m + t + 1)
                    row = X[:, b * TB + t] if isinstance(b, int) else X[:, bass.ds(b * TB + t, 1)].rearrange("p o h -> p (o h)")
                    dve.tensor_tensor(row, row, p_out[t], ALU.add).then_inc(added, 1)

            def q_features(g, n, i):
                dve.wait_ge(projected, NB * n + 4 + 2 * i)
                for j in range(2):
                    c = dve.tensor_scalar(ex[:, 2 * i + j], p_q[i][:, j], bias[:, g, 2 * i + j:2 * i + j + 1], 0.0, ALU.add, ALU.min)
                c.then_inc(clipped, 1)
                dve.wait_ge(exped, 3 * n + 2 + i)
                wait(dve, q_lo, 2 * n - 1 + i)
                for j in range(2):
                    f = dve.scalar_tensor_tensor(out=feat[:, 2 * i + j], in0=p_q[i][:, j], scalar=bias1[:, g, 2 * i + j:2 * i + j + 1],
                                                 in1=ex[:, 2 * i + j], op0=ALU.add, op1=ALU.max)
                f.then_inc(feat_q, 1)

            def body(g, n, b):
                first = isinstance(n, int) and n == 0
                dve.wait_ge(v_ready, n + 1)
                dve.tensor_scalar(ex[:, GROUP], p_kv[:, 0], bias[:, g, GROUP:GROUP + 1], 0.0, ALU.add, ALU.min).then_inc(clipped, 1)
                dve.wait_ge(exped, 3 * n + 1)
                dve.scalar_tensor_tensor(out=feat[:, GROUP], in0=p_kv[:, 0], scalar=bias1[:, g, GROUP:GROUP + 1],
                                         in1=ex[:, GROUP], op0=ALU.add, op1=ALU.max, accum_out=ksum[:, :]).then_inc(feat_k, 1)
                if not first:
                    normalise(n - 1)
                q_features(g, n, 0)
                dve.wait_ge(turned_hi, n + 1)
                dve.tensor_tensor(tl[:, :, :], p_tr, th[:, :, :].bitcast(F32), ALU.subtract).then_inc(turned_lo, 1)
                dve.wait_ge(feat_k, n + 1)
                wait(dve, applied, n)
                dve.tensor_scalar(kvh[:, DH:], ones[:, :], ksum[:, 0:1], None, ALU.mult).then_inc(state_hi, 1)
                dve.wait_ge(state_hi, 2 * n + 1)
                dve.tensor_scalar(kvl[:, DH:], kvh[:, DH:].bitcast(F32), -1.0, ksum[:, 0:1], ALU.mult, ALU.add).then_inc(state_lo, 1)
                if not first:
                    attn_lo(n - 1)
                q_features(g, n, 1)
                dve.wait_ge(state, n + 1)
                dve.tensor_copy(kvh[:, 0:DH], p_state).then_inc(state_hi, 1)
                dve.wait_ge(state_hi, 2 * n + 2)
                dve.tensor_tensor(kvl[:, 0:DH], p_state, kvh[:, 0:DH].bitcast(F32), ALU.subtract).then_inc(state_lo, 1)
                if not first:
                    add_out(n - 1, B - 1 if isinstance(b, int) else b - 1)

            dve.wait_ge(consts, 3)
            dve.wait_ge(bias_landed, 16)
            dve.wait_ge(xtok_landed, 16)
            dve.tensor_scalar(bias1[:, :, :], bias[:, :, :], 1.0, None, ALU.add).then_inc(bias1_ready, 1)
            dve.wait_ge(bias1_ready, 1)
            steps(dve, body)
            normalise(KVG * B - 1)
            attn_lo(KVG * B - 1)
            add_out(KVG * B - 1, B - 1)

        @block.tensor
        def _(pe):
            def product(out, pairs):
                terms = [t for lh, ll, rh, rl in pairs for t in ((lh, rl), (ll, rh), (lh, rh))]
                for i, (a, c) in enumerate(terms):
                    mm = pe.matmul(out, a, c, start=(i == 0), stop=(i == len(terms) - 1))
                return mm

            def project(i, out, b):
                cols = slice(b * S, (b + 1) * S) if isinstance(b, int) else bass.ds(b * S, S)
                w = slice(i * DH, (i + 1) * DH)
                product(out, [(wh[:, k, w], wl[:, k, w], xh[:, k, cols], xl[:, k, cols]) for k in range(HK)]).then_inc(projected, 1)

            def apply_state(m):
                pe.wait_ge(q_lo, 2 * m + 2)
                pe.wait_ge(q_hi, 2 * m + 2)
                pe.wait_ge(state_lo, 2 * m + 2)
                wait(pe, added, 2 * m)
                wait(pe, a_lo, 2 * m)
                for j in range(TB * GROUP):
                    h, s = j % GROUP, slice(j // GROUP * P, (j // GROUP + 1) * P)
                    mm = product(p_num[:, j // 2, j % 2], [(qh[:, h, s], ql[:, h, s], kvh[:, :], kvl[:, :])])
                mm.then_inc(applied, 1)

            def turn_attention(m):
                pe.wait_ge(normalised, 2 * m + 2)
                for t in range(TB):
                    for h in range(GROUP):
                        mm = pe.transpose(p_at[h // 2][:, h % 2, t * P:(t + 1) * P], at[:, t, h], ident[:, :])
                mm.then_inc(at_turned, 1)

            def project_out(m):
                pe.wait_ge(a_lo, 2 * m + 2)
                for t in range(TB):
                    s = slice(t * P, (t + 1) * P)
                    product(p_out[t], [(ah[:, h, s], al[:, h, s], woh[:, h], wol[:, h]) for h in range(GROUP)]).then_inc(out_done, 1)

            def body(g, n, b):
                first = isinstance(n, int) and n == 0
                wait(pe, state_lo, 2 * n)
                if isinstance(b, int):
                    pe.wait_ge(w_hi, g + 1)
                    pe.wait_ge(w_lo, g + 1)
                pe.wait_ge(x_hi, b + 1)
                pe.wait_ge(x_lo, b + 1)
                project(GROUP, p_kv[:, 0], b)
                project(GROUP + 1, p_kv[:, 1], b)
                if not first:
                    apply_state(n - 1)
                for h in range(GROUP):
                    if h % 2 == 0:
                        wait(pe, feat_q, 2 * n - 1 + h // 2)
                    project(h, p_q[h // 2][:, h % 2], b)
                    if h == 1:
                        pe.wait_ge(consts, 3)
                        pe.wait_ge(feat_k, n + 1)
                        pe.wait_ge(v_ready, n + 1)
                        wait(pe, turned_lo, n)
                        for t in range(TB):
                            for i in range(2):
                                mm = pe.transpose(p_tr[:, 2 * t + i], feat[:, GROUP + i, t * P:(t + 1) * P], ident[:, :])
                        mm.then_inc(turned, 1)
                        if not first:
                            turn_attention(n - 1)
                pe.wait_ge(turned_hi, n + 1)
                pe.wait_ge(turned_lo, n + 1)
                product(p_state, [(th[:, 2 * t], tl[:, 2 * t], th[:, 2 * t + 1], tl[:, 2 * t + 1]) for t in range(TB)]).then_inc(state, 1)
                if not first:
                    if not isinstance(b, int):
                        pe.wait_ge(wo_hi, g + 1)
                        pe.wait_ge(wo_lo, g + 1)
                    project_out(n - 1)

            steps(pe, body)
            apply_state(KVG * B - 1)
            turn_attention(KVG * B - 1)
            project_out(KVG * B - 1)


def project_context(nc, X, Q, K, V, ctx_cols, pos, w_q, w_k, w_v):
    HALF = XD // 2
    TWO_PI = 2 * np.pi
    PI2_HI = float(np.float32(6.28125))
    PI2_LO = float(np.float32(TWO_PI - 6.28125))
    ROUND = 12582912.0
    PI = float(np.nextafter(np.float32(np.pi), np.float32(0)))
    FREQS = [float(np.float32(10000.0 ** (-f / 4))) for f in range(4)]
    with ExitStack() as ctx:
        def sb(name, shape, dt=F32):
            return ctx.enter_context(nc.sbuf_tensor(name, shape, dt))

        def sem(name):
            return ctx.enter_context(nc.semaphore(name))

        wq = [Q[:, 12:16], sb("wq_h", [P, HK, HID], F32R), sb("wq_l", [P, HK, HID], F32R)]
        wk = [Q[:, 8:10], sb("wk_h", [P, CK, HID], F32R), sb("wk_l", [P, CK, HID], F32R)]
        wv = [Q[:, 10:12], sb("wv_h", [P, CK, HID], F32R), sb("wv_l", [P, CK, HID], F32R)]
        post = sb("positions", [P, NT, 2])
        ang, turns_, rad, bent = (sb(n, [P, NT * HALF]) for n in ("ang", "turns", "rad", "bent"))
        cosk, sink, cosq, sinq, nsink, nsinq = (sb(n, [P, NT, HALF]) for n in ("cosk", "sink", "cosq", "sinq", "nsink", "nsinq"))
        ident = sb("ident2", [P, P])
        c_raw = [sb(f"c_raw{i}", [P, CK, P]) for i in range(2)]
        c_h = [sb(f"c_h{i}", [P, CK, P], F32R) for i in range(2)]
        c_l = [sb(f"c_l{i}", [P, CK, P], F32R) for i in range(2)]
        xn = [sb(f"xn{i}", [P, HID]) for i in range(2)]
        x_h = [sb(f"xt_h{i}", [P, HK, P], F32R) for i in range(2)]
        x_l = [sb(f"xt_l{i}", [P, HK, P], F32R) for i in range(2)]
        stats, mv, std, rstd = sb("stats", [P, 6]), sb("mv", [P, 2]), sb("std", [P, 1]), sb("rstd", [P, 1])
        straight = [sb(f"straight{i}", [P, HID]) for i in range(2)]
        crossed = [sb(f"crossed{i}", [P, HID]) for i in range(2)]
        banks = ctx.enter_context(nc.psum_tensor("banks2", [P, 8, 512], F32))

        w_landed, pos_landed = [sem(f"xw_landed{i}") for i in range(3)], sem("pos_landed")
        c_landed = [sem("c_landed0"), sem("c_landed1")]
        w_hi, w_lo, consts = sem("xw_hi"), sem("xw_lo"), sem("consts2")
        table, sined, tables_ready = sem("table"), sem("sined"), sem("tables_ready")
        c_hi, c_lo = sem("c_hi"), sem("c_lo")
        stat, rooted, rooted_inv, xn_ready, x_kept = sem("stat"), sem("rooted"), sem("rooted_inv"), sem("xn_ready"), sem("x_kept")
        x_turned, x_hi, x_lo = sem("x_turned"), sem("xt_hi"), sem("xt_lo")
        k_done, v_done, q_done = sem("k_done"), sem("v_done"), sem("q_done")
        v_copied, k_mult, q_mult, k_rot, q_rot = sem("v_copied"), sem("k_mult"), sem("q_mult"), sem("k_rot"), sem("q_rot")

        block = ctx.enter_context(nc.Block())

        def tiles(eng, body):
            with eng.Fori(0, NT // 2 - 1) as p:
                for i in range(2):
                    body(2 * p + i, i, False)
            body(NT - 2, 0, False)
            body(NT - 1, 1, True)

        def tile_of(ap, t):
            if isinstance(t, int):
                return ap[:, t]
            return ap[:, bass.ds(t, 1)].squeeze(1)

        @block.sync
        def _(sp):
            sp.dma_start(post[:, :, :], pos).then_inc(pos_landed, 16)
            for w, src, landed in ((wk, w_k, w_landed[0]), (wv, w_v, w_landed[1]), (wq, w_q, w_landed[2])):
                sp.dma_start(w[0], src).then_inc(landed, 16)

            def body(t, i, last):
                if isinstance(t, int):
                    wait(sp, c_hi, t - 1)
                    wait(sp, c_lo, t - 1)
                    sp.dma_start(c_raw[i][:, :, :], ctx_cols[:, :, t * P:(t + 1) * P]).then_inc(c_landed[i], 16)
                else:
                    sp.wait_ge(c_hi, t - 1)
                    sp.wait_ge(c_lo, t - 1)
                    sp.dma_start(c_raw[i][:, :, :], ctx_cols[:, :, bass.ds(t * P, P)]).then_inc(c_landed[i], 16)

            for i in range(2):
                body(i, i, False)
            with sp.Fori(1, NT // 2) as p:
                for i in range(2):
                    body(2 * p + i, i, False)

        @block.gpsimd
        def _(pool):
            pool.memset(V[:, :, :, XD:XD + 1], 1.0).then_inc(consts, 1)
            pool.memset(ident[:, :], 0.0).then_inc(consts, 1)
            pool.wait_ge(consts, 2)
            pool.affine_select(out=ident[:, :], in_=ident[:, :], compare_op=ALU.not_equal, fill=1.0,
                               base=0, pattern=[[-1, P]], channel_multiplier=1).then_inc(consts, 1)
            for j, w in enumerate((wk, wv, wq)):
                pool.wait_ge(w_hi, j + 1)
                pool.tensor_tensor(w[2][:, :, :], w[0], w[1][:, :, :].bitcast(F32), ALU.subtract).then_inc(w_lo, 1)

            def body(t, i, last):
                pool.wait_ge(c_hi, t + 1)
                wait(pool, v_done, t - 1)
                pool.tensor_tensor(c_l[i][:, :, :], c_raw[i][:, :, :], c_h[i][:, :, :].bitcast(F32), ALU.subtract).then_inc(c_lo, 1)
                wait_apart(pool, k_mult, t + 1, consts, 3)
                pool.tensor_tensor(tile_of(K, t), straight[0][:, :], crossed[0][:, :], ALU.add).then_inc(k_rot, 1)
                wait_apart(pool, q_mult, t + 1, consts, 3)
                pool.tensor_tensor(tile_of(Q, t), straight[1][:, :], crossed[1][:, :], ALU.add).then_inc(q_rot, 1)

            body(0, 0, False)
            body(1, 1, False)
            with pool.Fori(1, NT // 2) as p:
                for i in range(2):
                    body(2 * p + i, i, False)

        @block.scalar
        def _(act):
            def context_hi(t, i):
                act.wait_ge(c_landed[i], 16 * (t // 2 + 1) if isinstance(t, int) else 8 * (t - i) + 16)
                wait(act, v_done, t - 1)
                act.copy(c_h[i][:, :, :], c_raw[i][:, :, :]).then_inc(c_hi, 1)

            def root(t):
                act.wait_ge(stat, 3 * t + 3)
                act.sqrt(std[:, :], std[:, :]).then_inc(rooted, 1)

            for j, w in enumerate((wk, wv, wq)):
                act.wait_ge(w_landed[j], 16)
                act.copy(w[1][:, :, :], w[0]).then_inc(w_hi, 1)
            act.wait_ge(table, 9)
            act.activation(sink[:, :, :].rearrange("p t f -> p (t f)"), rad[:, :], ACT.Sin).then_inc(sined, 1)
            act.activation(cosk[:, :, :].rearrange("p t f -> p (t f)"), bent[:, :], ACT.Sin).then_inc(sined, 1)
            root(0)

            def body(t, i, last):
                context_hi(t, i)
                act.wait_ge(xn_ready, t + 1)
                act.copy(tile_of(X, t), xn[i][:, :]).then_inc(x_kept, 1)
                act.wait_ge(x_turned, t + 1)
                wait(act, q_done, t - 1)
                act.copy(x_h[i][:, :, :], banks[:, i].rearrange("p (k s) -> p k s", k=HK)).then_inc(x_hi, 1)
                act.wait_ge(v_done, t + 1)
                act.copy(tile_of(V, t)[:, :, 0:XD], banks[:, 4 + i].rearrange("p (h d) -> p h d", d=XD)).then_inc(v_copied, 1)
                if not last:
                    root(t + 1)

            body(0, 0, False)
            body(1, 1, False)
            with act.Fori(1, NT // 2 - 1) as p:
                for i in range(2):
                    body(2 * p + i, i, False)
            body(NT - 2, 0, False)
            body(NT - 1, 1, True)

        @block.vector
        def _(dve):
            dve.wait_ge(pos_landed, 16)
            av = ang[:, :].rearrange("p (t a f) -> p t a f", a=2, f=4)
            for f in range(4):
                a = dve.tensor_scalar(av[:, :, :, f], post[:, :, :], FREQS[f], None, ALU.mult)
            a.then_inc(table, 1)
            steps = [
                lambda: dve.tensor_scalar(turns_[:, :], ang[:, :], 1.0 / TWO_PI, ROUND, ALU.mult, ALU.add),
                lambda: dve.tensor_scalar(turns_[:, :], turns_[:, :], -ROUND, None, ALU.add),
                lambda: dve.scalar_tensor_tensor(out=rad[:, :], in0=turns_[:, :], scalar=-PI2_HI, in1=ang[:, :], op0=ALU.mult, op1=ALU.add),
                lambda: dve.scalar_tensor_tensor(out=rad[:, :], in0=turns_[:, :], scalar=-PI2_LO, in1=rad[:, :], op0=ALU.mult, op1=ALU.add),
                lambda: dve.tensor_scalar(rad[:, :], rad[:, :], PI, -PI, ALU.min, ALU.max),
                lambda: dve.tensor_scalar(bent[:, :], rad[:, :], -1.0, None, ALU.mult),
                lambda: dve.tensor_tensor(bent[:, :], rad[:, :], bent[:, :], ALU.max),
                lambda: dve.tensor_scalar(bent[:, :], bent[:, :], -1.0, PI / 2, ALU.mult, ALU.add),
            ]
            for n, step in enumerate(steps):
                dve.wait_ge(table, n + 1)
                step().then_inc(table, 1)

            def norm_stats(t):
                dve.bn_stats(stats[:, :], tile_of(X, t)).then_inc(stat, 1)
                wait_apart(dve, stat, 3 * t + 1, pos_landed, 16)
                dve.bn_aggr(mv[:, :], stats[:, :]).then_inc(stat, 1)
                dve.wait_ge(stat, 3 * t + 2)
                dve.tensor_scalar(std[:, :], mv[:, 1:2], LN_EPS, None, ALU.add).then_inc(stat, 1)

            def normalise(t, i):
                dve.wait_ge(rooted, t + 1)
                dve.reciprocal(rstd[:, :], std[:, :]).then_inc(rooted_inv, 1)
                dve.wait_ge(rooted_inv, t + 1)
                wait(dve, x_turned, t - 1)
                wait(dve, x_kept, t - 1)
                dve.tensor_scalar(xn[i][:, :], tile_of(X, t), mv[:, 0:1], rstd[:, 0:1], ALU.subtract, ALU.mult).then_inc(xn_ready, 1)

            def rotate(t, which, bank, done, rotated, mult, cos, sin, nsin):
                dve.wait_ge(done, t + 1)
                wait(dve, rotated, t)
                y = banks[:, bank].rearrange("p (h s f) -> p h s f", s=2, f=HALF)
                st = straight[which][:, :].rearrange("p (h s f) -> p h s f", s=2, f=HALF)
                cr = crossed[which][:, :].rearrange("p (h s f) -> p h s f", s=2, f=HALF)
                one = [P, XH, HALF]
                dve.tensor_tensor(st, y, tile_of(cos, t).unsqueeze(1).unsqueeze(1).to_broadcast([P, XH, 2, HALF]), ALU.mult)
                dve.tensor_tensor(cr[:, :, 0], y[:, :, 1], tile_of(nsin, t).unsqueeze(1).to_broadcast(one), ALU.mult)
                dve.tensor_tensor(cr[:, :, 1], y[:, :, 0], tile_of(sin, t).unsqueeze(1).to_broadcast(one), ALU.mult).then_inc(mult, 1)

            norm_stats(0)
            dve.wait_ge(sined, 2)
            for k, (o, a, f) in enumerate(((nsink, sink, -1.0), (cosq, cosk, 0.25), (sinq, sink, 0.25), (nsinq, sink, -0.25))):
                dve.tensor_scalar(o[:, :, :], a[:, :, :], f, None, ALU.mult).then_inc(tables_ready, 1)
            dve.wait_ge(tables_ready, 4)
            normalise(0, 0)

            def body(t, i, last):
                if not last:
                    norm_stats(t + 1)
                dve.wait_ge(x_hi, t + 1)
                wait(dve, q_done, t - 1)
                dve.tensor_tensor(x_l[i][:, :, :], banks[:, i].rearrange("p (k s) -> p k s", k=HK),
                                  x_h[i][:, :, :].bitcast(F32), ALU.subtract).then_inc(x_lo, 1)
                rotate(t, 0, 2 + i, k_done, k_rot, k_mult, cosk, sink, nsink)
                if not last:
                    normalise(t + 1, 1 - i)
                rotate(t, 1, 6 + i, q_done, q_rot, q_mult, cosq, sinq, nsinq)

            body(0, 0, False)
            body(1, 1, False)
            with dve.Fori(1, NT // 2 - 1) as p:
                for i in range(2):
                    body(2 * p + i, i, False)
            body(NT - 2, 0, False)
            body(NT - 1, 1, True)

        @block.tensor
        def _(pe):
            def product(out, pairs):
                terms = [t for lh, ll, rh, rl in pairs for t in ((lh, rl), (ll, rh), (lh, rh))]
                for i, (a, c) in enumerate(terms):
                    mm = pe.matmul(out, a, c, start=(i == 0), stop=(i == len(terms) - 1))
                return mm

            pe.wait_ge(consts, 3)
            pe.wait_ge(w_hi, 3)
            pe.wait_ge(w_lo, 3)

            def body(t, i, last):
                pe.wait_ge(xn_ready, t + 1)
                wait(pe, x_lo, t - 1)
                for k in range(HK):
                    mm = pe.transpose(banks[:, i, k * P:(k + 1) * P], xn[i][:, k * P:(k + 1) * P], ident[:, :])
                mm.then_inc(x_turned, 1)
                pe.wait_ge(c_hi, t + 1)
                pe.wait_ge(c_lo, t + 1)
                wait(pe, k_mult, t - 1)
                product(banks[:, 2 + i], [(c_h[i][:, k], c_l[i][:, k], wk[1][:, k], wk[2][:, k]) for k in range(CK)]).then_inc(k_done, 1)
                wait(pe, v_copied, t - 1)
                product(banks[:, 4 + i], [(c_h[i][:, k], c_l[i][:, k], wv[1][:, k], wv[2][:, k]) for k in range(CK)]).then_inc(v_done, 1)
                pe.wait_ge(x_hi, t + 1)
                pe.wait_ge(x_lo, t + 1)
                wait(pe, q_mult, t - 1)
                product(banks[:, 6 + i], [(x_h[i][:, k], x_l[i][:, k], wq[1][:, k], wq[2][:, k]) for k in range(HK)]).then_inc(q_done, 1)

            body(0, 0, False)
            body(1, 1, False)
            with pe.Fori(1, NT // 2) as p:
                for i in range(2):
                    body(2 * p + i, i, False)


def softmax_attention(nc, X, Q, K, V, b_out):
    G = 8
    NG = XH // G
    R = 64
    M0 = 2 * XD
    D0 = M0 + 2
    QUAD = 4
    VR = P // QUAD
    with ExitStack() as ctx:
        def sb(name, shape, dt=F32):
            return ctx.enter_context(nc.sbuf_tensor(name, shape, dt))

        def sem(name):
            return ctx.enter_context(nc.semaphore(name))

        bout = sb("bout", [P, HID])
        ident = sb("ident3", [P, P])
        place = sb("place", [P, TB, S], F32R)
        qpad = [sb(f"qpad{i}", [P, TB, G, R], F32R) for i in range(2)]
        kpad = [sb(f"kpad{i}", [P, TB, G, R], F32R) for i in range(2)]
        qT = sb("qT", [P, G // 2, S], F32R)
        qmT = [sb(f"qmT{i}", [P, G // 2, S], F32R) for i in range(2)]
        kT = [sb(f"kT{i}", [P, G // 2, 2, S], F32R) for i in range(2)]
        vz = [sb(f"vz{i}", [P, TB, P - VR + G * P]) for i in range(2)]
        probs = [sb(f"probs{i}", [P, TB, S]) for i in range(2)]
        pvs = [sb(f"pvs{i}", [P, S]) for i in range(2)]
        top = [sb(f"top{i}", [P, TB, G]) for i in range(2)]
        rsum = [sb(f"rsum{i}", [P, TB, QUAD]) for i in range(2)]
        one = sb("one", [P, 1])
        banks = ctx.enter_context(nc.psum_tensor("banks3", [P, 8, 512], F32))
        p_turn = banks[:, 0:2].rearrange("p c (j s) -> p (c j) s", s=S)
        p_raw = [banks[:, 2 + i].rearrange("p (t s) -> p t s", t=TB) for i in range(2)]
        p_shift = [banks[:, 4 + i].rearrange("p (t s) -> p t s", t=TB) for i in range(2)]
        p_pv = banks[:, 6, 0:S]
        p_back = banks[:, 7, 0:S].rearrange("p (t h d) -> p t h d", t=TB, h=QUAD)

        bout_landed, consts, placed = sem("bout_landed"), sem("consts3"), sem("placed")
        q_hi, k_hi, padded, k_padded, v_laid = sem("pq_hi"), sem("pk_hi"), sem("padded"), sem("k_padded"), sem("v_laid")
        q_turned, k_turned, m_turned = sem("q_turned"), sem("k_turned"), sem("m_turned")
        qT_ready, kT_ready, qmT_ready = sem("qT_ready"), sem("kT_ready"), sem("qmT_ready")
        scored, maxed, shift_hi, shift_lo = sem("scored"), sem("maxed"), sem("shift_hi"), sem("shift_lo")
        shifted, exped, pv_done, pv_kept = sem("shifted"), sem("exped3"), sem("pv_done"), sem("pv_kept")
        backed, inverted, written = sem("backed"), sem("inverted3"), sem("written")
        biased = sem("biased")

        block = ctx.enter_context(nc.Block())

        def groups(eng, body):
            def batch(b, last):
                for g in range(NG):
                    nxt = (b, g + 1) if g + 1 < NG else (b + 1, 0)
                    body(b, g, b * NG + g, None if last and g == NG - 1 else nxt)
            batch(0, False)
            with eng.Fori(1, B - 1) as b:
                batch(b, False)
            batch(B - 1, True)

        def part(ap, b, g, width, quad=None):
            rows = slice(b * TB, (b + 1) * TB) if isinstance(b, int) else bass.ds(b * TB, TB)
            first, heads = (g * G, G) if quad is None else (g * G + quad * QUAD, QUAD)
            return ap[:, rows, first * width:(first + heads) * width].rearrange("p t (h d) -> p t h d", d=width)

        @block.sync
        def _(sp):
            sp.dma_start(bout[:, :], b_out.partition_broadcast(P)).then_inc(bout_landed, 16)

        @block.gpsimd
        def _(pool):
            pool.memset(ident[:, :], 0.0).then_inc(consts, 1)
            pool.memset(one[:, :], 1.0)
            for i in range(2):
                pool.memset(qpad[i][:, :, :, :].bitcast(F32), 0.0)
                pool.memset(kpad[i][:, :, :, :].bitcast(F32), 0.0).then_inc(consts, 1)
            pool.wait_ge(consts, 3)
            for i in range(2):
                pool.memset(kpad[i][:, :, :, M0:D0].bitcast(F32), 1.0)
            pool.affine_select(out=ident[:, :], in_=ident[:, :], compare_op=ALU.not_equal, fill=1.0,
                               base=0, pattern=[[-1, P]], channel_multiplier=1).then_inc(consts, 1)

            def pad(b, g, n):
                i = g % 2
                q, k = part(Q, b, g, XD), part(K, b, g, XD)
                if not isinstance(n, int) or n >= 2:
                    wait_apart(pool, m_turned, n - 1, consts, 4)
                by_one = one[:, :].unsqueeze(2).unsqueeze(3).to_broadcast([P, TB, G, XD])
                pool.tensor_tensor(qpad[i][:, :, :, 0:XD], q, by_one, ALU.mult)
                pool.tensor_copy(qpad[i][:, :, :, D0:D0 + XD], q).then_inc(q_hi, 1)
                pool.tensor_copy(kpad[i][:, :, :, 0:XD], k)
                pool.tensor_copy(kpad[i][:, :, :, XD:M0], k).then_inc(k_hi, 1)
                pool.memset(qpad[i][:, :, :, M0:D0].bitcast(F32), 0.0)
                wait_apart(pool, q_hi, n + 1, consts, 4)
                pool.tensor_tensor(qpad[i][:, :, :, XD:M0], q, qpad[i][:, :, :, 0:XD].bitcast(F32), ALU.subtract).then_inc(padded, 1)
                wait_apart(pool, k_hi, n + 1, consts, 4)
                pool.tensor_tensor(kpad[i][:, :, :, D0:D0 + XD], k, kpad[i][:, :, :, 0:XD].bitcast(F32), ALU.subtract).then_inc(k_padded, 1)

            def lay_v(b, g, n):
                i = g % 2
                rows = slice(b * TB, (b + 1) * TB) if isinstance(b, int) else bass.ds(b * TB, TB)
                if not isinstance(n, int) or n >= 2:
                    wait_apart(pool, pv_done, G * (n - 1), consts, 4)
                pool.tensor_copy(vz[i][:, :, P - VR:].rearrange("p t (h c) -> p t h c", c=P)[:, :, :, 0:XD + 1],
                                 V[:, rows, g * G:(g + 1) * G]).then_inc(v_laid, 1)

            pad(0, 0, 0)
            pool.wait_ge(placed, 3)
            lay_v(0, 0, 0)
            pool.wait_ge(bout_landed, 16)
            for t in range(NT):
                pool.tensor_tensor(X[:, t], X[:, t], bout[:, :], ALU.add).then_inc(biased, 1)

            def body(b, g, n, nxt):
                if nxt:
                    pad(*nxt, n + 1)
                    lay_v(*nxt, n + 1)

            groups(pool, body)

        @block.scalar
        def _(act):
            def keep_k(n, i, r):
                act.wait_ge(k_turned, n + 1)
                if not isinstance(n, int) or n >= 2:
                    act.wait_ge(shifted, G * (n - 1))
                rows = slice(r * R, (r + 1) * R)
                act.copy(kT[i][rows, :, r], p_turn[rows]).then_inc(kT_ready, 1)

            def keep_m(n, i):
                act.wait_ge(m_turned, n + 1)
                if not isinstance(n, int) or n >= 2:
                    act.wait_ge(shifted, G * (n - 1))
                act.copy(qmT[i][:, :, :], p_turn).then_inc(qmT_ready, 1)

            def keep_pv(n, quad):
                act.wait_ge(pv_done, G * n + QUAD * (quad + 1))
                if not isinstance(n, int) or n >= 1:
                    act.wait_ge(backed, 2 * n - 1 + quad)
                act.copy(pvs[quad][:, :], p_pv).then_inc(pv_kept, 1)

            act.wait_ge(placed, 3)
            for r in range(2):
                keep_k(0, 0, r)
            keep_m(0, 0)

            def body(b, g, n, nxt):
                for h in range(G):
                    act.wait_ge(shifted, G * n + h + 1)
                    if not isinstance(n, int) or G * n + h >= 2:
                        act.wait_ge(pv_done, G * n + h - 1)
                    act.activation(probs[h % 2][:, :, :], p_shift[h % 2], ACT.Exp).then_inc(exped, 1)
                    if h in (1, 2) and nxt:
                        keep_k(n + 1, (g + 1) % 2, h - 1)
                    if h == QUAD:
                        keep_pv(n, 0)
                if nxt:
                    keep_m(n + 1, (g + 1) % 2)
                keep_pv(n, 1)

            groups(act, body)

        @block.vector
        def _(dve):
            dve.memset(place[:, :, :].bitcast(F32), 0.0).then_inc(placed, 1)
            for i in range(2):
                dve.memset(kT[i][:, :, :, :].bitcast(F32), 0.0)
                z = dve.memset(vz[i][:, :, :], 0.0)
            z.then_inc(placed, 1)
            dve.wait_ge(consts, 4)
            dve.wait_ge(placed, 1)
            for t in range(TB):
                z = dve.tensor_copy(place[:, t, t * P:(t + 1) * P], ident[:, :])
            z.then_inc(placed, 1)

            def keep_q(n):
                dve.wait_ge(q_turned, n + 1)
                wait(dve, scored, G * n)
                dve.tensor_copy(qT[:, :, :], p_turn).then_inc(qT_ready, 1)

            def row_max(n, h, i):
                dve.wait_ge(scored, G * n + h + 1)
                dve.tensor_reduce(top[i][:, :, h], p_raw[h % 2], AX.X, ALU.max).then_inc(maxed, 1)

            def shift(n, i):
                dve.wait_ge(maxed, G * n + G)
                dve.tensor_scalar(qpad[i][:, :, :, M0], top[i][:, :, :], -1.0, None, ALU.mult).then_inc(shift_hi, 1)
                dve.wait_ge(shift_hi, n + 1)
                dve.scalar_tensor_tensor(out=qpad[i][:, :, :, M0 + 1], in0=top[i][:, :, :], scalar=-1.0,
                                         in1=qpad[i][:, :, :, M0].bitcast(F32), op0=ALU.mult, op1=ALU.subtract).then_inc(shift_lo, 1)

            def write(b, g, n, quad):
                dve.wait_ge(backed, 2 * n + quad + 1)
                wait(dve, written, 2 * n + quad)
                dve.reciprocal(rsum[quad][:, :, :], p_back[:, :, :, XD]).then_inc(inverted, 1)
                dve.wait_ge(inverted, 2 * n + quad + 1)
                dve.tensor_tensor(part(Q, b, g, XD, quad), p_back[:, :, :, 0:XD],
                                  rsum[quad][:, :, :].unsqueeze(3).to_broadcast([P, TB, QUAD, XD]), ALU.mult).then_inc(written, 1)

            keep_q(0)
            for h in range(G):
                row_max(0, h, 0)
            shift(0, 0)

            def body(b, g, n, nxt):
                if nxt:
                    keep_q(n + 1)
                if not (isinstance(n, int) and n == 0):
                    write(b if g else b - 1, (g - 1) % NG, n - 1, 1)
                if nxt:
                    for h in range(G - 2):
                        row_max(n + 1, h, (g + 1) % 2)
                write(b, g, n, 0)
                if nxt:
                    for h in range(G - 2, G):
                        row_max(n + 1, h, (g + 1) % 2)
                    shift(n + 1, (g + 1) % 2)

            groups(dve, body)
            write(B - 1, NG - 1, B * NG - 1, 1)

        @block.tensor
        def _(pe):
            def turn(pad, i, done):
                for j in range(G // 2):
                    for t in range(TB):
                        mm = pe.matmul(p_turn[:, j], pad[i][:, t, 2 * j:2 * j + 2].rearrange("p h r -> p (h r)"), place[:, t],
                                       start=(t == 0), stop=(t == TB - 1))
                mm.then_inc(done, 1)

            def turn_q(n, i):
                pe.wait_ge(padded, n + 1)
                wait(pe, qmT_ready, n)
                turn(qpad, i, q_turned)

            def turn_k(n, i):
                pe.wait_ge(k_padded, n + 1)
                pe.wait_ge(qT_ready, n + 1)
                turn(kpad, i, k_turned)

            def turn_m(n, i):
                pe.wait_ge(shift_lo, n + 1)
                pe.wait_ge(kT_ready, 2 * n + 2)
                turn(qpad, i, m_turned)

            def raw_scores(n, h, i):
                pe.wait_ge(kT_ready, 2 * n + 2)
                if not isinstance(n, int) or G * n + h >= 2:
                    pe.wait_ge(maxed, G * n + h - 1)
                for t in range(TB):
                    mm = pe.matmul(p_raw[h % 2][:, t], qT[:, h // 2, t * P:(t + 1) * P], kT[i][:, h // 2, h % 2], start=True, stop=True)
                mm.then_inc(scored, 1)

            def shifted_scores(n, h, i):
                pe.wait_ge(qmT_ready, n + 1)
                if not isinstance(n, int) or G * n + h >= 2:
                    pe.wait_ge(exped, G * n + h - 1)
                for t in range(TB):
                    mm = pe.matmul(p_shift[h % 2][:, t], kT[i][:, h // 2, h % 2, t * P:(t + 1) * P], qmT[i][:, h // 2], start=True, stop=True)
                mm.then_inc(shifted, 1)

            def values(n, h, i):
                pe.wait_ge(exped, G * n + h + 1)
                quad, j = h // QUAD, h % QUAD
                if j == 0:
                    pe.wait_ge(v_laid, n + 1)
                    wait(pe, pv_kept, 2 * n + quad)
                window = slice(P - VR + h * P - j * VR, P - VR + (h + 1) * P - j * VR)
                for kt in range(TB):
                    mm = pe.matmul(p_pv, vz[i][:, kt, window], probs[h % 2][:, kt],
                                   start=(j == 0 and kt == 0), stop=(j == QUAD - 1 and kt == TB - 1))
                mm.then_inc(pv_done, 1)

            def turn_back(n, quad):
                pe.wait_ge(pv_kept, 2 * n + quad + 1)
                wait(pe, written, 2 * n + quad)
                for t in range(TB):
                    mm = pe.transpose(p_back[:, t].rearrange("p h d -> p (h d)"), pvs[quad][:, t * P:(t + 1) * P], ident[:, :])
                mm.then_inc(backed, 1)

            pe.wait_ge(consts, 4)
            pe.wait_ge(placed, 3)
            turn_q(0, 0)
            turn_k(0, 0)
            for h in range(G):
                raw_scores(0, h, 0)
            turn_m(0, 0)

            def body(b, g, n, nxt):
                i, ni = g % 2, (g + 1) % 2
                for h in range(G):
                    shifted_scores(n, h, i)
                    if h == 0:
                        if nxt:
                            turn_q(n + 1, ni)
                    elif h == 1:
                        if not (isinstance(n, int) and n == 0):
                            turn_back(n - 1, 1)
                        if nxt:
                            turn_k(n + 1, ni)
                    elif h >= 3 and h < 7 and nxt:
                        raw_scores(n + 1, 2 * h - 6, ni)
                    if h == 5 and not nxt:
                        turn_back(n, 0)
                    if h:
                        values(n, h - 1, i)
                    if h >= 3 and h < 7 and nxt:
                        raw_scores(n + 1, 2 * h - 5, ni)
                        if h == 5:
                            turn_back(n, 0)
                if nxt:
                    turn_m(n + 1, ni)
                values(n, G - 1, i)

            groups(pe, body)
            turn_back(B * NG - 1, 1)




def project_attention(nc, X, A, xh, xl, w_out):
    with ExitStack() as ctx:
        def sb(name, shape, dt=F32):
            return ctx.enter_context(nc.sbuf_tensor(name, shape, dt))

        def sem(name):
            return ctx.enter_context(nc.semaphore(name))

        w_raw, wh, wl = sb("wo4_raw", [P, HK, HID]), sb("wo4_h", [P, HK, HID], F32R), sb("wo4_l", [P, HK, HID], F32R)
        ident = sb("ident4", [P, P])
        a_in = [sb(f"a_in{i}", [P, HID]) for i in range(2)]
        a_h = [sb(f"a4_h{i}", [P, HK, P], F32R) for i in range(2)]
        a_l = [sb(f"a4_l{i}", [P, HK, P], F32R) for i in range(2)]
        total = sb("total", [P, HID])
        xn = [sb(f"xn4_{i}", [P, HID]) for i in range(2)]
        stats, mv, std, rstd = sb("stats4", [P, 6]), sb("mv4", [P, 2]), sb("std4", [P, 1]), sb("rstd4", [P, 1])
        banks = ctx.enter_context(nc.psum_tensor("banks4", [P, 8, 512], F32))

        w_landed, w_hi, w_lo, consts = sem("wo4_landed"), sem("wo4_hi"), sem("wo4_lo"), sem("consts4")
        a_copied, a_turned, a_hi, a_lo = sem("a_copied"), sem("a_turned"), sem("a4_hi"), sem("a4_lo")
        out_done, stat, rooted, inverted, xn_ready, x_kept = (sem(n) for n in ("out4", "stat4", "rooted4", "inverted4", "xn4_ready", "x4_kept"))
        summed, x_turned, x_hi, x_lo = sem("summed4"), sem("x4_turned"), sem("x4_hi"), sem("x4_lo")

        block = ctx.enter_context(nc.Block())

        def tiles(eng, body):
            body(0, 0)
            body(1, 1)
            with eng.Fori(1, NT // 2) as p:
                for i in range(2):
                    body(2 * p + i, i)

        def tile_of(ap, t):
            if isinstance(t, int):
                return ap[:, t]
            return ap[:, bass.ds(t, 1)].squeeze(1)

        def columns_of(ap, t):
            return ap[:, :, t * P:(t + 1) * P] if isinstance(t, int) else ap[:, :, bass.ds(t * P, P)]

        @block.sync
        def _(sp):
            sp.dma_start(w_raw[:, :, :], w_out).then_inc(w_landed, 16)

        @block.gpsimd
        def _(pool):
            pool.memset(ident[:, :], 0.0).then_inc(consts, 1)
            pool.wait_ge(consts, 1)
            pool.affine_select(out=ident[:, :], in_=ident[:, :], compare_op=ALU.not_equal, fill=1.0,
                               base=0, pattern=[[-1, P]], channel_multiplier=1).then_inc(consts, 1)
            pool.wait_ge(w_hi, 1)
            pool.tensor_tensor(wl[:, :, :], w_raw[:, :, :], wh[:, :, :].bitcast(F32), ALU.subtract).then_inc(w_lo, 1)

        @block.scalar
        def _(act):
            act.wait_ge(w_landed, 16)
            act.copy(wh[:, :, :], w_raw[:, :, :]).then_inc(w_hi, 1)

            def x_split(t, i):
                act.wait_ge(x_turned, t + 1)
                act.copy(columns_of(xh, t), banks[:, 4 + i].rearrange("p (k s) -> p k s", k=HK)).then_inc(x_hi, 1)

            def body(t, i):
                wait(act, a_turned, t - 1)
                act.copy(a_in[i][:, :], tile_of(A, t)).then_inc(a_copied, 1)
                act.wait_ge(a_turned, t + 1)
                wait(act, out_done, t - 1)
                act.copy(a_h[i][:, :, :], banks[:, i].rearrange("p (k s) -> p k s", k=HK)).then_inc(a_hi, 1)
                if not isinstance(t, int) or t:
                    x_split(t - 1, 1 - i)
                act.wait_ge(stat, 3 * t + 3)
                act.sqrt(std[:, :], std[:, :]).then_inc(rooted, 1)
                act.wait_ge(xn_ready, t + 1)
                act.copy(tile_of(X, t), xn[i][:, :]).then_inc(x_kept, 1)

            tiles(act, body)
            x_split(NT - 1, (NT - 1) % 2)

        @block.vector
        def _(dve):
            def x_split(t, i):
                dve.wait_ge(x_hi, t + 1)
                dve.tensor_tensor(columns_of(xl, t), banks[:, 4 + i].rearrange("p (k s) -> p k s", k=HK),
                                  columns_of(xh, t).bitcast(F32), ALU.subtract).then_inc(x_lo, 1)

            def body(t, i):
                dve.wait_ge(a_hi, t + 1)
                dve.tensor_tensor(a_l[i][:, :, :], banks[:, i].rearrange("p (k s) -> p k s", k=HK),
                                  a_h[i][:, :, :].bitcast(F32), ALU.subtract).then_inc(a_lo, 1)
                if not isinstance(t, int) or t:
                    x_split(t - 1, 1 - i)
                dve.wait_ge(out_done, t + 1)
                wait(dve, xn_ready, t)
                dve.tensor_tensor(total[:, :], banks[:, 2 + i], tile_of(X, t), ALU.add).then_inc(summed, 1)
                dve.wait_ge(summed, t + 1)
                dve.bn_stats(stats[:, :], total[:, :]).then_inc(stat, 1)
                wait_apart(dve, stat, 3 * t + 1, w_landed, 16)
                dve.bn_aggr(mv[:, :], stats[:, :]).then_inc(stat, 1)
                dve.wait_ge(stat, 3 * t + 2)
                dve.tensor_scalar(std[:, :], mv[:, 1:2], LN_EPS, None, ALU.add).then_inc(stat, 1)
                dve.wait_ge(rooted, t + 1)
                dve.reciprocal(rstd[:, :], std[:, :]).then_inc(inverted, 1)
                dve.wait_ge(inverted, t + 1)
                wait(dve, x_turned, t - 1)
                wait(dve, x_kept, t - 1)
                dve.tensor_scalar(xn[i][:, :], total[:, :], mv[:, 0:1], rstd[:, 0:1], ALU.subtract, ALU.mult).then_inc(xn_ready, 1)

            dve.wait_ge(w_landed, 16)
            tiles(dve, body)
            x_split(NT - 1, (NT - 1) % 2)

        @block.tensor
        def _(pe):
            def product(out, pairs):
                terms = [t for lh, ll, rh, rl in pairs for t in ((lh, rl), (ll, rh), (lh, rh))]
                for i, (a, c) in enumerate(terms):
                    mm = pe.matmul(out, a, c, start=(i == 0), stop=(i == len(terms) - 1))
                return mm

            def turn_x(t, i):
                pe.wait_ge(xn_ready, t + 1)
                wait(pe, x_lo, t - 1)
                for k in range(HK):
                    mm = pe.transpose(banks[:, 4 + i, k * P:(k + 1) * P], xn[i][:, k * P:(k + 1) * P], ident[:, :])
                mm.then_inc(x_turned, 1)

            pe.wait_ge(consts, 2)
            pe.wait_ge(w_hi, 1)
            pe.wait_ge(w_lo, 1)

            def body(t, i):
                pe.wait_ge(a_copied, t + 1)
                wait(pe, a_lo, t - 1)
                for k in range(HK):
                    mm = pe.transpose(banks[:, i, k * P:(k + 1) * P], a_in[i][:, k * P:(k + 1) * P], ident[:, :])
                mm.then_inc(a_turned, 1)
                if not isinstance(t, int) or t:
                    turn_x(t - 1, 1 - i)
                pe.wait_ge(a_hi, t + 1)
                pe.wait_ge(a_lo, t + 1)
                wait(pe, summed, t - 1)
                product(banks[:, 2 + i], [(a_h[i][:, k], a_l[i][:, k], wh[:, k], wl[:, k]) for k in range(HK)]).then_inc(out_done, 1)

            tiles(pe, body)
            turn_x(NT - 1, (NT - 1) % 2)


def mixture(nc, X, scratch, xh, xl, gate_cols, expert_bias, w_gu, w_down, out):
    NE = E + 1
    NBLK = 4
    W = T // NBLK
    TPB = W // P
    MK = FF // P
    NONE = 3e38
    with ExitStack() as ctx:
        def sb(name, shape, dt=F32):
            return ctx.enter_context(nc.sbuf_tensor(name, shape, dt))

        def sem(name):
            return ctx.enter_context(nc.semaphore(name))

        flat = scratch[:, :, :].rearrange("p t h -> p (t h)")
        GU = HK * 2 * FF
        gu_raw = flat[:, 0:GU].rearrange("p (k f) -> p k f", k=HK)
        dn_raw = flat[:, GU:GU + MK * HID].rearrange("p (k h) -> p k h", k=MK)
        silu = flat[:, 3072:3072 + 2 * W].rearrange("p (m s) -> p m s", m=MK)
        hid = flat[:, 4096:4096 + 2 * W].rearrange("p (m s) -> p m s", m=MK)
        gu_h = [sb(f"gu_h{i}", [P, HK, 2 * FF], F32R) for i in range(2)]
        gu_l = [sb(f"gu_l{i}", [P, HK, 2 * FF], F32R) for i in range(2)]
        dn_h = [sb(f"dn_h{i}", [P, MK, HID], F32R) for i in range(2)]
        dn_l = [sb(f"dn_l{i}", [P, MK, HID], F32R) for i in range(2)]
        hid_h = [sb(f"hid_h{i}", [P, MK, W], F32R) for i in range(2)]
        hid_l = [sb(f"hid_l{i}", [P, MK, W], F32R) for i in range(2)]
        gw_raw = sb("gw_raw", [P, HK, E])
        gw_h, gw_l = sb("gw_h", [P, HK, E], F32R), sb("gw_l", [P, HK, E], F32R)
        ebias = sb("ebias", [P, E])
        ident = sb("ident5", [P, P])
        lcols = flat[0:E, 5120:5120 + T]
        score = sb("score", [P, NT, E])
        biased = sb("biased", [P, NT, E])
        best = sb("best", [P, NT, 8])
        left = sb("left", [P, NT, E])
        wsum = sb("wsum", [P, NT])
        weight = sb("weight", [P, NE, NT])
        stats, mv, std = sb("stats5", [P, NT, 6]), sb("mv5", [P, NT, 2]), sb("std5", [P, NT])
        banks = ctx.enter_context(nc.psum_tensor("banks5", [P, 8, 512], F32))

        gw_landed, eb_landed = sem("gw_landed"), sem("eb_landed")
        gu_landed, dn_landed = sem("gu_landed"), sem("dn_landed")
        consts, gw_hi, gw_lo = sem("consts5"), sem("gw_hi"), sem("gw_lo")
        gu_hi, gu_lo, dn_hi, dn_lo = sem("gu_hi"), sem("gu_lo"), sem("dn_hi"), sem("dn_lo")
        routed, lcopied, lturned, sigmoided, steps = (sem(n) for n in ("routed", "lcopied", "lturned", "sigmoided", "steps"))
        hidden, silued, gated, h_hi, h_lo = (sem(n) for n in ("hidden", "silued", "gated", "h_hi", "h_lo"))
        down, summed = sem("down"), sem("summed5")
        stat, rooted, normal, stored = sem("stat5"), sem("rooted5"), sem("normal5"), sem("stored")

        block = ctx.enter_context(nc.Block())

        def experts(eng, body):
            body(0, 0)
            body(1, 1)
            with eng.Fori(1, NE // 2) as p:
                for i in range(2):
                    body(2 * p + i, i)
            body(NE - 1, 0)

        def of_expert(ap, e):
            return ap[e] if isinstance(e, int) else ap[bass.ds(e, 1)].squeeze(0)

        @block.sync
        def _(sp):
            sp.dma_start(gw_raw[:, :, :], gate_cols).then_inc(gw_landed, 16)
            sp.dma_start(ebias[:, :], expert_bias.partition_broadcast(P)).then_inc(eb_landed, 16)

            def body(e, i):
                wait(sp, gu_hi, e)
                wait(sp, gu_lo, e)
                sp.dma_start(gu_raw, of_expert(w_gu, e)).then_inc(gu_landed, 16)
                wait(sp, dn_hi, e)
                wait(sp, dn_lo, e)
                sp.dma_start(dn_raw, of_expert(w_down, e)).then_inc(dn_landed, 16)

            experts(sp, body)
            for c in range(NBLK):
                sp.wait_ge(normal, TPB * (c + 1))
                sp.dma_start(out[:, c * TPB:(c + 1) * TPB], X[:, c * TPB:(c + 1) * TPB]).then_inc(stored, 16)
            sp.wait_ge(stored, 16 * NBLK)

        @block.gpsimd
        def _(pool):
            pool.memset(ident[:, :], 0.0).then_inc(consts, 1)
            pool.memset(weight[:, E], 1.0).then_inc(consts, 1)
            pool.wait_ge(consts, 2)
            pool.affine_select(out=ident[:, :], in_=ident[:, :], compare_op=ALU.not_equal, fill=1.0,
                               base=0, pattern=[[-1, P]], channel_multiplier=1).then_inc(consts, 1)
            pool.wait_ge(gw_hi, 1)
            pool.tensor_tensor(gw_l[:, :, :], gw_raw[:, :, :], gw_h[:, :, :].bitcast(F32), ALU.subtract).then_inc(gw_lo, 1)

            def body(e, i):
                pool.wait_ge(gu_hi, e + 1)
                pool.tensor_tensor(gu_l[i][:, :, :], gu_raw, gu_h[i][:, :, :].bitcast(F32), ALU.subtract).then_inc(gu_lo, 1)
                pool.wait_ge(dn_hi, e + 1)
                pool.tensor_tensor(dn_l[i][:, :, :], dn_raw, dn_h[i][:, :, :].bitcast(F32), ALU.subtract).then_inc(dn_lo, 1)

            experts(pool, body)

        @block.scalar
        def _(act):
            act.wait_ge(gw_landed, 16)
            act.copy(gw_h[:, :, :], gw_raw[:, :, :]).then_inc(gw_hi, 1)

            def split(e, i):
                act.wait_ge(gu_landed, 16 * e + 16)
                if not isinstance(e, int) or e >= 2:
                    act.wait_ge(down, TPB * NBLK * (e - 1))
                act.copy(gu_h[i][:, :, :], gu_raw).then_inc(gu_hi, 1)
                act.wait_ge(dn_landed, 16 * e + 16)
                act.copy(dn_h[i][:, :, :], dn_raw).then_inc(dn_hi, 1)

            split(0, 0)
            for c in range(NBLK):
                act.wait_ge(routed, c + 1)
                act.copy(lcols[:, c * W:(c + 1) * W], banks[0:E, c]).then_inc(lcopied, 1)
            act.wait_ge(lturned, 1)
            act.activation(score[:, :, :].rearrange("p t e -> p (t e)"), banks[:, 4, 0:NT * E], ACT.Sigmoid).then_inc(sigmoided, 1)

            def body(e, i):
                for c in range(NBLK):
                    n = NBLK * e + c
                    for m in range(MK):
                        act.wait_ge(hidden, 2 * MK * n + 2 * m + 1)
                        wait(act, gated, MK * n - MK + m + 1 if isinstance(n, int) else MK * n)
                        act.activation(silu[:, m], banks[:, 2 * m], ACT.Silu).then_inc(silued, 1)
                    for m in range(MK):
                        act.wait_ge(gated, MK * n + m + 1)
                        if not isinstance(n, int) or n >= 2:
                            act.wait_ge(down, TPB * (n - 1))
                        act.copy(hid_h[c % 2][:, m], hid[:, m]).then_inc(h_hi, 1)
                    if c == 0 and not (isinstance(e, int) and e == NE - 1):
                        split(e + 1, 1 - i)

            experts(act, body)
            act.wait_ge(stat, 2 * NT + 1)
            act.sqrt(std[:, :], std[:, :]).then_inc(rooted, 1)

        @block.vector
        def _(dve):
            dve.wait_ge(eb_landed, 16)
            dve.wait_ge(sigmoided, 1)
            n_steps = [0]

            def step(ins):
                n_steps[0] += 1
                ins.then_inc(steps, 1)
                dve.wait_ge(steps, n_steps[0])

            step(dve.tensor_tensor(biased[:, :, :], score[:, :, :], ebias[:, :].unsqueeze(1).to_broadcast([P, NT, E]), ALU.add))
            for t in range(NT):
                ins = dve.max(best[:, t], biased[:, t])
            step(ins)
            step(dve.memset(best[:, :, TOPK:], NONE))
            for t in range(NT):
                ins = dve.match_replace(left[:, t], best[:, t], biased[:, t], -NONE)
            step(ins)
            step(dve.tensor_tensor(left[:, :, :], left[:, :, :], biased[:, :, :], ALU.not_equal))
            step(dve.tensor_tensor(left[:, :, :], left[:, :, :], score[:, :, :], ALU.mult))
            step(dve.tensor_reduce(wsum[:, :], left[:, :, :], AX.X, ALU.add))
            step(dve.reciprocal(wsum[:, :], wsum[:, :]))
            dve.wait_ge(consts, 3)
            step(dve.tensor_tensor(weight[:, 0:E].rearrange("p e t -> p t e"), left[:, :, :],
                                   wsum[:, :].unsqueeze(2).to_broadcast([P, NT, E]), ALU.mult))

            def add_down(e, c):
                n = NBLK * e + c
                for t in range(TPB):
                    tile = c * TPB + t
                    dve.wait_ge(down, TPB * n + t + 1)
                    w = weight[:, e, tile:tile + 1] if isinstance(e, int) else weight[:, bass.ds(e, 1), tile]
                    dve.scalar_tensor_tensor(out=X[:, tile], in0=banks[:, 4 + t], scalar=w, in1=X[:, tile],
                                             op0=ALU.mult, op1=ALU.add).then_inc(summed, 1)

            def body(e, i):
                first = isinstance(e, int) and e == 0
                for c in range(NBLK):
                    n = NBLK * e + c
                    for m in range(MK):
                        dve.wait_ge(hidden, 2 * MK * n + 2 * m + 2)
                        dve.wait_ge(silued, MK * n + m + 1)
                        if not isinstance(n, int) or n >= 1:
                            dve.wait_ge(h_hi, MK * n)
                            dve.wait_ge(h_lo, MK * n)
                        dve.tensor_tensor(hid[:, m], silu[:, m], banks[:, 2 * m + 1], ALU.mult).then_inc(gated, 1)
                    for m in range(MK):
                        dve.wait_ge(h_hi, MK * n + m + 1)
                        dve.tensor_tensor(hid_l[c % 2][:, m], hid[:, m], hid_h[c % 2][:, m].bitcast(F32), ALU.subtract).then_inc(h_lo, 1)
                    if not (first and c == 0):
                        add_down(e if c else e - 1, c - 1 if c else NBLK - 1)

            experts(dve, body)
            add_down(NE - 1, NBLK - 1)
            for t in range(NT):
                dve.wait_ge(summed, TPB * NBLK * (NE - 1) + t + 1)
                dve.bn_stats(stats[:, t], X[:, t]).then_inc(stat, 1)
            for t in range(NT):
                dve.wait_ge(stat, t + 1)
                dve.bn_aggr(mv[:, t], stats[:, t]).then_inc(stat, 1)
            dve.wait_ge(stat, 2 * NT)
            dve.tensor_scalar(std[:, :], mv[:, :, 1], LN_EPS, None, ALU.add).then_inc(stat, 1)
            dve.wait_ge(rooted, 1)
            dve.reciprocal(std[:, :], std[:, :]).then_inc(rooted, 1)
            dve.wait_ge(rooted, 2)
            for t in range(NT):
                dve.tensor_scalar(X[:, t], X[:, t], mv[:, t, 0:1], std[:, t:t + 1], ALU.subtract, ALU.mult).then_inc(normal, 1)

        @block.tensor
        def _(pe):
            def product(out, pairs):
                terms = [t for lh, ll, rh, rl in pairs for t in ((lh, rl), (ll, rh), (lh, rh))]
                for i, (a, c) in enumerate(terms):
                    mm = pe.matmul(out, a, c, start=(i == 0), stop=(i == len(terms) - 1))
                return mm

            pe.wait_ge(consts, 3)
            pe.wait_ge(gw_hi, 1)
            pe.wait_ge(gw_lo, 1)
            for c in range(NBLK):
                s = slice(c * W, (c + 1) * W)
                product(banks[0:E, c], [(gw_h[:, k], gw_l[:, k], xh[:, k, s], xl[:, k, s]) for k in range(HK)]).then_inc(routed, 1)
            for t in range(NT):
                pe.wait_ge(lcopied, t * P // W + 1)
                mm = pe.transpose(banks[:, 4, t * E:(t + 1) * E], lcols[:, t * P:(t + 1) * P], ident[0:E, 0:E])
            mm.then_inc(lturned, 1)

            def hidden_block(e, i, c):
                n = NBLK * e + c
                s = slice(c * W, (c + 1) * W)
                for m in range(MK):
                    for j in range(2):
                        if not isinstance(n, int) or n >= 1:
                            pe.wait_ge(gated, MK * n - MK + m + 1 if isinstance(n, int) else MK * (n - 1) + m + 1)
                        f = slice(j * FF + m * P, j * FF + (m + 1) * P)
                        product(banks[:, 2 * m + j], [(gu_h[i][:, k, f], gu_l[i][:, k, f], xh[:, k, s], xl[:, k, s]) for k in range(HK)]).then_inc(hidden, 1)

            def down_block(e, i, c):
                n = NBLK * e + c
                pe.wait_ge(h_hi, MK * n + MK)
                pe.wait_ge(h_lo, MK * n + MK)
                for t in range(TPB):
                    if not isinstance(n, int) or n >= 1:
                        pe.wait_ge(summed, TPB * (n - 1) + t + 1)
                    else:
                        pe.wait_ge(sigmoided, 1)
                    s = slice(t * P, (t + 1) * P)
                    product(banks[:, 4 + t], [(hid_h[c % 2][:, m, s], hid_l[c % 2][:, m, s], dn_h[i][:, m], dn_l[i][:, m]) for m in range(MK)]).then_inc(down, 1)

            def body(e, i):
                pe.wait_ge(gu_hi, e + 1)
                pe.wait_ge(gu_lo, e + 1)
                for c in range(NBLK):
                    hidden_block(e, i, c)
                    if c == 0:
                        if not (isinstance(e, int) and e == 0):
                            down_block(e - 1, 1 - i, NBLK - 1)
                        pe.wait_ge(dn_hi, e + 1)
                        pe.wait_ge(dn_lo, e + 1)
                    else:
                        down_block(e, i, c - 1)

            pe.wait_ge(lcopied, NBLK)
            experts(pe, body)
            down_block(NE - 1, 0, NBLK - 1)


def decoder_layer(nc, x_cols, x_tok, w_qkv, b_qkv, w_attn_out, ctx_cols, pos, w_q, w_k, w_v, w_out, b_out,
                  gate_cols, expert_bias, w_gu, w_down, out):
    with ExitStack() as ctx:
        def sb(name, shape, dt=F32):
            return ctx.enter_context(nc.sbuf_tensor(name, shape, dt))

        X = sb("X", [P, NT, HID])
        linear_attention(nc, X, x_cols, x_tok, w_qkv, b_qkv, w_attn_out)
        Q = sb("Q", [P, NT, HID])
        with ExitStack() as inner:
            K = inner.enter_context(nc.sbuf_tensor("K", [P, NT, HID], F32))
            V = inner.enter_context(nc.sbuf_tensor("V", [P, NT, XH, XD + 1], F32))
            project_context(nc, X, Q, K, V, ctx_cols, pos, w_q, w_k, w_v)
            softmax_attention(nc, X, Q, K, V, b_out)
        xh = sb("x2h", [P, HK, T], F32R)
        xl = sb("x2l", [P, HK, T], F32R)
        project_attention(nc, X, Q, xh, xl, w_out)
        mixture(nc, X, Q, xh, xl, gate_cols, expert_bias, w_gu, w_down, out)


def kernel(**inputs):
    import concourse.bacc as _bacc
    from concourse.bass_utils import run_bass_kernel_spmd as _run

    a = {name: np.asarray(value) for name, value in inputs.items()}

    def rows(w):
        return w.reshape(-1, P, w.shape[-1]).transpose(1, 0, 2)

    def rotary(w):
        return w.reshape(w.shape[0], XH, 2, XD // 4, 2).transpose(0, 1, 4, 2, 3).reshape(w.shape)

    x = a["x"].reshape(T, HID)
    grouped = [a["L0_attn_Wq"].reshape(KVG, GROUP * DH, HID), a["L0_attn_Wk"].reshape(KVG, DH, HID),
               a["L0_attn_Wv"].reshape(KVG, DH, HID)]
    biases = [a["L0_attn_bq"].reshape(KVG, GROUP, DH), a["L0_attn_bk"].reshape(KVG, 1, DH), a["L0_attn_bv"].reshape(KVG, 1, DH)]
    w_kv = a["L0_xattn_Wkv"]
    gate = np.concatenate([a["L0_ffn_w_gate"], a["L0_ffn_sw_gate"][None]])
    up = np.concatenate([a["L0_ffn_w_up"], a["L0_ffn_sw_up"][None]])
    down = np.concatenate([a["L0_ffn_w_down"], a["L0_ffn_sw_down"][None]])
    laid = {
        "x_cols": rows(x.T),
        "x_tok": rows(x),
        "w_qkv": np.concatenate(grouped, 1).transpose(0, 2, 1).reshape(KVG, HK, P, -1).transpose(0, 2, 1, 3),
        "b_qkv": np.concatenate(biases, 1).transpose(2, 0, 1),
        "w_attn_out": a["L0_attn_Wo"].T.reshape(KVG, GROUP, P, HID).transpose(0, 2, 1, 3),
        "ctx_cols": rows(a["ctx_1024"].reshape(T, CTX).T),
        "pos": rows(a["fside_BxSx2_0"].reshape(T, 2)),
        "w_q": rows(rotary(a["L0_xattn_Wq"])),
        "w_k": rows(rotary(w_kv[:, :HID])),
        "w_v": rows(w_kv[:, HID:]),
        "w_out": rows(a["L0_xattn_Wout"]),
        "b_out": a["L0_xattn_bout"],
        "gate_cols": rows(a["L0_ffn_gate_w"].T),
        "expert_bias": a["L0_ffn_expert_bias"],
        "w_gu": np.concatenate([gate, up], 1).transpose(0, 2, 1).reshape(E + 1, HK, P, 2 * FF).transpose(0, 2, 1, 3),
        "w_down": down.transpose(0, 2, 1).reshape(E + 1, FF // P, P, HID).transpose(0, 2, 1, 3),
    }
    nc = _bacc.Bacc("TRN2", target_bir_lowering=False, num_devices=1)
    arrays, args = {}, []
    for name, value in laid.items():
        arrays[f"in_{name}"] = np.ascontiguousarray(value)
        args.append(nc.dram_tensor(f"in_{name}", value.shape, mybir.dt.from_np(value.dtype), kind="ExternalInput").ap())
    args.append(nc.dram_tensor("out_x", (P, NT, HID), F32, kind="ExternalOutput").ap())
    decoder_layer(nc, *args)
    got = _run(nc, [arrays], core_ids=[0]).results[0]["out_x"]
    return got.transpose(1, 0, 2).reshape(B, S, HID)
```

```python
from contextlib import ExitStack

import numpy as np
import concourse.bass as bass
from concourse import mybir

ALU = mybir.AluOpType
ACT = mybir.ActivationFunctionType
AX = mybir.AxisListType
F32 = mybir.dt.float32
F32R = mybir.dt.float32r

P = 128
B, S, HID = 8, 256, 512
T = B * S
NT = T // P
HK = HID // P
KVG, GROUP, DH = 4, 4, 128
NORM_EPS = 1e-6
LN_EPS = 1e-5
XH, XD = 32, 16
CTX = 256
CK = CTX // P
E, TOPK, FF = 16, 4, 256
TB = S // P


def wait(eng, sem, value):
    if not isinstance(value, int) or value > 0:
        eng.wait_ge(sem, value)


def wait_apart(eng, sem, value, met, count):
    if not isinstance(value, int):
        value = eng.to_reg(value)
    eng.wait_ge(met, count)
    eng.wait_ge(sem, value)


def linear_attention(nc, X, x_cols, x_tok, w_qkv, b_q, b_kv, w_out):
    KV = 2 * DH
    QW = GROUP * DH
    KH, KL, VH, ONE, KVW = 0, DH, 2 * DH, 4 * DH, 4 * DH + 2
    SW = KVW - VH
    with ExitStack() as ctx:
        def sb(name, shape, dt=F32):
            return ctx.enter_context(nc.sbuf_tensor(name, shape, dt))

        def sem(name):
            return ctx.enter_context(nc.semaphore(name))

        xh = sb("xh", [P, HK, T], F32R)
        xl = sb("xl", [P, HK, T], F32R)
        x_raw = sb("x_raw", [P, 2, HK, S])
        w_raw = sb("w_raw", [P, HK, QW + KV])
        wo_raw = sb("wo_raw", [P, GROUP, HID])
        wh = sb("wh", [P, HK, QW + KV], F32R)
        wl = sb("wl", [P, HK, QW + KV], F32R)
        woh = sb("woh", [P, GROUP, HID], F32R)
        wol = sb("wol", [P, GROUP, HID], F32R)
        bias = sb("bias", [P, KVG, GROUP])
        bias1 = sb("bias1", [P, KVG, GROUP])
        bias_kv = sb("bias_kv", [P, KVG * KV])
        ones = sb("ones", [P, GROUP])
        pick_r = sb("pick_r", [GROUP, GROUP, P], F32R)
        ykv = sb("ykv", [P, TB, KV])
        ek = sb("ek", [P, TB, DH])
        kvs = sb("kvs", [P, TB, KVW], F32R)
        feat = sb("feat", [P, GROUP, S])
        qh = sb("qh", [P, GROUP, S], F32R)
        ql = sb("ql", [P, GROUP, S], F32R)
        ssum = sb("ssum", [P, DH])
        ksum = sb("ksum", [P, 1])
        kvh = sb("kvh", [P, DH], F32R)
        kvl = sb("kvl", [P, DH], F32R)
        kselh = sb("kselh", [P, GROUP, GROUP + 1], F32R)
        ksell = sb("ksell", [P, GROUP, GROUP + 1], F32R)
        rec = sb("rec", [GROUP, S])
        rech = sb("rech", [GROUP, S], F32R)
        recl = sb("recl", [GROUP, S], F32R)
        at = sb("at", [P, GROUP, S])
        ah = sb("ah", [P, GROUP, S], F32R)
        al = sb("al", [P, GROUP, S], F32R)

        pick = at[0:GROUP, 0:2].rearrange("p i (j s) -> p (i j) s", j=2)

        banks = ctx.enter_context(nc.psum_tensor("banks", [P, 8, 512], F32))
        p_kv = banks[:, 0].rearrange("p (t c) -> p t c", t=TB)
        p_q = [banks[:, 1 + i].rearrange("p (i s) -> p i s", i=2) for i in range(2)]
        p_num = [banks[:, 3 + i] for i in range(2)]
        p_rec = [banks[:, 5 + i] for i in range(2)]
        p_out = [banks[:, 5], banks[:, 6]]
        p_state = banks[:, 7, 0:SW]
        p_norm = banks[0:GROUP, 7, 0:S]

        x_landed = [sem("x_landed0"), sem("x_landed1")]
        xtok_landed, bias_landed, bkv_landed = sem("xtok_landed"), sem("bias_landed"), sem("bkv_landed")
        w_landed, wo_landed = [sem("wkv_landed"), sem("wq_landed")], sem("wo_landed")
        x_hi, x_lo = sem("x_hi"), sem("x_lo")
        w_hi, w_lo = [sem("wkv_hi"), sem("wq_hi")], [sem("wkv_lo"), sem("wq_lo")]
        wo_hi, wo_lo = sem("wo_hi"), sem("wo_lo")
        consts, bias1_ready, zeroed = sem("consts"), sem("bias1_ready"), sem("zeroed")
        projected, kv_biased = sem("projected"), sem("kv_biased")
        clipped, exped, feat_k, feat_q = sem("clipped"), sem("exped"), sem("feat_k"), sem("feat_q")
        kv_hi, kv_lo, q_hi, q_lo = sem("kv_hi"), sem("kv_lo"), sem("q_hi"), sem("q_lo")
        state, state_sum, state_hi, state_lo = sem("state"), sem("state_sum"), sem("state_hi"), sem("state_lo")
        normed, norm_read, inverted, rec_hi, rec_lo = sem("normed"), sem("norm_read"), sem("inverted"), sem("rec_hi"), sem("rec_lo")
        applied, num_kept, spread, attended, a_hi, a_lo = (sem("applied"), sem("num_kept"), sem("spread"), sem("attended"),
                                                           sem("a_hi"), sem("a_lo"))
        out_done, added = sem("out_done"), sem("added")

        block = ctx.enter_context(nc.Block())

        def steps(eng, group):
            group(0)
            with eng.Fori(1, KVG) as g:
                group(g)

        def halves(lo):
            return kvs[:, :, 0:ONE].rearrange("p t (c l d) -> p t c l d", c=2, l=2)[:, :, :, lo]

        def by_kind(ap):
            return ap[:, :, :].rearrange("p t (c d) -> p t c d", c=2)

        W_COLS = [slice(QW, QW + KV), slice(0, QW)]

        @block.sync
        def _(sp):
            def load_w(g, part):
                sp.dma_start(w_raw[:, :, W_COLS[part]], w_qkv[g][:, :, W_COLS[part]]).then_inc(w_landed[part], 16)

            load_w(0, 0)
            sp.dma_start(x_raw[:, 0], x_cols[:, :, 0:S]).then_inc(x_landed[0], 16)
            sp.dma_start(bias_kv[:, :], b_kv.partition_broadcast(P)).then_inc(bkv_landed, 16)
            load_w(0, 1)
            sp.dma_start(bias[:, :, :], b_q).then_inc(bias_landed, 16)
            sp.dma_start(x_raw[:, 1], x_cols[:, :, S:2 * S]).then_inc(x_landed[1], 16)
            sp.dma_start(wo_raw[:, :, :], w_out[0]).then_inc(wo_landed, 16)
            sp.dma_start(X[:, :, :], x_tok).then_inc(xtok_landed, 16)
            for b in range(2, B):
                sp.wait_ge(x_hi, b - 1)
                sp.wait_ge(x_lo, b - 1)
                sp.dma_start(x_raw[:, b % 2], x_cols[:, :, b * S:(b + 1) * S]).then_inc(x_landed[b % 2], 16)
            for g in range(1, KVG):
                for part in range(2):
                    sp.wait_ge(w_hi[part], g)
                    sp.wait_ge(w_lo[part], g)
                    load_w(g, part)
                sp.wait_ge(wo_hi, g)
                sp.wait_ge(wo_lo, g)
                sp.dma_start(wo_raw[:, :, :], w_out[g]).then_inc(wo_landed, 16)

        @block.gpsimd
        def _(pool):
            pool.memset(ones[:, :], 1.0).then_inc(consts, 1)
            pool.memset(pick, 0.0).then_inc(consts, 1)
            pool.wait_ge(consts, 2)
            pool.affine_select(out=pick, in_=pick, compare_op=ALU.not_equal, fill=1.0,
                               base=0, pattern=[[-1, GROUP], [0, P]], channel_multiplier=1).then_inc(consts, 1)

            def split_x(b):
                pool.wait_ge(x_hi, b + 1)
                pool.tensor_tensor(xl[:, :, b * S:(b + 1) * S], x_raw[:, b % 2],
                                   xh[:, :, b * S:(b + 1) * S].bitcast(F32), ALU.subtract).then_inc(x_lo, 1)

            def group(g):
                for b in range(B):
                    n = B * g + b
                    if b == 0:
                        if isinstance(g, int):
                            split_x(0)
                        pool.wait_ge(w_hi[1], g + 1)
                        w = W_COLS[1]
                        pool.tensor_tensor(wl[:, :, w], w_raw[:, :, w], wh[:, :, w].bitcast(F32), ALU.subtract).then_inc(w_lo[1], 1)
                    pool.wait_ge(kv_hi, n + 1)
                    pool.tensor_tensor(halves(1), by_kind(ykv), halves(0).bitcast(F32), ALU.subtract).then_inc(kv_lo, 1)
                    for i in range(2):
                        pool.wait_ge(q_hi, 2 * n + i + 1)
                        pool.tensor_tensor(ql[:, 2 * i:2 * i + 2], feat[:, 2 * i:2 * i + 2],
                                           qh[:, 2 * i:2 * i + 2].bitcast(F32), ALU.subtract).then_inc(q_lo, 1)
                        if i == 0 and isinstance(g, int) and b + 1 < B:
                            split_x(b + 1)
                    if b == 0:
                        pool.wait_ge(wo_hi, g + 1)
                        pool.tensor_tensor(wol[:, :, :], wo_raw[:, :, :], woh[:, :, :].bitcast(F32), ALU.subtract).then_inc(wo_lo, 1)

            steps(pool, group)

        @block.scalar
        def _(act):
            def split_x(b):
                act.wait_ge(x_landed[b % 2], 16 * (b // 2 + 1))
                act.copy(xh[:, :, b * S:(b + 1) * S], x_raw[:, b % 2]).then_inc(x_hi, 1)

            def split_w(g, part):
                act.wait_ge(w_landed[part], 16 * (g + 1))
                wait(act, projected, 3 * B * g)
                act.copy(wh[:, :, W_COLS[part]], w_raw[:, :, W_COLS[part]]).then_inc(w_hi[part], 1)

            def attn_hi(m):
                for i in range(2):
                    act.wait_ge(attended, 2 * m + i + 1)
                    wait(act, out_done, 2 * m)
                    act.copy(ah[:, 2 * i:2 * i + 2], at[:, 2 * i:2 * i + 2]).then_inc(a_hi, 1)

            def keep_num(m):
                act.wait_ge(applied, m + 1)
                wait(act, a_lo, 2 * m)
                for i in range(2):
                    act.copy(at[:, 2 * i:2 * i + 2].rearrange("p i s -> p (i s)"), p_num[i]).then_inc(num_kept, 1)

            def group(g):
                for b in range(B):
                    n = B * g + b
                    first = isinstance(n, int) and n == 0
                    if b == 0:
                        split_w(g, 0)
                        if first:
                            split_x(0)
                        split_w(g, 1)
                    act.wait_ge(clipped, 3 * n + 1)
                    act.activation(ek[:, :, :], ek[:, :, :], ACT.Exp).then_inc(exped, 1)
                    act.wait_ge(feat_k, n + 1)
                    wait(act, state, n)
                    act.copy(halves(0), by_kind(ykv)).then_inc(kv_hi, 1)
                    if not first:
                        keep_num(n - 1)
                    for i in range(2):
                        act.wait_ge(clipped, 3 * n + 2 + i)
                        act.activation(feat[:, 2 * i:2 * i + 2], feat[:, 2 * i:2 * i + 2], ACT.Exp).then_inc(exped, 1)
                        act.wait_ge(feat_q, 2 * n + i + 1)
                        wait(act, applied, n)
                        act.copy(qh[:, 2 * i:2 * i + 2], feat[:, 2 * i:2 * i + 2]).then_inc(q_hi, 1)
                        if i == 0:
                            if not first:
                                attn_hi(n - 1)
                            if isinstance(g, int) and b + 1 < B:
                                split_x(b + 1)
                    if b == 0:
                        act.wait_ge(wo_landed, 16 * (g + 1))
                        wait(act, out_done, 2 * B * g)
                        act.copy(woh[:, :, :], wo_raw[:, :, :]).then_inc(wo_hi, 1)

            steps(act, group)
            keep_num(KVG * B - 1)
            attn_hi(KVG * B - 1)

        @block.vector
        def _(dve):
            def invert_norm(m):
                dve.wait_ge(normed, m + 1)
                dve.tensor_scalar(rec[:, :], p_norm, NORM_EPS, None, ALU.add).then_inc(norm_read, 1)
                dve.wait_ge(norm_read, m + 1)
                dve.reciprocal(rec[:, :], rec[:, :]).then_inc(inverted, 1)
                dve.wait_ge(inverted, m + 1)
                wait(dve, spread, m)
                dve.tensor_copy(rech[:, :], rec[:, :]).then_inc(rec_hi, 1)
                dve.wait_ge(rec_hi, m + 1)
                dve.tensor_tensor(recl[:, :], rec[:, :], rech[:, :].bitcast(F32), ALU.subtract).then_inc(rec_lo, 1)

            def attend(m):
                dve.wait_ge(spread, m + 1)
                dve.wait_ge(num_kept, 2 * m + 2)
                for i in range(2):
                    dve.tensor_tensor(at[:, 2 * i:2 * i + 2].rearrange("p i s -> p (i s)"), p_rec[i],
                                      at[:, 2 * i:2 * i + 2].rearrange("p i s -> p (i s)"), ALU.mult).then_inc(attended, 1)
                for i in range(2):
                    dve.wait_ge(a_hi, 2 * m + i + 1)
                    dve.tensor_tensor(al[:, 2 * i:2 * i + 2], at[:, 2 * i:2 * i + 2], ah[:, 2 * i:2 * i + 2].bitcast(F32),
                                      ALU.subtract).then_inc(a_lo, 1)

            def add_out(m, b):
                for t in range(TB):
                    dve.wait_ge(out_done, 2 * m + t + 1)
                    dve.tensor_tensor(X[:, b * TB + t], X[:, b * TB + t], p_out[t], ALU.add).then_inc(added, 1)

            def scalar_of(ap, g, h):
                return ap[:, g, h:h + 1] if isinstance(g, int) else ap[:, bass.ds(g, 1), h]

            def q_features(g, n, i):
                dve.wait_ge(projected, 3 * n + 2 + i)
                wait(dve, q_lo, 2 * n - 1 + i)
                for j in range(2):
                    c = dve.tensor_scalar(feat[:, 2 * i + j], p_q[i][:, j], scalar_of(bias, g, 2 * i + j), 0.0, ALU.add, ALU.min)
                c.then_inc(clipped, 1)
                dve.wait_ge(exped, 3 * n + 2 + i)
                for j in range(2):
                    f = dve.scalar_tensor_tensor(out=feat[:, 2 * i + j], in0=p_q[i][:, j], scalar=scalar_of(bias1, g, 2 * i + j),
                                                 in1=feat[:, 2 * i + j], op0=ALU.add, op1=ALU.max)
                f.then_inc(feat_q, 1)

            def split_state(n):
                dve.wait_ge(state, n + 1)
                dve.tensor_copy(ksum[:, :], p_state[:, 2 * DH:2 * DH + 1]).then_inc(state_sum, 1)
                dve.tensor_copy(ssum[:, :], p_state[:, 0:DH]).then_inc(state_sum, 1)
                dve.wait_ge(state_sum, 3 * n + 2)
                dve.tensor_tensor(ssum[:, :], p_state[:, DH:2 * DH], ssum[:, :], ALU.add).then_inc(state_sum, 1)
                wait(dve, applied, n)
                dve.tensor_scalar(kselh[:, :, 0], ones[:, :], ksum[:, 0:1], None, ALU.mult)
                dve.wait_ge(state_sum, 3 * n + 3)
                dve.tensor_copy(kvh[:, :], ssum[:, :]).then_inc(state_hi, 1)
                dve.wait_ge(state_hi, n + 1)
                dve.tensor_scalar(ksell[:, :, 0], kselh[:, :, 0].bitcast(F32), -1.0, ksum[:, 0:1], ALU.mult, ALU.add)
                dve.tensor_tensor(kvl[:, :], ssum[:, :], kvh[:, :].bitcast(F32), ALU.subtract).then_inc(state_lo, 1)

            dve.memset(kselh[:, :, :].bitcast(F32), 0.0)
            dve.memset(ksell[:, :, :].bitcast(F32), 0.0)
            dve.memset(kvs[:, :, ONE:].bitcast(F32), 1.0).then_inc(zeroed, 1)
            dve.wait_ge(zeroed, 1)
            dve.wait_ge(consts, 3)
            dve.tensor_copy(pick_r[:, :, :], pick).then_inc(zeroed, 1)

            def group(g):
                for b in range(B):
                    n = B * g + b
                    first = isinstance(n, int) and n == 0
                    if b == 0:
                        dve.wait_ge(w_hi[0], g + 1)
                        w = W_COLS[0]
                        dve.tensor_tensor(wl[:, :, w], w_raw[:, :, w], wh[:, :, w].bitcast(F32), ALU.subtract).then_inc(w_lo[0], 1)
                        if first:
                            dve.wait_ge(bkv_landed, 16)
                            dve.wait_ge(bias_landed, 16)
                            dve.tensor_scalar(bias1[:, :, :], bias[:, :, :], 1.0, None, ALU.add).then_inc(bias1_ready, 1)
                            dve.wait_ge(bias1_ready, 1)
                    dve.wait_ge(projected, 3 * n + 1)
                    wait(dve, kv_lo, n)
                    cols = slice(g * KV, (g + 1) * KV) if isinstance(g, int) else bass.ds(g * KV, KV)
                    dve.tensor_tensor(ykv[:, :, :], p_kv, bias_kv[:, cols].unsqueeze(1).to_broadcast([P, TB, KV]), ALU.add).then_inc(kv_biased, 1)
                    dve.wait_ge(kv_biased, n + 1)
                    dve.tensor_scalar(ek[:, :, :], ykv[:, :, 0:DH], 0.0, None, ALU.min).then_inc(clipped, 1)
                    dve.wait_ge(exped, 3 * n + 1)
                    dve.scalar_tensor_tensor(out=ykv[:, :, 0:DH], in0=ykv[:, :, 0:DH], scalar=1.0, in1=ek[:, :, :],
                                             op0=ALU.add, op1=ALU.max).then_inc(feat_k, 1)
                    if not first:
                        invert_norm(n - 1)
                    q_features(g, n, 0)
                    if not first:
                        attend(n - 1)
                    q_features(g, n, 1)
                    split_state(n)
                    if not first:
                        if isinstance(n, int) and n == 1:
                            dve.wait_ge(xtok_landed, 16)
                        add_out(n - 1, (b - 1) % B)

            steps(dve, group)
            invert_norm(KVG * B - 1)
            attend(KVG * B - 1)
            add_out(KVG * B - 1, B - 1)

        @block.tensor
        def _(pe):
            def product(out, pairs):
                terms = [t for lh, ll, rh, rl in pairs for t in ((lh, rl), (ll, rh), (lh, rh))]
                for i, (a, c) in enumerate(terms):
                    mm = pe.matmul(out, a, c, start=(i == 0), stop=(i == len(terms) - 1))
                return mm

            def project_kv(b):
                for t in range(TB):
                    tok = slice(b * S + t * P, b * S + (t + 1) * P)
                    mm = product(p_kv[:, t], [(xh[:, k, tok], xl[:, k, tok], wh[:, k, W_COLS[0]], wl[:, k, W_COLS[0]]) for k in range(HK)])
                mm.then_inc(projected, 1)

            def project_q(b, i):
                cols = slice(b * S, (b + 1) * S)
                for j in range(2):
                    w = slice((2 * i + j) * DH, (2 * i + j + 1) * DH)
                    mm = product(p_q[i][:, j], [(wh[:, k, w], wl[:, k, w], xh[:, k, cols], xl[:, k, cols]) for k in range(HK)])
                mm.then_inc(projected, 1)

            def apply_state(m):
                pe.wait_ge(q_lo, 2 * m + 2)
                pe.wait_ge(q_hi, 2 * m + 2)
                pe.wait_ge(state_lo, m + 1)
                sel = [s[:, :, :].rearrange("p a b -> p (a b)") for s in (kselh, ksell)]
                product(p_norm, [(sel[0][:, GROUP * h:GROUP * (h + 1)], sel[1][:, GROUP * h:GROUP * (h + 1)], qh[:, h], ql[:, h])
                                 for h in range(GROUP)]).then_inc(normed, 1)
                wait(pe, num_kept, 2 * m)
                for i in range(2):
                    pair = [s[:, 2 * i:2 * i + 2].rearrange("p i s -> p (i s)") for s in (qh, ql)]
                    mm = product(p_num[i], [(kvh[:, :], kvl[:, :], pair[0], pair[1])])
                mm.then_inc(applied, 1)

            def spread_norm(m):
                pe.wait_ge(rec_lo, m + 1)
                wait(pe, added, 2 * m)
                for h in range(GROUP):
                    out = p_rec[h // 2][:, h % 2 * S:(h % 2 + 1) * S]
                    pe.matmul(out, pick_r[:, h], recl[:, :], start=True, stop=False)
                    mm = pe.matmul(out, pick_r[:, h], rech[:, :], start=False, stop=True)
                mm.then_inc(spread, 1)

            def form_state(n):
                pe.wait_ge(kv_hi, n + 1)
                pe.wait_ge(kv_lo, n + 1)
                wait(pe, norm_read, n)
                terms = [(t, half) for t in range(TB) for half in (KL, KH)]
                for j, (t, half) in enumerate(terms):
                    mm = pe.matmul(p_state, kvs[:, t, half:half + DH], kvs[:, t, VH:], start=(j == 0), stop=(j == len(terms) - 1))
                mm.then_inc(state, 1)

            def project_out(m):
                pe.wait_ge(a_lo, 2 * m + 2)
                for t in range(TB):
                    s = slice(t * P, (t + 1) * P)
                    product(p_out[t], [(ah[:, h, s], al[:, h, s], woh[:, h], wol[:, h]) for h in range(GROUP)]).then_inc(out_done, 1)

            pe.wait_ge(zeroed, 2)

            def group(g):
                for b in range(B):
                    n = B * g + b
                    first = isinstance(n, int) and n == 0
                    if b == 0:
                        pe.wait_ge(w_hi[0], g + 1)
                        pe.wait_ge(w_lo[0], g + 1)
                    if isinstance(g, int):
                        pe.wait_ge(x_hi, b + 1)
                        pe.wait_ge(x_lo, b + 1)
                    wait(pe, kv_biased, n)
                    project_kv(b)
                    if not first:
                        apply_state(n - 1)
                    if b == 0:
                        pe.wait_ge(w_hi[1], g + 1)
                        pe.wait_ge(w_lo[1], g + 1)
                    wait(pe, feat_q, 2 * n - 1)
                    project_q(b, 0)
                    if not first:
                        spread_norm(n - 1)
                    wait(pe, feat_q, 2 * n)
                    project_q(b, 1)
                    form_state(n)
                    if not first:
                        if b == 1:
                            pe.wait_ge(wo_hi, g + 1)
                            pe.wait_ge(wo_lo, g + 1)
                        project_out(n - 1)

            steps(pe, group)
            apply_state(KVG * B - 1)
            spread_norm(KVG * B - 1)
            project_out(KVG * B - 1)


def project_context(nc, X, Q, K, V, ctx_cols, pos, w_q, w_k, w_v):
    HALF = XD // 2
    TWO_PI = 2 * np.pi
    PI2_HI = float(np.float32(6.28125))
    PI2_LO = float(np.float32(TWO_PI - 6.28125))
    ROUND = 12582912.0
    PI = float(np.nextafter(np.float32(np.pi), np.float32(0)))
    FREQS = [float(np.float32(10000.0 ** (-f / 4))) for f in range(4)]
    with ExitStack() as ctx:
        def sb(name, shape, dt=F32):
            return ctx.enter_context(nc.sbuf_tensor(name, shape, dt))

        def sem(name):
            return ctx.enter_context(nc.semaphore(name))

        wq = [Q[:, 12:16], sb("wq_h", [P, HK, HID], F32R), sb("wq_l", [P, HK, HID], F32R)]
        wk = [Q[:, 8:10], sb("wk_h", [P, CK, HID], F32R), sb("wk_l", [P, CK, HID], F32R)]
        wv = [Q[:, 10:12], sb("wv_h", [P, CK, HID], F32R), sb("wv_l", [P, CK, HID], F32R)]
        post = sb("positions", [P, NT, 2])
        cosk, sink, cosq, sinq, nsink, nsinq = (sb(n, [P, NT, HALF]) for n in ("cosk", "sink", "cosq", "sinq", "nsink", "nsinq"))
        ident = sb("ident2", [P, P])
        c_raw = [sb(f"c_raw{i}", [P, CK, P]) for i in range(2)]
        c_h = [sb(f"c_h{i}", [P, CK, P], F32R) for i in range(2)]
        c_l = [sb(f"c_l{i}", [P, CK, P], F32R) for i in range(2)]
        xn = [sb(f"xn{i}", [P, HID]) for i in range(2)]
        x_h = [sb(f"xt_h{i}", [P, HK, P], F32R) for i in range(2)]
        x_l = [sb(f"xt_l{i}", [P, HK, P], F32R) for i in range(2)]
        stats, mv, std, rstd = sb("stats", [P, 6]), sb("mv", [P, 2]), sb("std", [P, 1]), sb("rstd", [P, 1])
        straight = [sb(f"straight{i}", [P, HID]) for i in range(2)]
        crossed = [sb(f"crossed{i}", [P, HID]) for i in range(2)]
        ang, turns_, rad, bent = (straight[0][:, j * NT * HALF:(j + 1) * NT * HALF] for j in range(4))
        banks = ctx.enter_context(nc.psum_tensor("banks2", [P, 8, 512], F32))

        w_landed, pos_landed = [sem(f"xw_landed{i}") for i in range(3)], sem("pos_landed")
        c_landed = [sem("c_landed0"), sem("c_landed1")]
        w_hi, w_lo, consts = sem("xw_hi"), sem("xw_lo"), sem("consts2")
        table, sined, tables_ready = sem("table"), sem("sined"), sem("tables_ready")
        c_hi, c_lo = sem("c_hi"), sem("c_lo")
        stat, rooted, rooted_inv, xn_ready, x_kept = sem("stat"), sem("rooted"), sem("rooted_inv"), sem("xn_ready"), sem("x_kept")
        x_turned, x_hi, x_lo = sem("x_turned"), sem("xt_hi"), sem("xt_lo")
        k_done, v_done, q_done = sem("k_done"), sem("v_done"), sem("q_done")
        v_copied, k_mult, q_mult, k_rot, q_rot = sem("v_copied"), sem("k_mult"), sem("q_mult"), sem("k_rot"), sem("q_rot")

        block = ctx.enter_context(nc.Block())

        def tiles(eng, body):
            with eng.Fori(0, NT // 2 - 1) as p:
                for i in range(2):
                    body(2 * p + i, i, False)
            body(NT - 2, 0, False)
            body(NT - 1, 1, True)

        def tile_of(ap, t):
            if isinstance(t, int):
                return ap[:, t]
            return ap[:, bass.ds(t, 1)].squeeze(1)

        @block.sync
        def _(sp):
            sp.dma_start(post[:, :, :], pos).then_inc(pos_landed, 16)
            for w, src, landed in ((wk, w_k, w_landed[0]), (wv, w_v, w_landed[1]), (wq, w_q, w_landed[2])):
                sp.dma_start(w[0], src).then_inc(landed, 16)

            def body(t, i, last):
                if isinstance(t, int):
                    wait(sp, c_hi, t - 1)
                    wait(sp, c_lo, t - 1)
                    sp.dma_start(c_raw[i][:, :, :], ctx_cols[:, :, t * P:(t + 1) * P]).then_inc(c_landed[i], 16)
                else:
                    sp.wait_ge(c_hi, t - 1)
                    sp.wait_ge(c_lo, t - 1)
                    sp.dma_start(c_raw[i][:, :, :], ctx_cols[:, :, bass.ds(t * P, P)]).then_inc(c_landed[i], 16)

            for i in range(2):
                body(i, i, False)
            with sp.Fori(1, NT // 2) as p:
                for i in range(2):
                    body(2 * p + i, i, False)

        @block.gpsimd
        def _(pool):
            pool.memset(V[:, :, :, XD:XD + 1], 1.0).then_inc(consts, 1)
            pool.memset(ident[:, :], 0.0).then_inc(consts, 1)
            pool.wait_ge(consts, 2)
            pool.affine_select(out=ident[:, :], in_=ident[:, :], compare_op=ALU.not_equal, fill=1.0,
                               base=0, pattern=[[-1, P]], channel_multiplier=1).then_inc(consts, 1)
            for j, w in enumerate((wk, wv, wq)):
                pool.wait_ge(w_hi, j + 1)
                pool.tensor_tensor(w[2][:, :, :], w[0], w[1][:, :, :].bitcast(F32), ALU.subtract).then_inc(w_lo, 1)

            def context_lo(t, i):
                pool.wait_ge(c_hi, t + 1)
                pool.tensor_tensor(c_l[i][:, :, :], c_raw[i][:, :, :], c_h[i][:, :, :].bitcast(F32), ALU.subtract).then_inc(c_lo, 1)

            context_lo(0, 0)

            def body(t, i, last):
                if not last:
                    context_lo(t + 1, 1 - i)
                wait_apart(pool, k_mult, t + 1, consts, 3)
                pool.tensor_tensor(tile_of(K, t), straight[0][:, :], crossed[0][:, :], ALU.add).then_inc(k_rot, 1)
                wait_apart(pool, q_mult, t + 1, consts, 3)
                pool.tensor_tensor(tile_of(Q, t), straight[1][:, :], crossed[1][:, :], ALU.add).then_inc(q_rot, 1)

            body(0, 0, False)
            body(1, 1, False)
            with pool.Fori(1, NT // 2 - 1) as p:
                for i in range(2):
                    body(2 * p + i, i, False)
            body(NT - 2, 0, False)
            body(NT - 1, 1, True)

        @block.scalar
        def _(act):
            def context_hi(t, i):
                act.wait_ge(c_landed[i], 16 * (t // 2 + 1) if isinstance(t, int) else 8 * (t - i) + 16)
                wait(act, v_done, t - 1)
                act.copy(c_h[i][:, :, :], c_raw[i][:, :, :]).then_inc(c_hi, 1)

            def root(t):
                act.wait_ge(stat, 3 * t + 3)
                act.sqrt(std[:, :], std[:, :]).then_inc(rooted, 1)

            for j, w in enumerate((wk, wv, wq)):
                act.wait_ge(w_landed[j], 16)
                act.copy(w[1][:, :, :], w[0]).then_inc(w_hi, 1)
            act.wait_ge(table, 9)
            act.activation(sink[:, :, :].rearrange("p t f -> p (t f)"), rad[:, :], ACT.Sin).then_inc(sined, 1)
            act.activation(cosk[:, :, :].rearrange("p t f -> p (t f)"), bent[:, :], ACT.Sin).then_inc(sined, 1)
            root(0)
            context_hi(0, 0)

            def body(t, i, last):
                act.wait_ge(x_turned, t + 1)
                wait(act, q_done, t - 1)
                act.copy(x_h[i][:, :, :], banks[:, i].rearrange("p (k s) -> p k s", k=HK)).then_inc(x_hi, 1)
                if not last:
                    root(t + 1)
                    context_hi(t + 1, 1 - i)
                act.wait_ge(xn_ready, t + 1)
                act.copy(tile_of(X, t), xn[i][:, :]).then_inc(x_kept, 1)
                act.wait_ge(v_done, t + 1)
                act.copy(tile_of(V, t)[:, :, 0:XD], banks[:, 4 + i].rearrange("p (h d) -> p h d", d=XD)).then_inc(v_copied, 1)

            body(0, 0, False)
            body(1, 1, False)
            with act.Fori(1, NT // 2 - 1) as p:
                for i in range(2):
                    body(2 * p + i, i, False)
            body(NT - 2, 0, False)
            body(NT - 1, 1, True)

        @block.vector
        def _(dve):
            dve.wait_ge(pos_landed, 16)
            av = ang[:, :].rearrange("p (t a f) -> p t a f", a=2, f=4)
            for f in range(4):
                a = dve.tensor_scalar(av[:, :, :, f], post[:, :, :], FREQS[f], None, ALU.mult)
            a.then_inc(table, 1)
            steps = [
                lambda: dve.tensor_scalar(turns_[:, :], ang[:, :], 1.0 / TWO_PI, ROUND, ALU.mult, ALU.add),
                lambda: dve.tensor_scalar(turns_[:, :], turns_[:, :], -ROUND, None, ALU.add),
                lambda: dve.scalar_tensor_tensor(out=rad[:, :], in0=turns_[:, :], scalar=-PI2_HI, in1=ang[:, :], op0=ALU.mult, op1=ALU.add),
                lambda: dve.scalar_tensor_tensor(out=rad[:, :], in0=turns_[:, :], scalar=-PI2_LO, in1=rad[:, :], op0=ALU.mult, op1=ALU.add),
                lambda: dve.tensor_scalar(rad[:, :], rad[:, :], PI, -PI, ALU.min, ALU.max),
                lambda: dve.tensor_scalar(bent[:, :], rad[:, :], -1.0, None, ALU.mult),
                lambda: dve.tensor_tensor(bent[:, :], rad[:, :], bent[:, :], ALU.max),
                lambda: dve.tensor_scalar(bent[:, :], bent[:, :], -1.0, PI / 2, ALU.mult, ALU.add),
            ]
            for n, step in enumerate(steps):
                dve.wait_ge(table, n + 1)
                step().then_inc(table, 1)

            def norm_stats(t):
                dve.bn_stats(stats[:, :], tile_of(X, t)).then_inc(stat, 1)
                wait_apart(dve, stat, 3 * t + 1, pos_landed, 16)
                dve.bn_aggr(mv[:, :], stats[:, :]).then_inc(stat, 1)
                dve.wait_ge(stat, 3 * t + 2)
                dve.tensor_scalar(std[:, :], mv[:, 1:2], LN_EPS, None, ALU.add).then_inc(stat, 1)

            def normalise(t, i):
                dve.wait_ge(rooted, t + 1)
                dve.reciprocal(rstd[:, :], std[:, :]).then_inc(rooted_inv, 1)
                dve.wait_ge(rooted_inv, t + 1)
                wait(dve, x_turned, t - 1)
                wait(dve, x_kept, t - 1)
                dve.tensor_scalar(xn[i][:, :], tile_of(X, t), mv[:, 0:1], rstd[:, 0:1], ALU.subtract, ALU.mult).then_inc(xn_ready, 1)

            def rotate(t, which, bank, done, rotated, mult, cos, sin, nsin):
                dve.wait_ge(done, t + 1)
                wait(dve, rotated, t)
                y = banks[:, bank].rearrange("p (h s f) -> p h s f", s=2, f=HALF)
                st = straight[which][:, :].rearrange("p (h s f) -> p h s f", s=2, f=HALF)
                cr = crossed[which][:, :].rearrange("p (h s f) -> p h s f", s=2, f=HALF)
                one = [P, XH, HALF]
                dve.tensor_tensor(st, y, tile_of(cos, t).unsqueeze(1).unsqueeze(1).to_broadcast([P, XH, 2, HALF]), ALU.mult)
                dve.tensor_tensor(cr[:, :, 0], y[:, :, 1], tile_of(nsin, t).unsqueeze(1).to_broadcast(one), ALU.mult)
                dve.tensor_tensor(cr[:, :, 1], y[:, :, 0], tile_of(sin, t).unsqueeze(1).to_broadcast(one), ALU.mult).then_inc(mult, 1)

            norm_stats(0)
            dve.wait_ge(sined, 2)
            for k, (o, a, f) in enumerate(((nsink, sink, -1.0), (cosq, cosk, 0.25), (sinq, sink, 0.25), (nsinq, sink, -0.25))):
                dve.tensor_scalar(o[:, :, :], a[:, :, :], f, None, ALU.mult).then_inc(tables_ready, 1)
            dve.wait_ge(tables_ready, 4)
            normalise(0, 0)

            def body(t, i, last):
                if not last:
                    norm_stats(t + 1)
                dve.wait_ge(x_hi, t + 1)
                wait(dve, q_done, t - 1)
                dve.tensor_tensor(x_l[i][:, :, :], banks[:, i].rearrange("p (k s) -> p k s", k=HK),
                                  x_h[i][:, :, :].bitcast(F32), ALU.subtract).then_inc(x_lo, 1)
                rotate(t, 0, 2 + i, k_done, k_rot, k_mult, cosk, sink, nsink)
                if not last:
                    normalise(t + 1, 1 - i)
                rotate(t, 1, 6 + i, q_done, q_rot, q_mult, cosq, sinq, nsinq)

            body(0, 0, False)
            body(1, 1, False)
            with dve.Fori(1, NT // 2 - 1) as p:
                for i in range(2):
                    body(2 * p + i, i, False)
            body(NT - 2, 0, False)
            body(NT - 1, 1, True)

        @block.tensor
        def _(pe):
            def product(out, pairs):
                terms = [t for lh, ll, rh, rl in pairs for t in ((lh, rl), (ll, rh), (lh, rh))]
                for i, (a, c) in enumerate(terms):
                    mm = pe.matmul(out, a, c, start=(i == 0), stop=(i == len(terms) - 1))
                return mm

            pe.wait_ge(consts, 3)
            pe.wait_ge(w_hi, 3)
            pe.wait_ge(w_lo, 3)

            def body(t, i, last):
                pe.wait_ge(xn_ready, t + 1)
                wait(pe, x_lo, t - 1)
                for k in range(HK):
                    mm = pe.transpose(banks[:, i, k * P:(k + 1) * P], xn[i][:, k * P:(k + 1) * P], ident[:, :])
                mm.then_inc(x_turned, 1)
                pe.wait_ge(c_hi, t + 1)
                pe.wait_ge(c_lo, t + 1)
                wait(pe, k_mult, t - 1)
                product(banks[:, 2 + i], [(c_h[i][:, k], c_l[i][:, k], wk[1][:, k], wk[2][:, k]) for k in range(CK)]).then_inc(k_done, 1)
                wait(pe, v_copied, t - 1)
                product(banks[:, 4 + i], [(c_h[i][:, k], c_l[i][:, k], wv[1][:, k], wv[2][:, k]) for k in range(CK)]).then_inc(v_done, 1)
                pe.wait_ge(x_hi, t + 1)
                pe.wait_ge(x_lo, t + 1)
                wait(pe, q_mult, t - 1)
                product(banks[:, 6 + i], [(x_h[i][:, k], x_l[i][:, k], wq[1][:, k], wq[2][:, k]) for k in range(HK)]).then_inc(q_done, 1)

            body(0, 0, False)
            body(1, 1, False)
            with pe.Fori(1, NT // 2) as p:
                for i in range(2):
                    body(2 * p + i, i, False)


def softmax_attention(nc, X, Q, K, V, b_out):
    G = 8
    NG = XH // G
    R = 64
    M0 = 2 * XD
    D0 = M0 + 2
    QUAD = 4
    VR = P // QUAD
    with ExitStack() as ctx:
        def sb(name, shape, dt=F32):
            return ctx.enter_context(nc.sbuf_tensor(name, shape, dt))

        def sem(name):
            return ctx.enter_context(nc.semaphore(name))

        bout = sb("bout", [P, HID])
        ident = sb("ident3", [P, P])
        place = sb("place", [P, TB, S], F32R)
        qpad = [sb(f"qpad{i}", [P, TB, G, R], F32R) for i in range(2)]
        kpad = [sb(f"kpad{i}", [P, TB, G, R], F32R) for i in range(2)]
        qT = sb("qT", [P, G // 2, S], F32R)
        qmT = [sb(f"qmT{i}", [P, G // 2, S], F32R) for i in range(2)]
        kT = [sb(f"kT{i}", [P, G // 2, 2, S], F32R) for i in range(2)]
        vz = [sb(f"vz{i}", [P, TB, P - VR + G * P]) for i in range(2)]
        probs = [sb(f"probs{i}", [P, TB, S]) for i in range(2)]
        pvs = [sb(f"pvs{i}", [P, S]) for i in range(2)]
        top = [sb(f"top{i}", [P, TB, G]) for i in range(2)]
        rsum = [sb(f"rsum{i}", [P, TB, QUAD]) for i in range(2)]
        one = sb("one", [P, 1])
        banks = ctx.enter_context(nc.psum_tensor("banks3", [P, 8, 512], F32))
        p_turn = banks[:, 0:2].rearrange("p c (j s) -> p (c j) s", s=S)
        p_raw = [banks[:, 2 + i].rearrange("p (t s) -> p t s", t=TB) for i in range(2)]
        p_shift = [banks[:, 4 + i].rearrange("p (t s) -> p t s", t=TB) for i in range(2)]
        p_pv = banks[:, 6, 0:S]
        p_back = banks[:, 7, 0:S].rearrange("p (t h d) -> p t h d", t=TB, h=QUAD)

        bout_landed, consts, cleared, placed = sem("bout_landed"), sem("consts3"), sem("cleared"), sem("placed")
        q_hi, k_hi, padded, k_padded, v_laid = sem("pq_hi"), sem("pk_hi"), sem("padded"), sem("k_padded"), sem("v_laid")
        q_turned, k_turned, m_turned = sem("q_turned"), sem("k_turned"), sem("m_turned")
        qT_ready, kT_ready, qmT_ready = sem("qT_ready"), sem("kT_ready"), sem("qmT_ready")
        scored, maxed, shift_hi, shift_lo = sem("scored"), sem("maxed"), sem("shift_hi"), sem("shift_lo")
        shifted, exped, pv_done, pv_kept = sem("shifted"), sem("exped3"), sem("pv_done"), sem("pv_kept")
        backed, inverted, written = sem("backed"), sem("inverted3"), sem("written")
        biased = sem("biased")

        block = ctx.enter_context(nc.Block())

        def groups(eng, body):
            def batch(b, last):
                for g in range(NG):
                    nxt = (b, g + 1) if g + 1 < NG else (b + 1, 0)
                    body(b, g, b * NG + g, None if last and g == NG - 1 else nxt)
            batch(0, False)
            with eng.Fori(1, B - 1) as b:
                batch(b, False)
            batch(B - 1, True)

        def part(ap, b, g, width, quad=None):
            rows = slice(b * TB, (b + 1) * TB) if isinstance(b, int) else bass.ds(b * TB, TB)
            first, heads = (g * G, G) if quad is None else (g * G + quad * QUAD, QUAD)
            return ap[:, rows, first * width:(first + heads) * width].rearrange("p t (h d) -> p t h d", d=width)

        @block.sync
        def _(sp):
            sp.dma_start(bout[:, :], b_out.partition_broadcast(P)).then_inc(bout_landed, 16)

        @block.gpsimd
        def _(pool):
            def clear(i):
                pool.memset(qpad[i][:, :, :, :].bitcast(F32), 0.0)
                pool.memset(kpad[i][:, :, :, :].bitcast(F32), 0.0).then_inc(cleared, 1)
                pool.wait_ge(cleared, 2 * i + 1)
                pool.memset(kpad[i][:, :, :, M0:D0].bitcast(F32), 1.0).then_inc(cleared, 1)

            pool.memset(ident[:, :], 0.0).then_inc(consts, 1)
            pool.memset(one[:, :], 1.0).then_inc(consts, 1)
            pool.wait_ge(consts, 2)
            pool.affine_select(out=ident[:, :], in_=ident[:, :], compare_op=ALU.not_equal, fill=1.0,
                               base=0, pattern=[[-1, P]], channel_multiplier=1).then_inc(consts, 1)

            def pad(b, g, n):
                i = g % 2
                q, k = part(Q, b, g, XD), part(K, b, g, XD)
                if not isinstance(n, int) or n >= 2:
                    wait_apart(pool, m_turned, n - 1, consts, 3)
                by_one = one[:, :].unsqueeze(2).unsqueeze(3).to_broadcast([P, TB, G, XD])
                pool.tensor_tensor(qpad[i][:, :, :, 0:XD], q, by_one, ALU.mult)
                pool.tensor_copy(qpad[i][:, :, :, D0:D0 + XD], q).then_inc(q_hi, 1)
                pool.tensor_copy(kpad[i][:, :, :, 0:XD], k)
                pool.tensor_copy(kpad[i][:, :, :, XD:M0], k).then_inc(k_hi, 1)
                pool.memset(qpad[i][:, :, :, M0:D0].bitcast(F32), 0.0)
                wait_apart(pool, q_hi, n + 1, consts, 3)
                pool.tensor_tensor(qpad[i][:, :, :, XD:M0], q, qpad[i][:, :, :, 0:XD].bitcast(F32), ALU.subtract).then_inc(padded, 1)
                wait_apart(pool, k_hi, n + 1, consts, 3)
                pool.tensor_tensor(kpad[i][:, :, :, D0:D0 + XD], k, kpad[i][:, :, :, 0:XD].bitcast(F32), ALU.subtract).then_inc(k_padded, 1)

            def lay_v(b, g, n):
                i = g % 2
                rows = slice(b * TB, (b + 1) * TB) if isinstance(b, int) else bass.ds(b * TB, TB)
                if not isinstance(n, int) or n >= 2:
                    wait_apart(pool, pv_done, G * (n - 1), consts, 3)
                pool.tensor_copy(vz[i][:, :, P - VR:].rearrange("p t (h c) -> p t h c", c=P)[:, :, :, 0:XD + 1],
                                 V[:, rows, g * G:(g + 1) * G]).then_inc(v_laid, 1)

            clear(0)
            pool.wait_ge(cleared, 2)
            pad(0, 0, 0)
            clear(1)
            pool.wait_ge(cleared, 4)
            pool.wait_ge(placed, 4)
            lay_v(0, 0, 0)

            def body(b, g, n, nxt):
                if nxt:
                    pad(*nxt, n + 1)
                    lay_v(*nxt, n + 1)

            groups(pool, body)
            pool.wait_ge(bout_landed, 16)
            for t in range(NT):
                pool.tensor_tensor(X[:, t], X[:, t], bout[:, :], ALU.add).then_inc(biased, 1)

        @block.scalar
        def _(act):
            def keep_k(n, i, r):
                act.wait_ge(k_turned, n + 1)
                if not isinstance(n, int) or n >= 2:
                    act.wait_ge(shifted, G * (n - 1))
                rows = slice(r * R, (r + 1) * R)
                act.copy(kT[i][rows, :, r], p_turn[rows]).then_inc(kT_ready, 1)

            def keep_m(n, i):
                act.wait_ge(m_turned, n + 1)
                if not isinstance(n, int) or n >= 2:
                    act.wait_ge(shifted, G * (n - 1))
                act.copy(qmT[i][:, :, :], p_turn).then_inc(qmT_ready, 1)

            def keep_pv(n, quad):
                act.wait_ge(pv_done, G * n + QUAD * (quad + 1))
                if not isinstance(n, int) or n >= 1:
                    act.wait_ge(backed, 2 * n - 1 + quad)
                act.copy(pvs[quad][:, :], p_pv).then_inc(pv_kept, 1)

            act.wait_ge(placed, 3)
            for r in range(2):
                keep_k(0, 0, r)
            keep_m(0, 0)

            def body(b, g, n, nxt):
                for h in range(G):
                    act.wait_ge(shifted, G * n + h + 1)
                    if not isinstance(n, int) or G * n + h >= 2:
                        act.wait_ge(pv_done, G * n + h - 1)
                    act.activation(probs[h % 2][:, :, :], p_shift[h % 2], ACT.Exp).then_inc(exped, 1)
                    if h in (1, 2) and nxt:
                        keep_k(n + 1, (g + 1) % 2, h - 1)
                    if h == QUAD:
                        keep_pv(n, 0)
                if nxt:
                    keep_m(n + 1, (g + 1) % 2)
                keep_pv(n, 1)

            groups(act, body)

        @block.vector
        def _(dve):
            dve.memset(place[:, :, :].bitcast(F32), 0.0).then_inc(placed, 1)
            dve.wait_ge(consts, 3)
            dve.wait_ge(placed, 1)
            for t in range(TB):
                z = dve.tensor_copy(place[:, t, t * P:(t + 1) * P], ident[:, :])
            z.then_inc(placed, 1)
            for i in range(2):
                z = dve.memset(kT[i][:, :, :, :].bitcast(F32), 0.0)
            z.then_inc(placed, 1)
            for i in range(2):
                z = dve.memset(vz[i][:, :, :], 0.0)
            z.then_inc(placed, 1)

            def keep_q(n):
                dve.wait_ge(q_turned, n + 1)
                wait(dve, scored, G * n)
                dve.tensor_copy(qT[:, :, :], p_turn).then_inc(qT_ready, 1)

            def row_max(n, h, i):
                dve.wait_ge(scored, G * n + h + 1)
                dve.tensor_reduce(top[i][:, :, h], p_raw[h % 2], AX.X, ALU.max).then_inc(maxed, 1)

            def shift(n, i):
                dve.wait_ge(maxed, G * n + G)
                dve.tensor_scalar(qpad[i][:, :, :, M0], top[i][:, :, :], -1.0, None, ALU.mult).then_inc(shift_hi, 1)
                dve.wait_ge(shift_hi, n + 1)
                dve.scalar_tensor_tensor(out=qpad[i][:, :, :, M0 + 1], in0=top[i][:, :, :], scalar=-1.0,
                                         in1=qpad[i][:, :, :, M0].bitcast(F32), op0=ALU.mult, op1=ALU.subtract).then_inc(shift_lo, 1)

            def write(b, g, n, quad):
                dve.wait_ge(backed, 2 * n + quad + 1)
                wait(dve, written, 2 * n + quad)
                dve.reciprocal(rsum[quad][:, :, :], p_back[:, :, :, XD]).then_inc(inverted, 1)
                dve.wait_ge(inverted, 2 * n + quad + 1)
                dve.tensor_tensor(part(Q, b, g, XD, quad), p_back[:, :, :, 0:XD],
                                  rsum[quad][:, :, :].unsqueeze(3).to_broadcast([P, TB, QUAD, XD]), ALU.mult).then_inc(written, 1)

            keep_q(0)
            for h in range(G):
                row_max(0, h, 0)
            shift(0, 0)

            def body(b, g, n, nxt):
                if nxt:
                    keep_q(n + 1)
                if not (isinstance(n, int) and n == 0):
                    write(b if g else b - 1, (g - 1) % NG, n - 1, 1)
                if nxt:
                    for h in range(G - 2):
                        row_max(n + 1, h, (g + 1) % 2)
                write(b, g, n, 0)
                if nxt:
                    for h in range(G - 2, G):
                        row_max(n + 1, h, (g + 1) % 2)
                    shift(n + 1, (g + 1) % 2)

            groups(dve, body)
            write(B - 1, NG - 1, B * NG - 1, 1)

        @block.tensor
        def _(pe):
            def turn(pad, i, done):
                for j in range(G // 2):
                    for t in range(TB):
                        mm = pe.matmul(p_turn[:, j], pad[i][:, t, 2 * j:2 * j + 2].rearrange("p h r -> p (h r)"), place[:, t],
                                       start=(t == 0), stop=(t == TB - 1))
                mm.then_inc(done, 1)

            def turn_q(n, i):
                pe.wait_ge(padded, n + 1)
                wait(pe, qmT_ready, n)
                turn(qpad, i, q_turned)

            def turn_k(n, i):
                pe.wait_ge(k_padded, n + 1)
                pe.wait_ge(qT_ready, n + 1)
                turn(kpad, i, k_turned)

            def turn_m(n, i):
                pe.wait_ge(shift_lo, n + 1)
                pe.wait_ge(kT_ready, 2 * n + 2)
                turn(qpad, i, m_turned)

            def raw_scores(n, h, i):
                pe.wait_ge(kT_ready, 2 * n + 2)
                if not isinstance(n, int) or G * n + h >= 2:
                    pe.wait_ge(maxed, G * n + h - 1)
                for t in range(TB):
                    mm = pe.matmul(p_raw[h % 2][:, t], qT[:, h // 2, t * P:(t + 1) * P], kT[i][:, h // 2, h % 2], start=True, stop=True)
                mm.then_inc(scored, 1)

            def shifted_scores(n, h, i):
                pe.wait_ge(qmT_ready, n + 1)
                if not isinstance(n, int) or G * n + h >= 2:
                    pe.wait_ge(exped, G * n + h - 1)
                for t in range(TB):
                    mm = pe.matmul(p_shift[h % 2][:, t], kT[i][:, h // 2, h % 2, t * P:(t + 1) * P], qmT[i][:, h // 2], start=True, stop=True)
                mm.then_inc(shifted, 1)

            def values(n, h, i):
                pe.wait_ge(exped, G * n + h + 1)
                quad, j = h // QUAD, h % QUAD
                if j == 0:
                    pe.wait_ge(v_laid, n + 1)
                    wait(pe, pv_kept, 2 * n + quad)
                window = slice(P - VR + h * P - j * VR, P - VR + (h + 1) * P - j * VR)
                for kt in range(TB):
                    mm = pe.matmul(p_pv, vz[i][:, kt, window], probs[h % 2][:, kt],
                                   start=(j == 0 and kt == 0), stop=(j == QUAD - 1 and kt == TB - 1))
                mm.then_inc(pv_done, 1)

            def turn_back(n, quad):
                pe.wait_ge(pv_kept, 2 * n + quad + 1)
                wait(pe, written, 2 * n + quad)
                for t in range(TB):
                    mm = pe.transpose(p_back[:, t].rearrange("p h d -> p (h d)"), pvs[quad][:, t * P:(t + 1) * P], ident[:, :])
                mm.then_inc(backed, 1)

            pe.wait_ge(consts, 3)
            pe.wait_ge(placed, 2)
            turn_q(0, 0)
            turn_k(0, 0)
            for h in range(G):
                raw_scores(0, h, 0)
            turn_m(0, 0)

            def body(b, g, n, nxt):
                i, ni = g % 2, (g + 1) % 2
                for h in range(G):
                    shifted_scores(n, h, i)
                    if h == 0:
                        if nxt:
                            turn_q(n + 1, ni)
                    elif h == 1:
                        if not (isinstance(n, int) and n == 0):
                            turn_back(n - 1, 1)
                        if nxt:
                            turn_k(n + 1, ni)
                    elif h >= 3 and h < 7 and nxt:
                        raw_scores(n + 1, 2 * h - 6, ni)
                    if h == 5 and not nxt:
                        turn_back(n, 0)
                    if h:
                        values(n, h - 1, i)
                    if h >= 3 and h < 7 and nxt:
                        raw_scores(n + 1, 2 * h - 5, ni)
                        if h == 5:
                            turn_back(n, 0)
                if nxt:
                    turn_m(n + 1, ni)
                values(n, G - 1, i)

            groups(pe, body)
            turn_back(B * NG - 1, 1)




def project_attention(nc, X, A, xh, xl, w_out):
    with ExitStack() as ctx:
        def sb(name, shape, dt=F32):
            return ctx.enter_context(nc.sbuf_tensor(name, shape, dt))

        def sem(name):
            return ctx.enter_context(nc.semaphore(name))

        w_raw, wh, wl = sb("wo4_raw", [P, HK, HID]), sb("wo4_h", [P, HK, HID], F32R), sb("wo4_l", [P, HK, HID], F32R)
        ident = sb("ident4", [P, P])
        a_in = [sb(f"a_in{i}", [P, HID]) for i in range(2)]
        a_h = [sb(f"a4_h{i}", [P, HK, P], F32R) for i in range(2)]
        a_l = [sb(f"a4_l{i}", [P, HK, P], F32R) for i in range(2)]
        total = sb("total", [P, HID])
        xn = [sb(f"xn4_{i}", [P, HID]) for i in range(2)]
        stats, mv, std, rstd = sb("stats4", [P, 6]), sb("mv4", [P, 2]), sb("std4", [P, 1]), sb("rstd4", [P, 1])
        banks = ctx.enter_context(nc.psum_tensor("banks4", [P, 8, 512], F32))

        w_landed, w_hi, w_lo, consts = sem("wo4_landed"), sem("wo4_hi"), sem("wo4_lo"), sem("consts4")
        a_copied, a_turned, a_hi, a_lo = sem("a_copied"), sem("a_turned"), sem("a4_hi"), sem("a4_lo")
        out_done, stat, rooted, inverted, xn_ready, x_kept = (sem(n) for n in ("out4", "stat4", "rooted4", "inverted4", "xn4_ready", "x4_kept"))
        summed, x_turned, x_hi, x_lo = sem("summed4"), sem("x4_turned"), sem("x4_hi"), sem("x4_lo")

        block = ctx.enter_context(nc.Block())

        def tiles(eng, body):
            body(0, 0, False)
            body(1, 1, False)
            with eng.Fori(1, NT // 2 - 1) as p:
                for i in range(2):
                    body(2 * p + i, i, False)
            body(NT - 2, 0, False)
            body(NT - 1, 1, True)

        def tile_of(ap, t):
            if isinstance(t, int):
                return ap[:, t]
            return ap[:, bass.ds(t, 1)].squeeze(1)

        def columns_of(ap, t):
            return ap[:, :, t * P:(t + 1) * P] if isinstance(t, int) else ap[:, :, bass.ds(t * P, P)]

        @block.sync
        def _(sp):
            sp.dma_start(w_raw[:, :, :], w_out).then_inc(w_landed, 16)

        @block.gpsimd
        def _(pool):
            pool.memset(ident[:, :], 0.0).then_inc(consts, 1)
            pool.wait_ge(consts, 1)
            pool.affine_select(out=ident[:, :], in_=ident[:, :], compare_op=ALU.not_equal, fill=1.0,
                               base=0, pattern=[[-1, P]], channel_multiplier=1).then_inc(consts, 1)

            def body(t, i, last):
                wait_apart(pool, a_turned, t - 1, consts, 2) if not isinstance(t, int) else wait(pool, a_turned, t - 1)
                pool.tensor_copy(a_in[i][:, :], tile_of(A, t)).then_inc(a_copied, 1)

            tiles(pool, body)

        @block.scalar
        def _(act):
            def x_split(t, i):
                act.wait_ge(x_turned, t + 1)
                act.copy(columns_of(xh, t), banks[:, 4 + i].rearrange("p (k s) -> p k s", k=HK)).then_inc(x_hi, 1)

            def a_split(t, i):
                act.wait_ge(a_turned, t + 1)
                wait(act, out_done, t - 1)
                act.copy(a_h[i][:, :, :], banks[:, i].rearrange("p (k s) -> p k s", k=HK)).then_inc(a_hi, 1)

            a_split(0, 0)
            act.wait_ge(w_landed, 16)
            act.copy(wh[:, :, :], w_raw[:, :, :]).then_inc(w_hi, 1)

            def body(t, i, last):
                if not last:
                    a_split(t + 1, 1 - i)
                act.wait_ge(stat, 3 * t + 3)
                act.sqrt(std[:, :], std[:, :]).then_inc(rooted, 1)
                if not isinstance(t, int) or t:
                    x_split(t - 1, 1 - i)
                act.wait_ge(xn_ready, t + 1)
                act.copy(tile_of(X, t), xn[i][:, :]).then_inc(x_kept, 1)

            tiles(act, body)
            x_split(NT - 1, (NT - 1) % 2)

        @block.vector
        def _(dve):
            def x_split(t, i):
                dve.wait_ge(x_hi, t + 1)
                dve.tensor_tensor(columns_of(xl, t), banks[:, 4 + i].rearrange("p (k s) -> p k s", k=HK),
                                  columns_of(xh, t).bitcast(F32), ALU.subtract).then_inc(x_lo, 1)

            def a_split(t, i):
                dve.wait_ge(a_hi, t + 1)
                dve.tensor_tensor(a_l[i][:, :, :], banks[:, i].rearrange("p (k s) -> p k s", k=HK),
                                  a_h[i][:, :, :].bitcast(F32), ALU.subtract).then_inc(a_lo, 1)

            a_split(0, 0)
            dve.wait_ge(w_hi, 1)
            dve.tensor_tensor(wl[:, :, :], w_raw[:, :, :], wh[:, :, :].bitcast(F32), ALU.subtract).then_inc(w_lo, 1)

            def body(t, i, last):
                dve.wait_ge(out_done, t + 1)
                wait(dve, xn_ready, t)
                dve.tensor_tensor(total[:, :], banks[:, 2 + i], tile_of(X, t), ALU.add).then_inc(summed, 1)
                dve.wait_ge(summed, t + 1)
                dve.bn_stats(stats[:, :], total[:, :]).then_inc(stat, 1)
                wait_apart(dve, stat, 3 * t + 1, consts, 2)
                dve.bn_aggr(mv[:, :], stats[:, :]).then_inc(stat, 1)
                dve.wait_ge(stat, 3 * t + 2)
                dve.tensor_scalar(std[:, :], mv[:, 1:2], LN_EPS, None, ALU.add).then_inc(stat, 1)
                if not last:
                    a_split(t + 1, 1 - i)
                dve.wait_ge(rooted, t + 1)
                dve.reciprocal(rstd[:, :], std[:, :]).then_inc(inverted, 1)
                dve.wait_ge(inverted, t + 1)
                wait(dve, x_turned, t - 1)
                wait(dve, x_kept, t - 1)
                dve.tensor_scalar(xn[i][:, :], total[:, :], mv[:, 0:1], rstd[:, 0:1], ALU.subtract, ALU.mult).then_inc(xn_ready, 1)
                if not isinstance(t, int) or t:
                    x_split(t - 1, 1 - i)

            tiles(dve, body)
            x_split(NT - 1, (NT - 1) % 2)

        @block.tensor
        def _(pe):
            def product(out, pairs):
                terms = [t for lh, ll, rh, rl in pairs for t in ((lh, rl), (ll, rh), (lh, rh))]
                for i, (a, c) in enumerate(terms):
                    mm = pe.matmul(out, a, c, start=(i == 0), stop=(i == len(terms) - 1))
                return mm

            def turn_x(t, i):
                pe.wait_ge(xn_ready, t + 1)
                wait(pe, x_lo, t - 1)
                for k in range(HK):
                    mm = pe.transpose(banks[:, 4 + i, k * P:(k + 1) * P], xn[i][:, k * P:(k + 1) * P], ident[:, :])
                mm.then_inc(x_turned, 1)

            def turn_a(t, i):
                pe.wait_ge(a_copied, t + 1)
                wait(pe, a_lo, t - 1)
                for k in range(HK):
                    mm = pe.transpose(banks[:, i, k * P:(k + 1) * P], a_in[i][:, k * P:(k + 1) * P], ident[:, :])
                mm.then_inc(a_turned, 1)

            pe.wait_ge(consts, 2)
            turn_a(0, 0)

            def body(t, i, last):
                if not last:
                    turn_a(t + 1, 1 - i)
                if isinstance(t, int) and t == 0:
                    pe.wait_ge(w_hi, 1)
                    pe.wait_ge(w_lo, 1)
                pe.wait_ge(a_hi, t + 1)
                pe.wait_ge(a_lo, t + 1)
                wait(pe, summed, t - 1)
                product(banks[:, 2 + i], [(a_h[i][:, k], a_l[i][:, k], wh[:, k], wl[:, k]) for k in range(HK)]).then_inc(out_done, 1)
                if not isinstance(t, int) or t:
                    turn_x(t - 1, 1 - i)

            tiles(pe, body)
            turn_x(NT - 1, (NT - 1) % 2)


def mixture(nc, X, scratch, xh, xl, gate_cols, expert_bias, w_gu, w_down, out):
    NE = E + 1
    NBLK = 4
    W = T // NBLK
    TPB = W // P
    MK = FF // P
    NONE = 3e38
    with ExitStack() as ctx:
        def sb(name, shape, dt=F32):
            return ctx.enter_context(nc.sbuf_tensor(name, shape, dt))

        def sem(name):
            return ctx.enter_context(nc.semaphore(name))

        flat = scratch[:, :, :].rearrange("p t h -> p (t h)")
        GU = HK * 2 * FF
        gu_raw = flat[:, 0:GU].rearrange("p (k f) -> p k f", k=HK)
        dn_raw = flat[:, GU:GU + MK * HID].rearrange("p (k h) -> p k h", k=MK)
        silu = flat[:, 3072:3072 + 2 * W].rearrange("p (m s) -> p m s", m=MK)
        hid = flat[:, 4096:4096 + 2 * W].rearrange("p (m s) -> p m s", m=MK)
        gu_h = [sb(f"gu_h{i}", [P, HK, 2 * FF], F32R) for i in range(2)]
        gu_l = [sb(f"gu_l{i}", [P, HK, 2 * FF], F32R) for i in range(2)]
        dn_h = [sb(f"dn_h{i}", [P, MK, HID], F32R) for i in range(2)]
        dn_l = [sb(f"dn_l{i}", [P, MK, HID], F32R) for i in range(2)]
        hid_h = [sb(f"hid_h{i}", [P, MK, W], F32R) for i in range(2)]
        hid_l = [sb(f"hid_l{i}", [P, MK, W], F32R) for i in range(2)]
        gw_raw = sb("gw_raw", [P, HK, E])
        gw_h, gw_l = sb("gw_h", [P, HK, E], F32R), sb("gw_l", [P, HK, E], F32R)
        ebias = sb("ebias", [P, E])
        ident = sb("ident5", [P, P])
        lcols = flat[0:E, 5120:5120 + T]
        score = sb("score", [P, NT, E])
        biased = sb("biased", [P, NT, E])
        best = sb("best", [P, NT, 8])
        left = sb("left", [P, NT, E])
        wsum = sb("wsum", [P, NT])
        weight = sb("weight", [P, NE, NT])
        stats, mv, std = sb("stats5", [P, NT, 6]), sb("mv5", [P, NT, 2]), sb("std5", [P, NT])
        banks = ctx.enter_context(nc.psum_tensor("banks5", [P, 8, 512], F32))

        gw_landed, eb_landed = sem("gw_landed"), sem("eb_landed")
        gu_landed, dn_landed = sem("gu_landed"), sem("dn_landed")
        consts, gw_hi, gw_lo = sem("consts5"), sem("gw_hi"), sem("gw_lo")
        gu_hi, gu_lo, dn_hi, dn_lo = sem("gu_hi"), sem("gu_lo"), sem("dn_hi"), sem("dn_lo")
        routed, lcopied, lturned, sigmoided, steps = (sem(n) for n in ("routed", "lcopied", "lturned", "sigmoided", "steps"))
        hidden, silued, gated, h_hi, h_lo = (sem(n) for n in ("hidden", "silued", "gated", "h_hi", "h_lo"))
        down, summed = sem("down"), sem("summed5")
        stat, shifted, rooted, inverted, normal, stored = (sem(n) for n in ("stat5", "shifted5", "rooted5", "inverted5", "normal5", "stored"))

        block = ctx.enter_context(nc.Block())

        def experts(eng, body):
            body(0, 0)
            body(1, 1)
            with eng.Fori(1, NE // 2) as p:
                for i in range(2):
                    body(2 * p + i, i)
            body(NE - 1, 0)

        def of_expert(ap, e):
            return ap[e] if isinstance(e, int) else ap[bass.ds(e, 1)].squeeze(0)

        @block.sync
        def _(sp):
            sp.dma_start(gw_raw[:, :, :], gate_cols).then_inc(gw_landed, 16)
            sp.dma_start(ebias[:, :], expert_bias.partition_broadcast(P)).then_inc(eb_landed, 16)

            def body(e, i):
                wait(sp, gu_hi, e)
                wait(sp, gu_lo, e)
                sp.dma_start(gu_raw, of_expert(w_gu, e)).then_inc(gu_landed, 16)
                wait(sp, dn_hi, e)
                wait(sp, dn_lo, e)
                sp.dma_start(dn_raw, of_expert(w_down, e)).then_inc(dn_landed, 16)

            experts(sp, body)
            for c in range(NBLK):
                sp.wait_ge(normal, TPB * (c + 1))
                sp.dma_start(out[:, c * TPB:(c + 1) * TPB], X[:, c * TPB:(c + 1) * TPB]).then_inc(stored, 16)
            sp.wait_ge(stored, 16 * NBLK)

        @block.gpsimd
        def _(pool):
            pool.memset(ident[:, :], 0.0).then_inc(consts, 1)
            pool.memset(weight[:, E], 1.0).then_inc(consts, 1)
            pool.wait_ge(consts, 2)
            pool.affine_select(out=ident[:, :], in_=ident[:, :], compare_op=ALU.not_equal, fill=1.0,
                               base=0, pattern=[[-1, P]], channel_multiplier=1).then_inc(consts, 1)
            pool.wait_ge(gw_hi, 1)
            pool.tensor_tensor(gw_l[:, :, :], gw_raw[:, :, :], gw_h[:, :, :].bitcast(F32), ALU.subtract).then_inc(gw_lo, 1)

            def body(e, i):
                pool.wait_ge(gu_hi, e + 1)
                pool.tensor_tensor(gu_l[i][:, :, :], gu_raw, gu_h[i][:, :, :].bitcast(F32), ALU.subtract).then_inc(gu_lo, 1)
                pool.wait_ge(dn_hi, e + 1)
                pool.tensor_tensor(dn_l[i][:, :, :], dn_raw, dn_h[i][:, :, :].bitcast(F32), ALU.subtract).then_inc(dn_lo, 1)

            experts(pool, body)

        @block.scalar
        def _(act):
            act.wait_ge(gw_landed, 16)
            act.copy(gw_h[:, :, :], gw_raw[:, :, :]).then_inc(gw_hi, 1)

            def root(c):
                act.wait_ge(shifted, c + 1)
                cols = slice(c * TPB, (c + 1) * TPB)
                act.sqrt(std[:, cols], std[:, cols]).then_inc(rooted, 1)

            def split(e, i):
                act.wait_ge(gu_landed, 16 * e + 16)
                if not isinstance(e, int) or e >= 2:
                    act.wait_ge(down, TPB * NBLK * (e - 1))
                act.copy(gu_h[i][:, :, :], gu_raw).then_inc(gu_hi, 1)
                act.wait_ge(dn_landed, 16 * e + 16)
                act.copy(dn_h[i][:, :, :], dn_raw).then_inc(dn_hi, 1)

            split(0, 0)
            for c in range(NBLK):
                act.wait_ge(routed, c + 1)
                act.copy(lcols[:, c * W:(c + 1) * W], banks[0:E, c]).then_inc(lcopied, 1)
            act.wait_ge(lturned, 1)
            act.activation(score[:, :, :].rearrange("p t e -> p (t e)"), banks[:, 4, 0:NT * E], ACT.Sigmoid).then_inc(sigmoided, 1)

            def body(e, i):
                for c in range(NBLK):
                    n = NBLK * e + c
                    for m in range(MK):
                        act.wait_ge(hidden, 2 * MK * n + 2 * m + 1)
                        wait(act, gated, MK * n - MK + m + 1 if isinstance(n, int) else MK * n)
                        act.activation(silu[:, m], banks[:, 2 * m], ACT.Silu).then_inc(silued, 1)
                    for m in range(MK):
                        act.wait_ge(gated, MK * n + m + 1)
                        if not isinstance(n, int) or n >= 2:
                            act.wait_ge(down, TPB * (n - 1))
                        act.copy(hid_h[c % 2][:, m], hid[:, m]).then_inc(h_hi, 1)
                    if isinstance(e, int) and e == NE - 1:
                        if c:
                            root(c - 1)
                    elif c == 0:
                        split(e + 1, 1 - i)

            experts(act, body)
            root(NBLK - 1)

        @block.vector
        def _(dve):
            dve.wait_ge(eb_landed, 16)
            dve.wait_ge(sigmoided, 1)
            n_steps = [0]

            def step(ins):
                n_steps[0] += 1
                ins.then_inc(steps, 1)
                dve.wait_ge(steps, n_steps[0])

            step(dve.tensor_tensor(biased[:, :, :], score[:, :, :], ebias[:, :].unsqueeze(1).to_broadcast([P, NT, E]), ALU.add))
            for t in range(NT):
                ins = dve.max(best[:, t], biased[:, t])
            step(ins)
            step(dve.memset(best[:, :, TOPK:], NONE))
            for t in range(NT):
                ins = dve.match_replace(left[:, t], best[:, t], biased[:, t], -NONE)
            step(ins)
            step(dve.tensor_tensor(left[:, :, :], left[:, :, :], biased[:, :, :], ALU.not_equal))
            step(dve.tensor_tensor(left[:, :, :], left[:, :, :], score[:, :, :], ALU.mult))
            step(dve.tensor_reduce(wsum[:, :], left[:, :, :], AX.X, ALU.add))
            step(dve.reciprocal(wsum[:, :], wsum[:, :]))
            dve.wait_ge(consts, 3)
            step(dve.tensor_tensor(weight[:, 0:E].rearrange("p e t -> p t e"), left[:, :, :],
                                   wsum[:, :].unsqueeze(2).to_broadcast([P, NT, E]), ALU.mult))

            def add_down(e, c):
                n = NBLK * e + c
                for t in range(TPB):
                    tile = c * TPB + t
                    dve.wait_ge(down, TPB * n + t + 1)
                    w = weight[:, e, tile:tile + 1] if isinstance(e, int) else weight[:, bass.ds(e, 1), tile]
                    dve.scalar_tensor_tensor(out=X[:, tile], in0=banks[:, 4 + t], scalar=w, in1=X[:, tile],
                                             op0=ALU.mult, op1=ALU.add).then_inc(summed, 1)

            def normalise(c):
                tiles, cols = range(c * TPB, (c + 1) * TPB), slice(c * TPB, (c + 1) * TPB)
                for t in tiles:
                    dve.wait_ge(summed, TPB * NBLK * (NE - 1) + t + 1)
                    dve.bn_stats(stats[:, t], X[:, t]).then_inc(stat, 1)
                dve.wait_ge(stat, TPB * (2 * c + 1))
                for t in tiles:
                    dve.bn_aggr(mv[:, t], stats[:, t]).then_inc(stat, 1)
                dve.wait_ge(stat, TPB * (2 * c + 2))
                dve.tensor_scalar(std[:, cols], mv[:, cols, 1], LN_EPS, None, ALU.add).then_inc(shifted, 1)
                dve.wait_ge(rooted, c + 1)
                dve.reciprocal(std[:, cols], std[:, cols]).then_inc(inverted, 1)
                dve.wait_ge(inverted, c + 1)
                for t in tiles:
                    dve.tensor_scalar(X[:, t], X[:, t], mv[:, t, 0:1], std[:, t:t + 1], ALU.subtract, ALU.mult).then_inc(normal, 1)

            def body(e, i):
                first = isinstance(e, int) and e == 0
                last = isinstance(e, int) and e == NE - 1
                for c in range(NBLK):
                    n = NBLK * e + c
                    for m in range(MK):
                        dve.wait_ge(hidden, 2 * MK * n + 2 * m + 2)
                        dve.wait_ge(silued, MK * n + m + 1)
                        if not isinstance(n, int) or n >= 1:
                            dve.wait_ge(h_hi, MK * n)
                            dve.wait_ge(h_lo, MK * n)
                        dve.tensor_tensor(hid[:, m], silu[:, m], banks[:, 2 * m + 1], ALU.mult).then_inc(gated, 1)
                    for m in range(MK):
                        dve.wait_ge(h_hi, MK * n + m + 1)
                        dve.tensor_tensor(hid_l[c % 2][:, m], hid[:, m], hid_h[c % 2][:, m].bitcast(F32), ALU.subtract).then_inc(h_lo, 1)
                    if not (first and c == 0):
                        add_down(e if c else e - 1, c - 1 if c else NBLK - 1)
                    if last and c:
                        normalise(c - 1)

            experts(dve, body)
            add_down(NE - 1, NBLK - 1)
            normalise(NBLK - 1)

        @block.tensor
        def _(pe):
            def product(out, pairs):
                terms = [t for lh, ll, rh, rl in pairs for t in ((lh, rl), (ll, rh), (lh, rh))]
                for i, (a, c) in enumerate(terms):
                    mm = pe.matmul(out, a, c, start=(i == 0), stop=(i == len(terms) - 1))
                return mm

            pe.wait_ge(consts, 3)
            pe.wait_ge(gw_hi, 1)
            pe.wait_ge(gw_lo, 1)
            for c in range(NBLK):
                s = slice(c * W, (c + 1) * W)
                product(banks[0:E, c], [(gw_h[:, k], gw_l[:, k], xh[:, k, s], xl[:, k, s]) for k in range(HK)]).then_inc(routed, 1)
            for t in range(NT):
                pe.wait_ge(lcopied, t * P // W + 1)
                mm = pe.transpose(banks[:, 4, t * E:(t + 1) * E], lcols[:, t * P:(t + 1) * P], ident[0:E, 0:E])
            mm.then_inc(lturned, 1)

            def hidden_block(e, i, c):
                n = NBLK * e + c
                s = slice(c * W, (c + 1) * W)
                for m in range(MK):
                    for j in range(2):
                        if not isinstance(n, int) or n >= 1:
                            pe.wait_ge(gated, MK * n - MK + m + 1 if isinstance(n, int) else MK * (n - 1) + m + 1)
                        f = slice(j * FF + m * P, j * FF + (m + 1) * P)
                        product(banks[:, 2 * m + j], [(gu_h[i][:, k, f], gu_l[i][:, k, f], xh[:, k, s], xl[:, k, s]) for k in range(HK)]).then_inc(hidden, 1)

            def down_block(e, i, c):
                n = NBLK * e + c
                pe.wait_ge(h_hi, MK * n + MK)
                pe.wait_ge(h_lo, MK * n + MK)
                for t in range(TPB):
                    if not isinstance(n, int) or n >= 1:
                        pe.wait_ge(summed, TPB * (n - 1) + t + 1)
                    else:
                        pe.wait_ge(sigmoided, 1)
                    s = slice(t * P, (t + 1) * P)
                    product(banks[:, 4 + t], [(hid_h[c % 2][:, m, s], hid_l[c % 2][:, m, s], dn_h[i][:, m], dn_l[i][:, m]) for m in range(MK)]).then_inc(down, 1)

            def body(e, i):
                pe.wait_ge(gu_hi, e + 1)
                pe.wait_ge(gu_lo, e + 1)
                for c in range(NBLK):
                    hidden_block(e, i, c)
                    if c == 0:
                        if not (isinstance(e, int) and e == 0):
                            down_block(e - 1, 1 - i, NBLK - 1)
                        pe.wait_ge(dn_hi, e + 1)
                        pe.wait_ge(dn_lo, e + 1)
                    else:
                        down_block(e, i, c - 1)

            pe.wait_ge(lcopied, NBLK)
            experts(pe, body)
            down_block(NE - 1, 0, NBLK - 1)


def decoder_layer(nc, x_cols, x_tok, w_qkv, b_q, b_kv, w_attn_out, ctx_cols, pos, w_q, w_k, w_v, w_out, b_out,
                  gate_cols, expert_bias, w_gu, w_down, out):
    with ExitStack() as ctx:
        def sb(name, shape, dt=F32):
            return ctx.enter_context(nc.sbuf_tensor(name, shape, dt))

        X = sb("X", [P, NT, HID])
        linear_attention(nc, X, x_cols, x_tok, w_qkv, b_q, b_kv, w_attn_out)
        Q = sb("Q", [P, NT, HID])
        with ExitStack() as inner:
            K = inner.enter_context(nc.sbuf_tensor("K", [P, NT, HID], F32))
            V = inner.enter_context(nc.sbuf_tensor("V", [P, NT, XH, XD + 1], F32))
            project_context(nc, X, Q, K, V, ctx_cols, pos, w_q, w_k, w_v)
            softmax_attention(nc, X, Q, K, V, b_out)
        xh = sb("x2h", [P, HK, T], F32R)
        xl = sb("x2l", [P, HK, T], F32R)
        project_attention(nc, X, Q, xh, xl, w_out)
        mixture(nc, X, Q, xh, xl, gate_cols, expert_bias, w_gu, w_down, out)


def kernel(**inputs):
    import concourse.bacc as _bacc
    from concourse.bass_utils import run_bass_kernel_spmd as _run

    a = {name: np.asarray(value) for name, value in inputs.items()}

    def rows(w):
        return w.reshape(-1, P, w.shape[-1]).transpose(1, 0, 2)

    def rotary(w):
        return w.reshape(w.shape[0], XH, 2, XD // 4, 2).transpose(0, 1, 4, 2, 3).reshape(w.shape)

    x = a["x"].reshape(T, HID)
    grouped = [a["L0_attn_Wq"].reshape(KVG, GROUP * DH, HID), a["L0_attn_Wk"].reshape(KVG, DH, HID),
               a["L0_attn_Wv"].reshape(KVG, DH, HID)]
    b_kv = np.concatenate([a["L0_attn_bk"].reshape(KVG, DH), a["L0_attn_bv"].reshape(KVG, DH)], 1)
    w_kv = a["L0_xattn_Wkv"]
    gate = np.concatenate([a["L0_ffn_w_gate"], a["L0_ffn_sw_gate"][None]])
    up = np.concatenate([a["L0_ffn_w_up"], a["L0_ffn_sw_up"][None]])
    down = np.concatenate([a["L0_ffn_w_down"], a["L0_ffn_sw_down"][None]])
    laid = {
        "x_cols": rows(x.T),
        "x_tok": rows(x),
        "w_qkv": np.concatenate(grouped, 1).transpose(0, 2, 1).reshape(KVG, HK, P, -1).transpose(0, 2, 1, 3),
        "b_q": a["L0_attn_bq"].reshape(KVG, GROUP, DH).transpose(2, 0, 1),
        "b_kv": b_kv.reshape(-1),
        "w_attn_out": a["L0_attn_Wo"].T.reshape(KVG, GROUP, P, HID).transpose(0, 2, 1, 3),
        "ctx_cols": rows(a["ctx_1024"].reshape(T, CTX).T),
        "pos": rows(a["fside_BxSx2_0"].reshape(T, 2)),
        "w_q": rows(rotary(a["L0_xattn_Wq"])),
        "w_k": rows(rotary(w_kv[:, :HID])),
        "w_v": rows(w_kv[:, HID:]),
        "w_out": rows(a["L0_xattn_Wout"]),
        "b_out": a["L0_xattn_bout"],
        "gate_cols": rows(a["L0_ffn_gate_w"].T),
        "expert_bias": a["L0_ffn_expert_bias"],
        "w_gu": np.concatenate([gate, up], 1).transpose(0, 2, 1).reshape(E + 1, HK, P, 2 * FF).transpose(0, 2, 1, 3),
        "w_down": down.transpose(0, 2, 1).reshape(E + 1, FF // P, P, HID).transpose(0, 2, 1, 3),
    }
    nc = _bacc.Bacc("TRN2", target_bir_lowering=False, num_devices=1)
    arrays, args = {}, []
    for name, value in laid.items():
        arrays[f"in_{name}"] = np.ascontiguousarray(value)
        args.append(nc.dram_tensor(f"in_{name}", value.shape, mybir.dt.from_np(value.dtype), kind="ExternalInput").ap())
    args.append(nc.dram_tensor("out_x", (P, NT, HID), F32, kind="ExternalOutput").ap())
    decoder_layer(nc, *args)
    got = _run(nc, [arrays], core_ids=[0]).results[0]["out_x"]
    return got.transpose(1, 0, 2).reshape(B, S, HID)
```

```python
from contextlib import ExitStack

import numpy as np
import concourse.bass as bass
from concourse import mybir

ALU = mybir.AluOpType
ACT = mybir.ActivationFunctionType
AX = mybir.AxisListType
F32 = mybir.dt.float32
F32R = mybir.dt.float32r
U32, I32 = mybir.dt.uint32, mybir.dt.int32

P = 128
B, S, HID = 8, 256, 512
T = B * S
NT = T // P
HK = HID // P
KVG, GROUP, DH = 4, 4, 128
NORM_EPS = 1e-6
LN_EPS = 1e-5
XH, XD = 32, 16
CTX = 256
CK = CTX // P
E, TOPK, FF = 16, 4, 256
TB = S // P
SLOTS = 256
TILES = (T * TOPK + E * (SLOTS - 1)) // SLOTS


def wait(eng, sem, value):
    if not isinstance(value, int) or value > 0:
        eng.wait_ge(sem, value)


def wait_apart(eng, sem, value, met, count):
    if not isinstance(value, int):
        value = eng.to_reg(value)
    eng.wait_ge(met, count)
    eng.wait_ge(sem, value)


def linear_attention(nc, X, x_cols, x_tok, w_qkv, b_q, b_kv, w_out):
    KV = 2 * DH
    QW = GROUP * DH
    KH, KL, VH, ONE, KVW = 0, DH, 2 * DH, 4 * DH, 4 * DH + 2
    SW = KVW - VH
    with ExitStack() as ctx:
        def sb(name, shape, dt=F32):
            return ctx.enter_context(nc.sbuf_tensor(name, shape, dt))

        signals = []

        def sem(name):
            signals.append(ctx.enter_context(nc.semaphore(name)))
            return signals[-1]

        xh = sb("xh", [P, HK, T], F32R)
        xl = sb("xl", [P, HK, T], F32R)
        x_raw = sb("x_raw", [P, 2, HK, S])
        w_raw = sb("w_raw", [P, HK, QW + KV])
        wo_raw = sb("wo_raw", [P, GROUP, HID])
        wh = sb("wh", [P, HK, QW + KV], F32R)
        wl = sb("wl", [P, HK, QW + KV], F32R)
        woh = sb("woh", [P, GROUP, HID], F32R)
        wol = sb("wol", [P, GROUP, HID], F32R)
        bias = sb("bias", [P, KVG, GROUP])
        bias1 = sb("bias1", [P, KVG, GROUP])
        bias_kv = sb("bias_kv", [P, KVG * KV])
        ones = sb("ones", [P, GROUP])
        pick_r = sb("pick_r", [GROUP, GROUP, P], F32R)
        ykv = sb("ykv", [P, TB, KV])
        ek = sb("ek", [P, TB, DH])
        kvs = sb("kvs", [P, TB, KVW], F32R)
        feat = sb("feat", [P, GROUP, S])
        qh = sb("qh", [P, GROUP, S], F32R)
        ql = sb("ql", [P, GROUP, S], F32R)
        ssum = sb("ssum", [P, DH])
        ksum = sb("ksum", [P, 1])
        kvh = sb("kvh", [P, DH], F32R)
        kvl = sb("kvl", [P, DH], F32R)
        kselh = sb("kselh", [P, GROUP, GROUP + 1], F32R)
        ksell = sb("ksell", [P, GROUP, GROUP + 1], F32R)
        rec = sb("rec", [GROUP, S])
        rech = sb("rech", [GROUP, S], F32R)
        recl = sb("recl", [GROUP, S], F32R)
        at = sb("at", [P, GROUP, S])
        ah = sb("ah", [P, GROUP, S], F32R)
        al = sb("al", [P, GROUP, S], F32R)

        pick = at[0:GROUP, 0:2].rearrange("p i (j s) -> p (i j) s", j=2)

        banks = ctx.enter_context(nc.psum_tensor("banks", [P, 8, 512], F32))
        p_kv = banks[:, 0].rearrange("p (t c) -> p t c", t=TB)
        p_q = [banks[:, 1 + i].rearrange("p (i s) -> p i s", i=2) for i in range(2)]
        p_num = [banks[:, 3 + i] for i in range(2)]
        p_rec = [banks[:, 5 + i] for i in range(2)]
        p_out = [banks[:, 5], banks[:, 6]]
        p_state = banks[:, 7, 0:SW]
        p_norm = banks[0:GROUP, 7, 0:S]

        x_landed = [sem("x_landed0"), sem("x_landed1")]
        xtok_landed, bias_landed, bkv_landed = sem("xtok_landed"), sem("bias_landed"), sem("bkv_landed")
        w_landed, wo_landed = [sem("wkv_landed"), sem("wq_landed")], sem("wo_landed")
        x_hi, x_lo = sem("x_hi"), sem("x_lo")
        w_hi, w_lo = [sem("wkv_hi"), sem("wq_hi")], [sem("wkv_lo"), sem("wq_lo")]
        wo_hi, wo_lo = sem("wo_hi"), sem("wo_lo")
        consts, bias1_ready, zeroed = sem("consts"), sem("bias1_ready"), sem("zeroed")
        projected, kv_biased = sem("projected"), sem("kv_biased")
        clipped, exped, feat_k, feat_q = sem("clipped"), sem("exped"), sem("feat_k"), sem("feat_q")
        kv_hi, kv_lo, q_hi, q_lo = sem("kv_hi"), sem("kv_lo"), sem("q_hi"), sem("q_lo")
        state, state_sum, state_hi, state_lo = sem("state"), sem("state_sum"), sem("state_hi"), sem("state_lo")
        normed, norm_read, inverted, rec_hi, rec_lo = sem("normed"), sem("norm_read"), sem("inverted"), sem("rec_hi"), sem("rec_lo")
        applied, num_kept, spread, attended, a_hi, a_lo = (sem("applied"), sem("num_kept"), sem("spread"), sem("attended"),
                                                           sem("a_hi"), sem("a_lo"))
        out_done, added = sem("out_done"), sem("added")

        block = ctx.enter_context(nc.Block())

        def steps(eng, group):
            group(0)
            with eng.Fori(1, KVG) as g:
                group(g)

        def halves(lo):
            return kvs[:, :, 0:ONE].rearrange("p t (c l d) -> p t c l d", c=2, l=2)[:, :, :, lo]

        def by_kind(ap):
            return ap[:, :, :].rearrange("p t (c d) -> p t c d", c=2)

        W_COLS = [slice(QW, QW + KV), slice(0, QW)]

        @block.sync
        def _(sp):
            def load_w(g, part):
                sp.dma_start(w_raw[:, :, W_COLS[part]], w_qkv[g][:, :, W_COLS[part]]).then_inc(w_landed[part], 16)

            load_w(0, 0)
            sp.dma_start(x_raw[:, 0], x_cols[:, :, 0:S]).then_inc(x_landed[0], 16)
            sp.dma_start(bias_kv[:, :], b_kv.partition_broadcast(P)).then_inc(bkv_landed, 16)
            load_w(0, 1)
            sp.dma_start(bias[:, :, :], b_q).then_inc(bias_landed, 16)
            sp.dma_start(x_raw[:, 1], x_cols[:, :, S:2 * S]).then_inc(x_landed[1], 16)
            sp.dma_start(wo_raw[:, :, :], w_out[0]).then_inc(wo_landed, 16)
            sp.dma_start(X[:, :, :], x_tok).then_inc(xtok_landed, 16)
            for b in range(2, B):
                sp.wait_ge(x_hi, b - 1)
                sp.wait_ge(x_lo, b - 1)
                sp.dma_start(x_raw[:, b % 2], x_cols[:, :, b * S:(b + 1) * S]).then_inc(x_landed[b % 2], 16)
            for g in range(1, KVG):
                for part in range(2):
                    sp.wait_ge(w_hi[part], g)
                    sp.wait_ge(w_lo[part], g)
                    load_w(g, part)
                sp.wait_ge(wo_hi, g)
                sp.wait_ge(wo_lo, g)
                sp.dma_start(wo_raw[:, :, :], w_out[g]).then_inc(wo_landed, 16)

        @block.gpsimd
        def _(pool):
            pool.memset(ones[:, :], 1.0).then_inc(consts, 1)
            pool.memset(pick, 0.0).then_inc(consts, 1)
            pool.wait_ge(consts, 2)
            pool.affine_select(out=pick, in_=pick, compare_op=ALU.not_equal, fill=1.0,
                               base=0, pattern=[[-1, GROUP], [0, P]], channel_multiplier=1).then_inc(consts, 1)

            def split_x(b):
                pool.wait_ge(x_hi, b + 1)
                pool.tensor_tensor(xl[:, :, b * S:(b + 1) * S], x_raw[:, b % 2],
                                   xh[:, :, b * S:(b + 1) * S].bitcast(F32), ALU.subtract).then_inc(x_lo, 1)

            def group(g):
                for b in range(B):
                    n = B * g + b
                    if b == 0:
                        if isinstance(g, int):
                            split_x(0)
                        pool.wait_ge(w_hi[1], g + 1)
                        w = W_COLS[1]
                        pool.tensor_tensor(wl[:, :, w], w_raw[:, :, w], wh[:, :, w].bitcast(F32), ALU.subtract).then_inc(w_lo[1], 1)
                    pool.wait_ge(kv_hi, n + 1)
                    pool.tensor_tensor(halves(1), by_kind(ykv), halves(0).bitcast(F32), ALU.subtract).then_inc(kv_lo, 1)
                    for i in range(2):
                        pool.wait_ge(q_hi, 2 * n + i + 1)
                        pool.tensor_tensor(ql[:, 2 * i:2 * i + 2], feat[:, 2 * i:2 * i + 2],
                                           qh[:, 2 * i:2 * i + 2].bitcast(F32), ALU.subtract).then_inc(q_lo, 1)
                        if i == 0 and isinstance(g, int) and b + 1 < B:
                            split_x(b + 1)
                    if b == 0:
                        pool.wait_ge(wo_hi, g + 1)
                        pool.tensor_tensor(wol[:, :, :], wo_raw[:, :, :], woh[:, :, :].bitcast(F32), ALU.subtract).then_inc(wo_lo, 1)

            steps(pool, group)

        @block.scalar
        def _(act):
            def split_x(b):
                act.wait_ge(x_landed[b % 2], 16 * (b // 2 + 1))
                act.copy(xh[:, :, b * S:(b + 1) * S], x_raw[:, b % 2]).then_inc(x_hi, 1)

            def split_w(g, part):
                act.wait_ge(w_landed[part], 16 * (g + 1))
                wait(act, projected, 3 * B * g)
                act.copy(wh[:, :, W_COLS[part]], w_raw[:, :, W_COLS[part]]).then_inc(w_hi[part], 1)

            def attn_hi(m):
                for i in range(2):
                    act.wait_ge(attended, 2 * m + i + 1)
                    wait(act, out_done, 2 * m)
                    act.copy(ah[:, 2 * i:2 * i + 2], at[:, 2 * i:2 * i + 2]).then_inc(a_hi, 1)

            def keep_num(m):
                act.wait_ge(applied, m + 1)
                wait(act, a_lo, 2 * m)
                for i in range(2):
                    act.copy(at[:, 2 * i:2 * i + 2].rearrange("p i s -> p (i s)"), p_num[i]).then_inc(num_kept, 1)

            def group(g):
                for b in range(B):
                    n = B * g + b
                    first = isinstance(n, int) and n == 0
                    if b == 0:
                        split_w(g, 0)
                        if first:
                            split_x(0)
                        split_w(g, 1)
                    act.wait_ge(clipped, 3 * n + 1)
                    act.activation(ek[:, :, :], ek[:, :, :], ACT.Exp).then_inc(exped, 1)
                    act.wait_ge(feat_k, n + 1)
                    wait(act, state, n)
                    act.copy(halves(0), by_kind(ykv)).then_inc(kv_hi, 1)
                    if not first:
                        keep_num(n - 1)
                    for i in range(2):
                        act.wait_ge(clipped, 3 * n + 2 + i)
                        act.activation(feat[:, 2 * i:2 * i + 2], feat[:, 2 * i:2 * i + 2], ACT.Exp).then_inc(exped, 1)
                        if i == 0 and not first:
                            attn_hi(n - 1)
                        act.wait_ge(feat_q, 2 * n + i + 1)
                        wait(act, applied, n)
                        act.copy(qh[:, 2 * i:2 * i + 2], feat[:, 2 * i:2 * i + 2]).then_inc(q_hi, 1)
                        if i == 0 and isinstance(g, int) and b + 1 < B:
                            split_x(b + 1)
                    if b == 0:
                        act.wait_ge(wo_landed, 16 * (g + 1))
                        wait(act, out_done, 2 * B * g)
                        act.copy(woh[:, :, :], wo_raw[:, :, :]).then_inc(wo_hi, 1)

            steps(act, group)
            keep_num(KVG * B - 1)
            attn_hi(KVG * B - 1)

        @block.vector
        def _(dve):
            def invert_norm(m):
                dve.wait_ge(normed, m + 1)
                dve.tensor_scalar(rec[:, :], p_norm, NORM_EPS, None, ALU.add).then_inc(norm_read, 1)
                dve.wait_ge(norm_read, m + 1)
                dve.reciprocal(rec[:, :], rec[:, :]).then_inc(inverted, 1)
                dve.wait_ge(inverted, m + 1)
                wait(dve, spread, m)
                dve.tensor_copy(rech[:, :], rec[:, :]).then_inc(rec_hi, 1)
                dve.wait_ge(rec_hi, m + 1)
                dve.tensor_tensor(recl[:, :], rec[:, :], rech[:, :].bitcast(F32), ALU.subtract).then_inc(rec_lo, 1)

            def attend(m):
                dve.wait_ge(spread, m + 1)
                dve.wait_ge(num_kept, 2 * m + 2)
                for i in range(2):
                    dve.tensor_tensor(at[:, 2 * i:2 * i + 2].rearrange("p i s -> p (i s)"), p_rec[i],
                                      at[:, 2 * i:2 * i + 2].rearrange("p i s -> p (i s)"), ALU.mult).then_inc(attended, 1)

            def attend_lo(m):
                for i in range(2):
                    dve.wait_ge(a_hi, 2 * m + i + 1)
                    dve.tensor_tensor(al[:, 2 * i:2 * i + 2], at[:, 2 * i:2 * i + 2], ah[:, 2 * i:2 * i + 2].bitcast(F32),
                                      ALU.subtract).then_inc(a_lo, 1)

            def add_out(m, b):
                for t in range(TB):
                    dve.wait_ge(out_done, 2 * m + t + 1)
                    dve.tensor_tensor(X[:, b * TB + t], X[:, b * TB + t], p_out[t], ALU.add).then_inc(added, 1)

            def scalar_of(ap, g, h):
                return ap[:, g, h:h + 1] if isinstance(g, int) else ap[:, bass.ds(g, 1), h]

            def q_clip(g, n, i):
                dve.wait_ge(projected, 3 * n + 2 + i)
                wait(dve, q_lo, 2 * n - 1 + i)
                for j in range(2):
                    c = dve.tensor_scalar(feat[:, 2 * i + j], p_q[i][:, j], scalar_of(bias, g, 2 * i + j), 0.0, ALU.add, ALU.min)
                c.then_inc(clipped, 1)

            def q_features(g, n, i):
                dve.wait_ge(exped, 3 * n + 2 + i)
                for j in range(2):
                    f = dve.scalar_tensor_tensor(out=feat[:, 2 * i + j], in0=p_q[i][:, j], scalar=scalar_of(bias1, g, 2 * i + j),
                                                 in1=feat[:, 2 * i + j], op0=ALU.add, op1=ALU.max)
                f.then_inc(feat_q, 1)

            def split_state(n):
                dve.wait_ge(state, n + 1)
                dve.tensor_copy(ksum[:, :], p_state[:, 2 * DH:2 * DH + 1]).then_inc(state_sum, 1)
                dve.tensor_copy(ssum[:, :], p_state[:, 0:DH]).then_inc(state_sum, 1)
                dve.wait_ge(state_sum, 3 * n + 2)
                dve.tensor_tensor(ssum[:, :], p_state[:, DH:2 * DH], ssum[:, :], ALU.add).then_inc(state_sum, 1)
                wait(dve, applied, n)
                dve.tensor_scalar(kselh[:, :, 0], ones[:, :], ksum[:, 0:1], None, ALU.mult)
                dve.wait_ge(state_sum, 3 * n + 3)
                dve.tensor_copy(kvh[:, :], ssum[:, :]).then_inc(state_hi, 1)
                dve.wait_ge(state_hi, n + 1)
                dve.tensor_scalar(ksell[:, :, 0], kselh[:, :, 0].bitcast(F32), -1.0, ksum[:, 0:1], ALU.mult, ALU.add)
                dve.tensor_tensor(kvl[:, :], ssum[:, :], kvh[:, :].bitcast(F32), ALU.subtract).then_inc(state_lo, 1)

            dve.memset(kselh[:, :, :].bitcast(F32), 0.0)
            dve.memset(ksell[:, :, :].bitcast(F32), 0.0)
            dve.memset(kvs[:, :, ONE:].bitcast(F32), 1.0).then_inc(zeroed, 1)
            dve.wait_ge(zeroed, 1)
            dve.wait_ge(consts, 3)
            dve.tensor_copy(pick_r[:, :, :], pick).then_inc(zeroed, 1)

            def group(g):
                for b in range(B):
                    n = B * g + b
                    first = isinstance(n, int) and n == 0
                    if b == 0:
                        dve.wait_ge(w_hi[0], g + 1)
                        w = W_COLS[0]
                        dve.tensor_tensor(wl[:, :, w], w_raw[:, :, w], wh[:, :, w].bitcast(F32), ALU.subtract).then_inc(w_lo[0], 1)
                        if first:
                            dve.wait_ge(bkv_landed, 16)
                            dve.wait_ge(bias_landed, 16)
                            dve.tensor_scalar(bias1[:, :, :], bias[:, :, :], 1.0, None, ALU.add).then_inc(bias1_ready, 1)
                            dve.wait_ge(bias1_ready, 1)
                    dve.wait_ge(projected, 3 * n + 1)
                    wait(dve, kv_lo, n)
                    cols = slice(g * KV, (g + 1) * KV) if isinstance(g, int) else bass.ds(g * KV, KV)
                    dve.tensor_tensor(ykv[:, :, :], p_kv, bias_kv[:, cols].unsqueeze(1).to_broadcast([P, TB, KV]), ALU.add).then_inc(kv_biased, 1)
                    dve.wait_ge(kv_biased, n + 1)
                    dve.tensor_scalar(ek[:, :, :], ykv[:, :, 0:DH], 0.0, None, ALU.min).then_inc(clipped, 1)
                    dve.wait_ge(exped, 3 * n + 1)
                    dve.scalar_tensor_tensor(out=ykv[:, :, 0:DH], in0=ykv[:, :, 0:DH], scalar=1.0, in1=ek[:, :, :],
                                             op0=ALU.add, op1=ALU.max).then_inc(feat_k, 1)
                    if not first:
                        invert_norm(n - 1)
                    q_clip(g, n, 0)
                    if not first:
                        attend(n - 1)
                    q_features(g, n, 0)
                    if not first:
                        attend_lo(n - 1)
                    q_clip(g, n, 1)
                    q_features(g, n, 1)
                    split_state(n)
                    if not first:
                        if isinstance(n, int) and n == 1:
                            dve.wait_ge(xtok_landed, 16)
                        add_out(n - 1, (b - 1) % B)

            steps(dve, group)
            invert_norm(KVG * B - 1)
            attend(KVG * B - 1)
            attend_lo(KVG * B - 1)
            add_out(KVG * B - 1, B - 1)

        @block.tensor
        def _(pe):
            def product(out, pairs):
                terms = [t for lh, ll, rh, rl in pairs for t in ((lh, rl), (ll, rh), (lh, rh))]
                for i, (a, c) in enumerate(terms):
                    mm = pe.matmul(out, a, c, start=(i == 0), stop=(i == len(terms) - 1))
                return mm

            def project_kv(b):
                for t in range(TB):
                    tok = slice(b * S + t * P, b * S + (t + 1) * P)
                    mm = product(p_kv[:, t], [(xh[:, k, tok], xl[:, k, tok], wh[:, k, W_COLS[0]], wl[:, k, W_COLS[0]]) for k in range(HK)])
                mm.then_inc(projected, 1)

            def project_q(b, i):
                cols = slice(b * S, (b + 1) * S)
                for j in range(2):
                    w = slice((2 * i + j) * DH, (2 * i + j + 1) * DH)
                    mm = product(p_q[i][:, j], [(wh[:, k, w], wl[:, k, w], xh[:, k, cols], xl[:, k, cols]) for k in range(HK)])
                mm.then_inc(projected, 1)

            def apply_state(m):
                pe.wait_ge(q_lo, 2 * m + 2)
                pe.wait_ge(q_hi, 2 * m + 2)
                pe.wait_ge(state_lo, m + 1)
                sel = [s[:, :, :].rearrange("p a b -> p (a b)") for s in (kselh, ksell)]
                product(p_norm, [(sel[0][:, GROUP * h:GROUP * (h + 1)], sel[1][:, GROUP * h:GROUP * (h + 1)], qh[:, h], ql[:, h])
                                 for h in range(GROUP)]).then_inc(normed, 1)
                wait(pe, num_kept, 2 * m)
                for i in range(2):
                    pair = [s[:, 2 * i:2 * i + 2].rearrange("p i s -> p (i s)") for s in (qh, ql)]
                    mm = product(p_num[i], [(kvh[:, :], kvl[:, :], pair[0], pair[1])])
                mm.then_inc(applied, 1)

            def spread_norm(m):
                pe.wait_ge(rec_lo, m + 1)
                wait(pe, added, 2 * m)
                for h in range(GROUP):
                    out = p_rec[h // 2][:, h % 2 * S:(h % 2 + 1) * S]
                    pe.matmul(out, pick_r[:, h], recl[:, :], start=True, stop=False)
                    mm = pe.matmul(out, pick_r[:, h], rech[:, :], start=False, stop=True)
                mm.then_inc(spread, 1)

            def form_state(n):
                pe.wait_ge(kv_hi, n + 1)
                pe.wait_ge(kv_lo, n + 1)
                wait(pe, norm_read, n)
                terms = [(t, half) for t in range(TB) for half in (KL, KH)]
                for j, (t, half) in enumerate(terms):
                    mm = pe.matmul(p_state, kvs[:, t, half:half + DH], kvs[:, t, VH:], start=(j == 0), stop=(j == len(terms) - 1))
                mm.then_inc(state, 1)

            def project_out(m):
                pe.wait_ge(a_lo, 2 * m + 2)
                for t in range(TB):
                    s = slice(t * P, (t + 1) * P)
                    product(p_out[t], [(ah[:, h, s], al[:, h, s], woh[:, h], wol[:, h]) for h in range(GROUP)]).then_inc(out_done, 1)

            pe.wait_ge(zeroed, 2)

            def group(g):
                for b in range(B):
                    n = B * g + b
                    first = isinstance(n, int) and n == 0
                    if b == 0:
                        pe.wait_ge(w_hi[0], g + 1)
                        pe.wait_ge(w_lo[0], g + 1)
                    if isinstance(g, int):
                        pe.wait_ge(x_hi, b + 1)
                        pe.wait_ge(x_lo, b + 1)
                    wait(pe, kv_biased, n)
                    project_kv(b)
                    if not first:
                        apply_state(n - 1)
                    if b == 0:
                        pe.wait_ge(w_hi[1], g + 1)
                        pe.wait_ge(w_lo[1], g + 1)
                    wait(pe, feat_q, 2 * n - 1)
                    project_q(b, 0)
                    if not first:
                        spread_norm(n - 1)
                    wait(pe, feat_q, 2 * n)
                    project_q(b, 1)
                    form_state(n)
                    if not first:
                        if b == 1:
                            pe.wait_ge(wo_hi, g + 1)
                            pe.wait_ge(wo_lo, g + 1)
                        project_out(n - 1)

            steps(pe, group)
            apply_state(KVG * B - 1)
            spread_norm(KVG * B - 1)
            project_out(KVG * B - 1)

    with nc.Block() as block:
        @block.gpsimd
        def _(pool):
            for signal in signals:
                pool.sem_clear(signal)


def project_context(nc, X, Q, K, V, ctx_cols, pos, w_q, w_k, w_v):
    HALF = XD // 2
    TWO_PI = 2 * np.pi
    PI2_HI = float(np.float32(6.28125))
    PI2_LO = float(np.float32(TWO_PI - 6.28125))
    ROUND = 12582912.0
    PI = float(np.nextafter(np.float32(np.pi), np.float32(0)))
    FREQS = [float(np.float32(10000.0 ** (-f / 4))) for f in range(4)]
    with ExitStack() as ctx:
        def sb(name, shape, dt=F32):
            return ctx.enter_context(nc.sbuf_tensor(name, shape, dt))

        def sem(name):
            return ctx.enter_context(nc.semaphore(name))

        wq = [Q[:, 12:16], sb("wq_h", [P, HK, HID], F32R), sb("wq_l", [P, HK, HID], F32R)]
        wk = [Q[:, 8:10], sb("wk_h", [P, CK, HID], F32R), sb("wk_l", [P, CK, HID], F32R)]
        wv = [Q[:, 10:12], sb("wv_h", [P, CK, HID], F32R), sb("wv_l", [P, CK, HID], F32R)]
        post = sb("positions", [P, NT, 2])
        cosk, sink, cosq, sinq, nsink, nsinq = (sb(n, [P, NT, HALF]) for n in ("cosk", "sink", "cosq", "sinq", "nsink", "nsinq"))
        ident = sb("ident2", [P, P])
        c_raw = [sb(f"c_raw{i}", [P, CK, P]) for i in range(2)]
        c_h = [sb(f"c_h{i}", [P, CK, P], F32R) for i in range(2)]
        c_l = [sb(f"c_l{i}", [P, CK, P], F32R) for i in range(2)]
        xn = [sb(f"xn{i}", [P, HID]) for i in range(2)]
        x_h = [sb(f"xt_h{i}", [P, HK, P], F32R) for i in range(2)]
        x_l = [sb(f"xt_l{i}", [P, HK, P], F32R) for i in range(2)]
        stats, mv, std, rstd = sb("stats", [P, 6]), sb("mv", [P, 2]), sb("std", [P, 1]), sb("rstd", [P, 1])
        straight = [sb(f"straight{i}", [P, HID]) for i in range(2)]
        crossed = [sb(f"crossed{i}", [P, HID]) for i in range(2)]
        ang, turns_, rad, bent = (straight[0][:, j * NT * HALF:(j + 1) * NT * HALF] for j in range(4))
        banks = ctx.enter_context(nc.psum_tensor("banks2", [P, 8, 512], F32))

        w_landed, pos_landed = [sem(f"xw_landed{i}") for i in range(3)], sem("pos_landed")
        c_landed = [sem("c_landed0"), sem("c_landed1")]
        w_hi, w_lo, wq_lo, consts = sem("xw_hi"), sem("xw_lo"), sem("xwq_lo"), sem("consts2")
        table, sined, tables_ready = sem("table"), sem("sined"), sem("tables_ready")
        c_hi, c_lo = sem("c_hi"), sem("c_lo")
        stat, rooted, rooted_inv, xn_ready, x_kept = sem("stat"), sem("rooted"), sem("rooted_inv"), sem("xn_ready"), sem("x_kept")
        x_turned, x_hi, x_lo = sem("x_turned"), sem("xt_hi"), sem("xt_lo")
        k_done, v_done, q_done = sem("k_done"), sem("v_done"), sem("q_done")
        v_copied, k_mult, q_mult, k_rot, q_rot = sem("v_copied"), sem("k_mult"), sem("q_mult"), sem("k_rot"), sem("q_rot")

        block = ctx.enter_context(nc.Block())

        def tiles(eng, body):
            with eng.Fori(0, NT // 2 - 1) as p:
                for i in range(2):
                    body(2 * p + i, i, False)
            body(NT - 2, 0, False)
            body(NT - 1, 1, True)

        def tile_of(ap, t):
            if isinstance(t, int):
                return ap[:, t]
            return ap[:, bass.ds(t, 1)].squeeze(1)

        @block.sync
        def _(sp):
            sp.dma_start(wk[0], w_k).then_inc(w_landed[0], 16)

            def body(t, i, last):
                if isinstance(t, int):
                    wait(sp, c_hi, t - 1)
                    wait(sp, c_lo, t - 1)
                    sp.dma_start(c_raw[i][:, :, :], ctx_cols[:, :, t * P:(t + 1) * P]).then_inc(c_landed[i], 16)
                else:
                    sp.wait_ge(c_hi, t - 1)
                    sp.wait_ge(c_lo, t - 1)
                    sp.dma_start(c_raw[i][:, :, :], ctx_cols[:, :, bass.ds(t * P, P)]).then_inc(c_landed[i], 16)

            body(0, 0, False)
            sp.dma_start(post[:, :, :], pos).then_inc(pos_landed, 16)
            sp.dma_start(wv[0], w_v).then_inc(w_landed[1], 16)
            sp.dma_start(wq[0], w_q).then_inc(w_landed[2], 16)
            body(1, 1, False)
            with sp.Fori(1, NT // 2) as p:
                for i in range(2):
                    body(2 * p + i, i, False)

        @block.gpsimd
        def _(pool):
            pool.memset(V[:, :, :, XD:XD + 1], 1.0).then_inc(consts, 1)
            pool.memset(ident[:, :], 0.0).then_inc(consts, 1)
            pool.wait_ge(consts, 2)
            pool.affine_select(out=ident[:, :], in_=ident[:, :], compare_op=ALU.not_equal, fill=1.0,
                               base=0, pattern=[[-1, P]], channel_multiplier=1).then_inc(consts, 1)
            def weights_lo(j, w):
                pool.wait_ge(w_hi, j + 1)
                pool.tensor_tensor(w[2][:, :, :], w[0], w[1][:, :, :].bitcast(F32), ALU.subtract).then_inc(w_lo, 1)

            weights_lo(0, wk)

            def context_lo(t, i):
                pool.wait_ge(c_hi, t + 1)
                pool.tensor_tensor(c_l[i][:, :, :], c_raw[i][:, :, :], c_h[i][:, :, :].bitcast(F32), ALU.subtract).then_inc(c_lo, 1)

            context_lo(0, 0)
            weights_lo(1, wv)

            def body(t, i, last):
                if not last:
                    context_lo(t + 1, 1 - i)
                wait_apart(pool, k_mult, t + 1, consts, 3)
                pool.tensor_tensor(tile_of(K, t), straight[0][:, :], crossed[0][:, :], ALU.add).then_inc(k_rot, 1)
                wait_apart(pool, q_mult, t + 1, consts, 3)
                pool.tensor_tensor(tile_of(Q, t), straight[1][:, :], crossed[1][:, :], ALU.add).then_inc(q_rot, 1)

            body(0, 0, False)
            body(1, 1, False)
            with pool.Fori(1, NT // 2 - 1) as p:
                for i in range(2):
                    body(2 * p + i, i, False)
            body(NT - 2, 0, False)
            body(NT - 1, 1, True)

        @block.scalar
        def _(act):
            def context_hi(t, i):
                act.wait_ge(c_landed[i], 16 * (t // 2 + 1) if isinstance(t, int) else 8 * (t - i) + 16)
                wait(act, v_done, t - 1)
                act.copy(c_h[i][:, :, :], c_raw[i][:, :, :]).then_inc(c_hi, 1)

            def root(t):
                act.wait_ge(stat, 3 * t + 3)
                act.sqrt(std[:, :], std[:, :]).then_inc(rooted, 1)

            root(0)
            for j, w in enumerate((wk, wv, wq)):
                act.wait_ge(w_landed[j], 16)
                act.copy(w[1][:, :, :], w[0]).then_inc(w_hi, 1)
                if j == 0:
                    context_hi(0, 0)
            act.wait_ge(table, 9)
            act.activation(sink[:, :, :].rearrange("p t f -> p (t f)"), rad[:, :], ACT.Sin).then_inc(sined, 1)
            act.activation(cosk[:, :, :].rearrange("p t f -> p (t f)"), bent[:, :], ACT.Sin).then_inc(sined, 1)

            def body(t, i, last):
                act.wait_ge(x_turned, t + 1)
                wait(act, q_done, t - 1)
                act.copy(x_h[i][:, :, :], banks[:, i].rearrange("p (k s) -> p k s", k=HK)).then_inc(x_hi, 1)
                if not last:
                    root(t + 1)
                    context_hi(t + 1, 1 - i)
                act.wait_ge(xn_ready, t + 1)
                act.copy(tile_of(X, t), xn[i][:, :]).then_inc(x_kept, 1)
                act.wait_ge(v_done, t + 1)
                act.copy(tile_of(V, t)[:, :, 0:XD], banks[:, 4 + i].rearrange("p (h d) -> p h d", d=XD)).then_inc(v_copied, 1)

            body(0, 0, False)
            body(1, 1, False)
            with act.Fori(1, NT // 2 - 1) as p:
                for i in range(2):
                    body(2 * p + i, i, False)
            body(NT - 2, 0, False)
            body(NT - 1, 1, True)

        @block.vector
        def _(dve):
            def norm_stats(t):
                dve.bn_stats(stats[:, :], tile_of(X, t)).then_inc(stat, 1)
                wait_apart(dve, stat, 3 * t + 1, pos_landed, 16)
                dve.bn_aggr(mv[:, :], stats[:, :]).then_inc(stat, 1)
                dve.wait_ge(stat, 3 * t + 2)
                dve.tensor_scalar(std[:, :], mv[:, 1:2], LN_EPS, None, ALU.add).then_inc(stat, 1)

            def normalise(t, i):
                dve.wait_ge(rooted, t + 1)
                dve.reciprocal(rstd[:, :], std[:, :]).then_inc(rooted_inv, 1)
                dve.wait_ge(rooted_inv, t + 1)
                wait(dve, x_turned, t - 1)
                wait(dve, x_kept, t - 1)
                dve.tensor_scalar(xn[i][:, :], tile_of(X, t), mv[:, 0:1], rstd[:, 0:1], ALU.subtract, ALU.mult).then_inc(xn_ready, 1)

            norm_stats(0)
            normalise(0, 0)
            dve.wait_ge(pos_landed, 16)
            av = ang[:, :].rearrange("p (t a f) -> p t a f", a=2, f=4)
            for f in range(4):
                a = dve.tensor_scalar(av[:, :, :, f], post[:, :, :], FREQS[f], None, ALU.mult)
            a.then_inc(table, 1)
            steps = [
                lambda: dve.tensor_scalar(turns_[:, :], ang[:, :], 1.0 / TWO_PI, ROUND, ALU.mult, ALU.add),
                lambda: dve.tensor_scalar(turns_[:, :], turns_[:, :], -ROUND, None, ALU.add),
                lambda: dve.scalar_tensor_tensor(out=rad[:, :], in0=turns_[:, :], scalar=-PI2_HI, in1=ang[:, :], op0=ALU.mult, op1=ALU.add),
                lambda: dve.scalar_tensor_tensor(out=rad[:, :], in0=turns_[:, :], scalar=-PI2_LO, in1=rad[:, :], op0=ALU.mult, op1=ALU.add),
                lambda: dve.tensor_scalar(rad[:, :], rad[:, :], PI, -PI, ALU.min, ALU.max),
                lambda: dve.tensor_scalar(bent[:, :], rad[:, :], -1.0, None, ALU.mult),
                lambda: dve.tensor_tensor(bent[:, :], rad[:, :], bent[:, :], ALU.max),
                lambda: dve.tensor_scalar(bent[:, :], bent[:, :], -1.0, PI / 2, ALU.mult, ALU.add),
            ]
            for n, step in enumerate(steps):
                dve.wait_ge(table, n + 1)
                step().then_inc(table, 1)

            def rotate(t, which, bank, done, rotated, mult, cos, sin, nsin):
                dve.wait_ge(done, t + 1)
                wait(dve, rotated, t)
                y = banks[:, bank].rearrange("p (h s f) -> p h s f", s=2, f=HALF)
                st = straight[which][:, :].rearrange("p (h s f) -> p h s f", s=2, f=HALF)
                cr = crossed[which][:, :].rearrange("p (h s f) -> p h s f", s=2, f=HALF)
                one = [P, XH, HALF]
                dve.tensor_tensor(st, y, tile_of(cos, t).unsqueeze(1).unsqueeze(1).to_broadcast([P, XH, 2, HALF]), ALU.mult)
                dve.tensor_tensor(cr[:, :, 0], y[:, :, 1], tile_of(nsin, t).unsqueeze(1).to_broadcast(one), ALU.mult)
                dve.tensor_tensor(cr[:, :, 1], y[:, :, 0], tile_of(sin, t).unsqueeze(1).to_broadcast(one), ALU.mult).then_inc(mult, 1)

            dve.wait_ge(w_hi, 3)
            dve.tensor_tensor(wq[2][:, :, :], wq[0], wq[1][:, :, :].bitcast(F32), ALU.subtract).then_inc(wq_lo, 1)
            dve.wait_ge(sined, 2)
            for k, (o, a, f) in enumerate(((nsink, sink, -1.0), (cosq, cosk, 0.25), (sinq, sink, 0.25), (nsinq, sink, -0.25))):
                dve.tensor_scalar(o[:, :, :], a[:, :, :], f, None, ALU.mult).then_inc(tables_ready, 1)
            dve.wait_ge(tables_ready, 4)

            def body(t, i, last):
                if not last:
                    norm_stats(t + 1)
                dve.wait_ge(x_hi, t + 1)
                wait(dve, q_done, t - 1)
                dve.tensor_tensor(x_l[i][:, :, :], banks[:, i].rearrange("p (k s) -> p k s", k=HK),
                                  x_h[i][:, :, :].bitcast(F32), ALU.subtract).then_inc(x_lo, 1)
                rotate(t, 0, 2 + i, k_done, k_rot, k_mult, cosk, sink, nsink)
                if not last:
                    normalise(t + 1, 1 - i)
                rotate(t, 1, 6 + i, q_done, q_rot, q_mult, cosq, sinq, nsinq)

            body(0, 0, False)
            body(1, 1, False)
            with dve.Fori(1, NT // 2 - 1) as p:
                for i in range(2):
                    body(2 * p + i, i, False)
            body(NT - 2, 0, False)
            body(NT - 1, 1, True)

        @block.tensor
        def _(pe):
            def product(out, pairs):
                terms = [t for lh, ll, rh, rl in pairs for t in ((lh, rl), (ll, rh), (lh, rh))]
                for i, (a, c) in enumerate(terms):
                    mm = pe.matmul(out, a, c, start=(i == 0), stop=(i == len(terms) - 1))
                return mm

            pe.wait_ge(consts, 3)

            def weights_split(t, hi, lo, count):
                if isinstance(t, int) and t == 0:
                    pe.wait_ge(w_hi, hi)
                    pe.wait_ge(lo, count)

            def body(t, i, last):
                pe.wait_ge(xn_ready, t + 1)
                wait(pe, x_lo, t - 1)
                for k in range(HK):
                    mm = pe.transpose(banks[:, i, k * P:(k + 1) * P], xn[i][:, k * P:(k + 1) * P], ident[:, :])
                mm.then_inc(x_turned, 1)
                pe.wait_ge(c_hi, t + 1)
                pe.wait_ge(c_lo, t + 1)
                weights_split(t, 1, w_lo, 1)
                wait(pe, k_mult, t - 1)
                product(banks[:, 2 + i], [(c_h[i][:, k], c_l[i][:, k], wk[1][:, k], wk[2][:, k]) for k in range(CK)]).then_inc(k_done, 1)
                weights_split(t, 2, w_lo, 2)
                wait(pe, v_copied, t - 1)
                product(banks[:, 4 + i], [(c_h[i][:, k], c_l[i][:, k], wv[1][:, k], wv[2][:, k]) for k in range(CK)]).then_inc(v_done, 1)
                pe.wait_ge(x_hi, t + 1)
                pe.wait_ge(x_lo, t + 1)
                weights_split(t, 3, wq_lo, 1)
                wait(pe, q_mult, t - 1)
                product(banks[:, 6 + i], [(x_h[i][:, k], x_l[i][:, k], wq[1][:, k], wq[2][:, k]) for k in range(HK)]).then_inc(q_done, 1)

            body(0, 0, False)
            body(1, 1, False)
            with pe.Fori(1, NT // 2) as p:
                for i in range(2):
                    body(2 * p + i, i, False)


def softmax_attention(nc, X, Q, K, V, b_out):
    G = 8
    NG = XH // G
    R = 64
    M0 = 2 * XD
    D0 = M0 + 2
    QUAD = 4
    VR = P // QUAD
    with ExitStack() as ctx:
        def sb(name, shape, dt=F32):
            return ctx.enter_context(nc.sbuf_tensor(name, shape, dt))

        def sem(name):
            return ctx.enter_context(nc.semaphore(name))

        bout = sb("bout", [P, HID])
        ident = sb("ident3", [P, P])
        place = sb("place", [P, TB, S], F32R)
        qpad = [sb(f"qpad{i}", [P, TB, G, R], F32R) for i in range(2)]
        kpad = [sb(f"kpad{i}", [P, TB, G, R], F32R) for i in range(2)]
        qT = sb("qT", [P, G // 2, S], F32R)
        qmT = [sb(f"qmT{i}", [P, G // 2, S], F32R) for i in range(2)]
        kT = [sb(f"kT{i}", [P, G // 2, 2, S], F32R) for i in range(2)]
        vz = [sb(f"vz{i}", [P, TB, P - VR + G * P]) for i in range(2)]
        probs = [sb(f"probs{i}", [P, TB, S]) for i in range(2)]
        pvs = [sb(f"pvs{i}", [P, S]) for i in range(2)]
        top = [sb(f"top{i}", [P, TB, G]) for i in range(2)]
        rsum = [sb(f"rsum{i}", [P, TB, QUAD]) for i in range(2)]
        one = sb("one", [P, 1])
        banks = ctx.enter_context(nc.psum_tensor("banks3", [P, 8, 512], F32))
        p_turn = banks[:, 0:2].rearrange("p c (j s) -> p (c j) s", s=S)
        p_raw = [banks[:, 2 + i].rearrange("p (t s) -> p t s", t=TB) for i in range(2)]
        p_shift = [banks[:, 4 + i].rearrange("p (t s) -> p t s", t=TB) for i in range(2)]
        p_pv = banks[:, 6, 0:S]
        p_back = banks[:, 7, 0:S].rearrange("p (t h d) -> p t h d", t=TB, h=QUAD)

        bout_landed, consts, cleared, placed = sem("bout_landed"), sem("consts3"), sem("cleared"), sem("placed")
        q_hi, k_hi, padded, k_padded, v_laid = sem("pq_hi"), sem("pk_hi"), sem("padded"), sem("k_padded"), sem("v_laid")
        q_turned, k_turned, m_turned = sem("q_turned"), sem("k_turned"), sem("m_turned")
        qT_ready, kT_ready, qmT_ready = sem("qT_ready"), sem("kT_ready"), sem("qmT_ready")
        scored, maxed, shift_hi, shift_lo = sem("scored"), sem("maxed"), sem("shift_hi"), sem("shift_lo")
        shifted, exped, pv_done, pv_kept = sem("shifted"), sem("exped3"), sem("pv_done"), sem("pv_kept")
        backed, inverted, written = sem("backed"), sem("inverted3"), sem("written")
        biased = sem("biased")

        block = ctx.enter_context(nc.Block())

        def groups(eng, body):
            def batch(b, last):
                for g in range(NG):
                    nxt = (b, g + 1) if g + 1 < NG else (b + 1, 0)
                    body(b, g, b * NG + g, None if last and g == NG - 1 else nxt)
            batch(0, False)
            with eng.Fori(1, B - 1) as b:
                batch(b, False)
            batch(B - 1, True)

        def part(ap, b, g, width, quad=None):
            rows = slice(b * TB, (b + 1) * TB) if isinstance(b, int) else bass.ds(b * TB, TB)
            first, heads = (g * G, G) if quad is None else (g * G + quad * QUAD, QUAD)
            return ap[:, rows, first * width:(first + heads) * width].rearrange("p t (h d) -> p t h d", d=width)

        @block.sync
        def _(sp):
            sp.dma_start(bout[:, :], b_out.partition_broadcast(P)).then_inc(bout_landed, 16)

        @block.gpsimd
        def _(pool):
            def clear(i):
                pool.memset(qpad[i][:, :, :, :].bitcast(F32), 0.0)
                pool.memset(kpad[i][:, :, :, :].bitcast(F32), 0.0).then_inc(cleared, 1)
                pool.wait_ge(cleared, 2 * i + 1)
                pool.memset(kpad[i][:, :, :, M0:D0].bitcast(F32), 1.0).then_inc(cleared, 1)

            pool.memset(ident[:, :], 0.0).then_inc(consts, 1)
            pool.memset(one[:, :], 1.0).then_inc(consts, 1)
            pool.wait_ge(consts, 2)
            pool.affine_select(out=ident[:, :], in_=ident[:, :], compare_op=ALU.not_equal, fill=1.0,
                               base=0, pattern=[[-1, P]], channel_multiplier=1).then_inc(consts, 1)

            def pad(b, g, n):
                i = g % 2
                q, k = part(Q, b, g, XD), part(K, b, g, XD)
                if not isinstance(n, int) or n >= 2:
                    wait_apart(pool, m_turned, n - 1, consts, 3)
                by_one = one[:, :].unsqueeze(2).unsqueeze(3).to_broadcast([P, TB, G, XD])
                pool.tensor_tensor(qpad[i][:, :, :, 0:XD], q, by_one, ALU.mult)
                pool.tensor_copy(qpad[i][:, :, :, D0:D0 + XD], q).then_inc(q_hi, 1)
                pool.tensor_copy(kpad[i][:, :, :, 0:XD], k)
                pool.tensor_copy(kpad[i][:, :, :, XD:M0], k).then_inc(k_hi, 1)
                pool.memset(qpad[i][:, :, :, M0:D0].bitcast(F32), 0.0)
                wait_apart(pool, q_hi, n + 1, consts, 3)
                pool.tensor_tensor(qpad[i][:, :, :, XD:M0], q, qpad[i][:, :, :, 0:XD].bitcast(F32), ALU.subtract).then_inc(padded, 1)
                wait_apart(pool, k_hi, n + 1, consts, 3)
                pool.tensor_tensor(kpad[i][:, :, :, D0:D0 + XD], k, kpad[i][:, :, :, 0:XD].bitcast(F32), ALU.subtract).then_inc(k_padded, 1)

            def lay_v(b, g, n):
                i = g % 2
                rows = slice(b * TB, (b + 1) * TB) if isinstance(b, int) else bass.ds(b * TB, TB)
                if not isinstance(n, int) or n >= 2:
                    wait_apart(pool, pv_done, G * (n - 1), consts, 3)
                pool.tensor_copy(vz[i][:, :, P - VR:].rearrange("p t (h c) -> p t h c", c=P)[:, :, :, 0:XD + 1],
                                 V[:, rows, g * G:(g + 1) * G]).then_inc(v_laid, 1)

            clear(0)
            pool.wait_ge(cleared, 2)
            pad(0, 0, 0)
            clear(1)
            pool.wait_ge(cleared, 4)
            pool.wait_ge(placed, 4)
            lay_v(0, 0, 0)

            def body(b, g, n, nxt):
                if nxt:
                    pad(*nxt, n + 1)
                    lay_v(*nxt, n + 1)

            groups(pool, body)
            pool.wait_ge(bout_landed, 16)
            for t in range(NT):
                pool.tensor_tensor(X[:, t], X[:, t], bout[:, :], ALU.add).then_inc(biased, 1)

        @block.scalar
        def _(act):
            def keep_k(n, i, r):
                act.wait_ge(k_turned, n + 1)
                if not isinstance(n, int) or n >= 2:
                    act.wait_ge(shifted, G * (n - 1))
                rows = slice(r * R, (r + 1) * R)
                act.copy(kT[i][rows, :, r], p_turn[rows]).then_inc(kT_ready, 1)

            def keep_m(n, i):
                act.wait_ge(m_turned, n + 1)
                if not isinstance(n, int) or n >= 2:
                    act.wait_ge(shifted, G * (n - 1))
                act.copy(qmT[i][:, :, :], p_turn).then_inc(qmT_ready, 1)

            def keep_pv(n, quad):
                act.wait_ge(pv_done, G * n + QUAD * (quad + 1))
                if not isinstance(n, int) or n >= 1:
                    act.wait_ge(backed, 2 * n - 1 + quad)
                act.copy(pvs[quad][:, :], p_pv).then_inc(pv_kept, 1)

            act.wait_ge(placed, 3)
            for r in range(2):
                keep_k(0, 0, r)
            keep_m(0, 0)

            def body(b, g, n, nxt):
                for h in range(G):
                    act.wait_ge(shifted, G * n + h + 1)
                    if not isinstance(n, int) or G * n + h >= 2:
                        act.wait_ge(pv_done, G * n + h - 1)
                    act.activation(probs[h % 2][:, :, :], p_shift[h % 2], ACT.Exp).then_inc(exped, 1)
                    if h in (1, 2) and nxt:
                        keep_k(n + 1, (g + 1) % 2, h - 1)
                    if h == QUAD:
                        keep_pv(n, 0)
                if nxt:
                    keep_m(n + 1, (g + 1) % 2)
                keep_pv(n, 1)

            groups(act, body)

        @block.vector
        def _(dve):
            dve.memset(place[:, :, :].bitcast(F32), 0.0).then_inc(placed, 1)
            dve.wait_ge(consts, 3)
            dve.wait_ge(placed, 1)
            for t in range(TB):
                z = dve.tensor_copy(place[:, t, t * P:(t + 1) * P], ident[:, :])
            z.then_inc(placed, 1)
            for i in range(2):
                z = dve.memset(kT[i][:, :, :, :].bitcast(F32), 0.0)
            z.then_inc(placed, 1)
            for i in range(2):
                z = dve.memset(vz[i][:, :, :], 0.0)
            z.then_inc(placed, 1)

            def keep_q(n):
                dve.wait_ge(q_turned, n + 1)
                wait(dve, scored, G * n)
                dve.tensor_copy(qT[:, :, :], p_turn).then_inc(qT_ready, 1)

            def row_max(n, h, i):
                dve.wait_ge(scored, G * n + h + 1)
                dve.tensor_reduce(top[i][:, :, h], p_raw[h % 2], AX.X, ALU.max).then_inc(maxed, 1)

            def shift(n, i):
                dve.wait_ge(maxed, G * n + G)
                dve.tensor_scalar(qpad[i][:, :, :, M0], top[i][:, :, :], -1.0, None, ALU.mult).then_inc(shift_hi, 1)
                dve.wait_ge(shift_hi, n + 1)
                dve.scalar_tensor_tensor(out=qpad[i][:, :, :, M0 + 1], in0=top[i][:, :, :], scalar=-1.0,
                                         in1=qpad[i][:, :, :, M0].bitcast(F32), op0=ALU.mult, op1=ALU.subtract).then_inc(shift_lo, 1)

            def write(b, g, n, quad):
                dve.wait_ge(backed, 2 * n + quad + 1)
                wait(dve, written, 2 * n + quad)
                dve.reciprocal(rsum[quad][:, :, :], p_back[:, :, :, XD]).then_inc(inverted, 1)
                dve.wait_ge(inverted, 2 * n + quad + 1)
                dve.tensor_tensor(part(Q, b, g, XD, quad), p_back[:, :, :, 0:XD],
                                  rsum[quad][:, :, :].unsqueeze(3).to_broadcast([P, TB, QUAD, XD]), ALU.mult).then_inc(written, 1)

            keep_q(0)
            for h in range(G):
                row_max(0, h, 0)
            shift(0, 0)

            def body(b, g, n, nxt):
                if nxt:
                    keep_q(n + 1)
                if not (isinstance(n, int) and n == 0):
                    write(b if g else b - 1, (g - 1) % NG, n - 1, 1)
                if nxt:
                    for h in range(G - 2):
                        row_max(n + 1, h, (g + 1) % 2)
                write(b, g, n, 0)
                if nxt:
                    for h in range(G - 2, G):
                        row_max(n + 1, h, (g + 1) % 2)
                    shift(n + 1, (g + 1) % 2)

            groups(dve, body)
            write(B - 1, NG - 1, B * NG - 1, 1)

        @block.tensor
        def _(pe):
            def turn(pad, i, done):
                for j in range(G // 2):
                    for t in range(TB):
                        mm = pe.matmul(p_turn[:, j], pad[i][:, t, 2 * j:2 * j + 2].rearrange("p h r -> p (h r)"), place[:, t],
                                       start=(t == 0), stop=(t == TB - 1))
                mm.then_inc(done, 1)

            def turn_q(n, i):
                pe.wait_ge(padded, n + 1)
                wait(pe, qmT_ready, n)
                turn(qpad, i, q_turned)

            def turn_k(n, i):
                pe.wait_ge(k_padded, n + 1)
                pe.wait_ge(qT_ready, n + 1)
                turn(kpad, i, k_turned)

            def turn_m(n, i):
                pe.wait_ge(shift_lo, n + 1)
                pe.wait_ge(kT_ready, 2 * n + 2)
                turn(qpad, i, m_turned)

            def raw_scores(n, h, i):
                pe.wait_ge(kT_ready, 2 * n + 2)
                if not isinstance(n, int) or G * n + h >= 2:
                    pe.wait_ge(maxed, G * n + h - 1)
                for t in range(TB):
                    mm = pe.matmul(p_raw[h % 2][:, t], qT[:, h // 2, t * P:(t + 1) * P], kT[i][:, h // 2, h % 2], start=True, stop=True)
                mm.then_inc(scored, 1)

            def shifted_scores(n, h, i):
                pe.wait_ge(qmT_ready, n + 1)
                if not isinstance(n, int) or G * n + h >= 2:
                    pe.wait_ge(exped, G * n + h - 1)
                for t in range(TB):
                    mm = pe.matmul(p_shift[h % 2][:, t], kT[i][:, h // 2, h % 2, t * P:(t + 1) * P], qmT[i][:, h // 2], start=True, stop=True)
                mm.then_inc(shifted, 1)

            def values(n, h, i):
                pe.wait_ge(exped, G * n + h + 1)
                quad, j = h // QUAD, h % QUAD
                if j == 0:
                    pe.wait_ge(v_laid, n + 1)
                    wait(pe, pv_kept, 2 * n + quad)
                window = slice(P - VR + h * P - j * VR, P - VR + (h + 1) * P - j * VR)
                for kt in range(TB):
                    mm = pe.matmul(p_pv, vz[i][:, kt, window], probs[h % 2][:, kt],
                                   start=(j == 0 and kt == 0), stop=(j == QUAD - 1 and kt == TB - 1))
                mm.then_inc(pv_done, 1)

            def turn_back(n, quad):
                pe.wait_ge(pv_kept, 2 * n + quad + 1)
                wait(pe, written, 2 * n + quad)
                for t in range(TB):
                    mm = pe.transpose(p_back[:, t].rearrange("p h d -> p (h d)"), pvs[quad][:, t * P:(t + 1) * P], ident[:, :])
                mm.then_inc(backed, 1)

            pe.wait_ge(consts, 3)
            pe.wait_ge(placed, 2)
            turn_q(0, 0)
            turn_k(0, 0)
            for h in range(G):
                raw_scores(0, h, 0)
            turn_m(0, 0)

            def body(b, g, n, nxt):
                i, ni = g % 2, (g + 1) % 2
                for h in range(G):
                    shifted_scores(n, h, i)
                    if h == 0 and nxt:
                        turn_q(n + 1, ni)
                    if h == 1 and not (isinstance(n, int) and n == 0):
                        turn_back(n - 1, 1)
                    scored_beside = nxt and 3 <= h < G - 1
                    if scored_beside and h > 3:
                        raw_scores(n + 1, 2 * h - 6, ni)
                    if h:
                        values(n, h - 1, i)
                    if h == 1 and nxt:
                        turn_k(n + 1, ni)
                    if scored_beside and h == 3:
                        raw_scores(n + 1, 0, ni)
                    if scored_beside:
                        raw_scores(n + 1, 2 * h - 5, ni)
                    if h == 5:
                        turn_back(n, 0)
                if nxt:
                    turn_m(n + 1, ni)
                values(n, G - 1, i)

            groups(pe, body)
            turn_back(B * NG - 1, 1)




def project_attention(nc, X, A, xh, xl, w_out):
    with ExitStack() as ctx:
        def sb(name, shape, dt=F32):
            return ctx.enter_context(nc.sbuf_tensor(name, shape, dt))

        def sem(name):
            return ctx.enter_context(nc.semaphore(name))

        w_raw, wh, wl = sb("wo4_raw", [P, HK, HID]), sb("wo4_h", [P, HK, HID], F32R), sb("wo4_l", [P, HK, HID], F32R)
        ident = sb("ident4", [P, P])
        a_in = [sb(f"a_in{i}", [P, HID]) for i in range(2)]
        a_h = [sb(f"a4_h{i}", [P, HK, P], F32R) for i in range(2)]
        a_l = [sb(f"a4_l{i}", [P, HK, P], F32R) for i in range(2)]
        total = sb("total", [P, HID])
        xn = [sb(f"xn4_{i}", [P, HID]) for i in range(2)]
        stats, mv, std, rstd = sb("stats4", [P, 6]), sb("mv4", [P, 2]), sb("std4", [P, 1]), sb("rstd4", [P, 1])
        banks = ctx.enter_context(nc.psum_tensor("banks4", [P, 8, 512], F32))

        w_landed, w_hi, w_lo, consts = sem("wo4_landed"), sem("wo4_hi"), sem("wo4_lo"), sem("consts4")
        a_copied, a_turned, a_hi, a_lo = sem("a_copied"), sem("a_turned"), sem("a4_hi"), sem("a4_lo")
        out_done, stat, rooted, inverted, xn_ready, x_kept = (sem(n) for n in ("out4", "stat4", "rooted4", "inverted4", "xn4_ready", "x4_kept"))
        summed, x_turned, x_hi, x_lo = sem("summed4"), sem("x4_turned"), sem("x4_hi"), sem("x4_lo")

        block = ctx.enter_context(nc.Block())

        def tiles(eng, body):
            body(0, 0, False)
            body(1, 1, False)
            with eng.Fori(1, NT // 2 - 1) as p:
                for i in range(2):
                    body(2 * p + i, i, False)
            body(NT - 2, 0, False)
            body(NT - 1, 1, True)

        def tile_of(ap, t):
            if isinstance(t, int):
                return ap[:, t]
            return ap[:, bass.ds(t, 1)].squeeze(1)

        def columns_of(ap, t):
            return ap[:, :, t * P:(t + 1) * P] if isinstance(t, int) else ap[:, :, bass.ds(t * P, P)]

        @block.sync
        def _(sp):
            sp.dma_start(w_raw[:, :, :], w_out).then_inc(w_landed, 16)

        @block.gpsimd
        def _(pool):
            pool.memset(ident[:, :], 0.0).then_inc(consts, 1)
            pool.wait_ge(consts, 1)
            pool.affine_select(out=ident[:, :], in_=ident[:, :], compare_op=ALU.not_equal, fill=1.0,
                               base=0, pattern=[[-1, P]], channel_multiplier=1).then_inc(consts, 1)

            def body(t, i, last):
                wait_apart(pool, a_turned, t - 1, consts, 2) if not isinstance(t, int) else wait(pool, a_turned, t - 1)
                pool.tensor_copy(a_in[i][:, :], tile_of(A, t)).then_inc(a_copied, 1)

            tiles(pool, body)

        @block.scalar
        def _(act):
            def x_split(t, i):
                act.wait_ge(x_turned, t + 1)
                act.copy(columns_of(xh, t), banks[:, 4 + i].rearrange("p (k s) -> p k s", k=HK)).then_inc(x_hi, 1)

            def a_split(t, i):
                act.wait_ge(a_turned, t + 1)
                wait(act, out_done, t - 1)
                act.copy(a_h[i][:, :, :], banks[:, i].rearrange("p (k s) -> p k s", k=HK)).then_inc(a_hi, 1)

            a_split(0, 0)
            act.wait_ge(w_landed, 16)
            act.copy(wh[:, :, :], w_raw[:, :, :]).then_inc(w_hi, 1)

            def body(t, i, last):
                if not last:
                    a_split(t + 1, 1 - i)
                act.wait_ge(stat, 3 * t + 3)
                act.sqrt(std[:, :], std[:, :]).then_inc(rooted, 1)
                if not isinstance(t, int) or t:
                    x_split(t - 1, 1 - i)
                act.wait_ge(xn_ready, t + 1)
                act.copy(tile_of(X, t), xn[i][:, :]).then_inc(x_kept, 1)

            tiles(act, body)
            x_split(NT - 1, (NT - 1) % 2)

        @block.vector
        def _(dve):
            def x_split(t, i):
                dve.wait_ge(x_hi, t + 1)
                dve.tensor_tensor(columns_of(xl, t), banks[:, 4 + i].rearrange("p (k s) -> p k s", k=HK),
                                  columns_of(xh, t).bitcast(F32), ALU.subtract).then_inc(x_lo, 1)

            def a_split(t, i):
                dve.wait_ge(a_hi, t + 1)
                dve.tensor_tensor(a_l[i][:, :, :], banks[:, i].rearrange("p (k s) -> p k s", k=HK),
                                  a_h[i][:, :, :].bitcast(F32), ALU.subtract).then_inc(a_lo, 1)

            a_split(0, 0)
            dve.wait_ge(w_hi, 1)
            dve.tensor_tensor(wl[:, :, :], w_raw[:, :, :], wh[:, :, :].bitcast(F32), ALU.subtract).then_inc(w_lo, 1)

            def body(t, i, last):
                dve.wait_ge(out_done, t + 1)
                wait(dve, xn_ready, t)
                dve.tensor_tensor(total[:, :], banks[:, 2 + i], tile_of(X, t), ALU.add).then_inc(summed, 1)
                dve.wait_ge(summed, t + 1)
                dve.bn_stats(stats[:, :], total[:, :]).then_inc(stat, 1)
                wait_apart(dve, stat, 3 * t + 1, consts, 2)
                dve.bn_aggr(mv[:, :], stats[:, :]).then_inc(stat, 1)
                dve.wait_ge(stat, 3 * t + 2)
                dve.tensor_scalar(std[:, :], mv[:, 1:2], LN_EPS, None, ALU.add).then_inc(stat, 1)
                if not last:
                    a_split(t + 1, 1 - i)
                dve.wait_ge(rooted, t + 1)
                dve.reciprocal(rstd[:, :], std[:, :]).then_inc(inverted, 1)
                dve.wait_ge(inverted, t + 1)
                wait(dve, x_turned, t - 1)
                wait(dve, x_kept, t - 1)
                dve.tensor_scalar(xn[i][:, :], total[:, :], mv[:, 0:1], rstd[:, 0:1], ALU.subtract, ALU.mult).then_inc(xn_ready, 1)
                if not isinstance(t, int) or t:
                    x_split(t - 1, 1 - i)

            tiles(dve, body)
            x_split(NT - 1, (NT - 1) % 2)

        @block.tensor
        def _(pe):
            def product(out, pairs):
                terms = [t for lh, ll, rh, rl in pairs for t in ((lh, rl), (ll, rh), (lh, rh))]
                for i, (a, c) in enumerate(terms):
                    mm = pe.matmul(out, a, c, start=(i == 0), stop=(i == len(terms) - 1))
                return mm

            def turn_x(t, i):
                pe.wait_ge(xn_ready, t + 1)
                wait(pe, x_lo, t - 1)
                for k in range(HK):
                    mm = pe.transpose(banks[:, 4 + i, k * P:(k + 1) * P], xn[i][:, k * P:(k + 1) * P], ident[:, :])
                mm.then_inc(x_turned, 1)

            def turn_a(t, i):
                pe.wait_ge(a_copied, t + 1)
                wait(pe, a_lo, t - 1)
                for k in range(HK):
                    mm = pe.transpose(banks[:, i, k * P:(k + 1) * P], a_in[i][:, k * P:(k + 1) * P], ident[:, :])
                mm.then_inc(a_turned, 1)

            pe.wait_ge(consts, 2)
            turn_a(0, 0)

            def body(t, i, last):
                if not last:
                    turn_a(t + 1, 1 - i)
                if isinstance(t, int) and t == 0:
                    pe.wait_ge(w_hi, 1)
                    pe.wait_ge(w_lo, 1)
                pe.wait_ge(a_hi, t + 1)
                pe.wait_ge(a_lo, t + 1)
                wait(pe, summed, t - 1)
                product(banks[:, 2 + i], [(a_h[i][:, k], a_l[i][:, k], wh[:, k], wl[:, k]) for k in range(HK)]).then_inc(out_done, 1)
                if not isinstance(t, int) or t:
                    turn_x(t - 1, 1 - i)

            tiles(pe, body)
            turn_x(NT - 1, (NT - 1) % 2)


def prefix_sums(step, dve, src, spare, n):
    reach = 1
    while reach < n:
        dve.tensor_copy(spare[..., 0:reach], src[..., 0:reach])
        step(dve.tensor_tensor(spare[..., reach:n], src[..., reach:n], src[..., 0:n - reach], ALU.add))
        src, spare = spare, src
        reach *= 2
    return src


def route_and_share(nc, X, scratch, xh, xl, gate_cols, expert_bias, w_gu, w_down, shape_consts, x_rows, sums, tables):
    source, target, share, owner = tables
    NBLK = 4
    W = T // NBLK
    TPB = W // P
    MK = FF // P
    NONE = 3e38
    ROUND = 12582912.0
    HALVES = TILES * SLOTS // P
    DOWN_BANKS = 3
    with ExitStack() as ctx:
        def sb(name, shape, dt=F32):
            return ctx.enter_context(nc.sbuf_tensor(name, shape, dt))

        def sem(name):
            return ctx.enter_context(nc.semaphore(name))

        flat = scratch[:, :, :].rearrange("p t h -> p (t h)")
        GU = HK * 2 * FF
        gu_raw = flat[:, 0:GU].rearrange("p (k f) -> p k f", k=HK)
        dn_raw = flat[:, GU:GU + MK * HID].rearrange("p (k h) -> p k h", k=MK)
        silu = flat[:, 3072:3072 + 2 * W].rearrange("p (m s) -> p m s", m=MK)
        hid = flat[:, 4096:4096 + 2 * W].rearrange("p (m s) -> p m s", m=MK)
        lcols = flat[0:E, 5120:5120 + T]
        picked, product_ = (flat[:, 5120 + i * T:5120 + i * T + TOPK * NT * E].rearrange("p (k t e) -> p k t e", k=TOPK, t=NT) for i in range(2))
        gu_h, gu_l = sb("gus_h", [P, HK, 2 * FF], F32R), sb("gus_l", [P, HK, 2 * FF], F32R)
        dn_h, dn_l = sb("dns_h", [P, MK, HID], F32R), sb("dns_l", [P, MK, HID], F32R)
        hid_h = [sb(f"hids_h{i}", [P, MK, W], F32R) for i in range(2)]
        hid_l = [sb(f"hids_l{i}", [P, MK, W], F32R) for i in range(2)]
        gw_raw = sb("gw_raw", [P, HK, E])
        gw_h, gw_l = sb("gw_h", [P, HK, E], F32R), sb("gw_l", [P, HK, E], F32R)
        ebias = sb("ebias", [P, E])
        ident, ones = sb("ident5", [P, P]), sb("ones5", [P, P])
        zeros = sb("zeros5", [P, HID])
        shapes = sb("shapes", [P, 2 * P + NT + 1])
        seq, before, token1, spare_row1 = shapes[:, 0:P], shapes[:, P:2 * P], shapes[:, 2 * P:2 * P + NT], shapes[:, 2 * P + NT:]
        score, biased, chosen, weight, slot = (sb(n, [P, NT, E]) for n in ("score", "biased", "chosen", "weight", "slot"))
        total, psum_a, psum_b, left = (sb(n, [P, NT, E]) for n in ("total5", "prefix_a", "prefix_b", "left"))
        best = sb("best", [P, NT, 8])
        wsum = sb("wsum", [P, NT])
        ntiles, ends, ends_b, base = (sb(n, [P, E]) for n in ("ntiles", "ends", "ends_b", "base"))
        passed, owner_f = sb("passed", [1, TILES, E]), sb("owner_f", [1, TILES])
        slot_k, half_k, place_k, half_r = (sb(n, [P, TOPK, NT]) for n in ("slot_k", "half_k", "place_k", "half_r"))
        weight_k, weight_kh = sb("weight_k", [P, TOPK, NT]), sb("weight_kh", [P, TOPK, NT], F32R)
        entry = sb("entry", [P, NT, TOPK, 3])
        at_place = [sb(f"at_place{i}", [P, TOPK, P], F32R) for i in range(2)]
        in_half = [sb(f"in_half{i}", [P, TOPK, HALVES]) for i in range(2)]
        valued = [sb(f"valued{i}", [P, TOPK, 3, HALVES], F32R) for i in range(2)]
        found, spare_rows, index_f = sb("found", [P, HALVES]), sb("spare_rows", [P, HALVES]), sb("index_f", [P, HALVES])
        banks = ctx.enter_context(nc.psum_tensor("banks5", [P, 8, 512], F32))
        p_within, p_total = banks[:, 7, 0:NT * E], banks[:, 7, NT * E:2 * NT * E]
        p_table = banks[:, 7, 0:3 * HALVES]

        gw_landed, eb_landed, shapes_landed = sem("gw_landed"), sem("eb_landed"), sem("shapes_landed")
        gu_landed, dn_landed = sem("gus_landed"), sem("dns_landed")
        consts, gw_hi, gw_lo = sem("consts5"), sem("gw_hi"), sem("gw_lo")
        gu_hi, gu_lo, dn_hi, dn_lo = sem("gus_hi"), sem("gus_lo"), sem("dns_hi"), sem("dns_lo")
        routed, lcopied, lturned, sigmoided, steps = (sem(n) for n in ("routed", "lcopied", "lturned", "sigmoided", "steps"))
        counted, counts_read, onehot, tabled = sem("counted"), sem("counts_read"), sem("onehot"), sem("tabled")
        chosen_ready, entered = sem("chosen_ready"), sem("entered")
        hidden, silued, gated, h_hi, h_lo = (sem(n) for n in ("hidden_s", "silued_s", "gated_s", "hs_hi", "hs_lo"))
        down, summed = sem("down_s"), sem("summed_s")
        rows_stored, sums_stored, spare_stored, zeros_stored = sem("rows_stored"), sem("sums_stored"), sem("spare_stored"), sem("zeros_stored")

        block = ctx.enter_context(nc.Block())

        def by_tile(dram):
            return dram.rearrange("(t p) h -> p t h", p=P)

        @block.sync
        def _(sp):
            sp.dma_start(gw_raw[:, :, :], gate_cols).then_inc(gw_landed, 16)
            sp.dma_start(ebias[:, :], expert_bias.partition_broadcast(P)).then_inc(eb_landed, 16)
            sp.dma_start(gu_raw, w_gu[E]).then_inc(gu_landed, 16)
            sp.dma_start(shapes[:, :], shape_consts).then_inc(shapes_landed, 16)
            sp.dma_start(dn_raw, w_down[E]).then_inc(dn_landed, 16)
            sp.dma_start(by_tile(x_rows), X[:, :, :]).then_inc(rows_stored, 16)
            sp.wait_ge(consts, 4)
            sp.dma_start(sums[0][T:T + P], zeros[:, :]).then_inc(spare_stored, 16)
            sp.dma_start(by_tile(sums[1]), zeros[:, :].unsqueeze(1).to_broadcast([P, NT + 1, HID])).then_inc(zeros_stored, 16)
            for c in range(NBLK):
                sp.wait_ge(summed, TPB * (c + 1))
                tiles = slice(c * TPB, (c + 1) * TPB)
                sp.dma_start(by_tile(sums[0][0:T])[:, tiles], X[:, tiles]).then_inc(sums_stored, 16)
            sp.wait_ge(spare_stored, 16)
            sp.wait_ge(zeros_stored, 16)
            sp.wait_ge(sums_stored, 16 * NBLK)

        @block.gpsimd
        def _(pool):
            pool.memset(ident[:, :], 0.0).then_inc(consts, 1)
            pool.memset(ones[:, :], 1.0).then_inc(consts, 1)
            pool.memset(zeros[:, :], 0.0).then_inc(consts, 1)
            pool.wait_ge(consts, 3)
            pool.affine_select(out=ident[:, :], in_=ident[:, :], compare_op=ALU.not_equal, fill=1.0,
                               base=0, pattern=[[-1, P]], channel_multiplier=1).then_inc(consts, 1)
            pool.wait_ge(gw_hi, 1)
            pool.tensor_tensor(gw_l[:, :, :], gw_raw[:, :, :], gw_h[:, :, :].bitcast(F32), ALU.subtract).then_inc(gw_lo, 1)
            pool.wait_ge(gu_hi, 1)
            pool.tensor_tensor(gu_l[:, :, :], gu_raw, gu_h[:, :, :].bitcast(F32), ALU.subtract).then_inc(gu_lo, 1)
            pool.wait_ge(dn_hi, 1)
            pool.tensor_tensor(dn_l[:, :, :], dn_raw, dn_h[:, :, :].bitcast(F32), ALU.subtract).then_inc(dn_lo, 1)
            for t in range(NT):
                i = t % 2
                pool.wait_ge(onehot, t + 1)
                wait(pool, tabled, t - 1)
                pool.tensor_tensor(valued[i][:, :, :, :], in_half[i][:, :, :].unsqueeze(2).to_broadcast([P, TOPK, 3, HALVES]),
                                   entry[:, t].unsqueeze(3).to_broadcast([P, TOPK, 3, HALVES]), ALU.mult).then_inc(entered, 1)

        @block.scalar
        def _(act):
            act.wait_ge(gw_landed, 16)
            act.copy(gw_h[:, :, :], gw_raw[:, :, :]).then_inc(gw_hi, 1)
            act.wait_ge(gu_landed, 16)
            act.copy(gu_h[:, :, :], gu_raw).then_inc(gu_hi, 1)
            for c in range(NBLK):
                act.wait_ge(routed, c + 1)
                act.copy(lcols[:, c * W:(c + 1) * W], banks[0:E, c]).then_inc(lcopied, 1)
            act.wait_ge(lturned, 1)
            act.activation(score[:, :, :].rearrange("p t e -> p (t e)"), banks[:, 4, 0:NT * E], ACT.Sigmoid).then_inc(sigmoided, 1)
            act.wait_ge(dn_landed, 16)
            act.copy(dn_h[:, :, :], dn_raw).then_inc(dn_hi, 1)
            for c in range(NBLK):
                for m in range(MK):
                    act.wait_ge(hidden, 2 * MK * c + 2 * m + 1)
                    wait(act, gated, MK * (c - 1) + m + 1)
                    act.activation(silu[:, m], banks[:, 2 * m], ACT.Silu).then_inc(silued, 1)
                for m in range(MK):
                    act.wait_ge(gated, MK * c + m + 1)
                    wait(act, down, TPB * (c - 1))
                    act.copy(hid_h[c % 2][:, m], hid[:, m]).then_inc(h_hi, 1)

        @block.vector
        def _(dve):
            n_steps = [0]

            def step(ins):
                n_steps[0] += 1
                ins.then_inc(steps, 1)
                dve.wait_ge(steps, n_steps[0])

            def choose():
                dve.wait_ge(eb_landed, 16)
                dve.wait_ge(sigmoided, 1)
                step(dve.tensor_tensor(biased[:, :, :], score[:, :, :], ebias[:, :].unsqueeze(1).to_broadcast([P, NT, E]), ALU.add))
                for t in range(NT):
                    ins = dve.max(best[:, t], biased[:, t])
                step(ins)
                step(dve.memset(best[:, :, TOPK:], NONE))
                for t in range(NT):
                    ins = dve.match_replace(left[:, t], best[:, t], biased[:, t], -NONE)
                step(ins)
                step(dve.tensor_tensor(chosen[:, :, :], left[:, :, :], biased[:, :, :], ALU.not_equal))
                dve.tensor_tensor(weight[:, :, :], chosen[:, :, :], score[:, :, :], ALU.mult).then_inc(chosen_ready, 1)
                dve.wait_ge(chosen_ready, 1)
                step(dve.tensor_reduce(wsum[:, :], weight[:, :, :], AX.X, ALU.add))
                step(dve.reciprocal(wsum[:, :], wsum[:, :]))
                step(dve.tensor_tensor(weight[:, :, :], weight[:, :, :], wsum[:, :].unsqueeze(2).to_broadcast([P, NT, E]), ALU.mult))

            def place():
                dve.tensor_copy(total[:, :, :], chosen[:, :, :]).then_inc(chosen_ready, 1)
                dve.wait_ge(chosen_ready, 2)
                order = prefix_sums(step, dve, total[:, :, :], psum_a[:, :, :], E)
                for k in range(TOPK):
                    ins = dve.scalar_tensor_tensor(out=picked[:, k], in0=order, scalar=float(k + 1), in1=chosen[:, :, :],
                                                   op0=ALU.is_equal, op1=ALU.mult)
                step(ins)
                dve.wait_ge(counted, 1)
                step(dve.tensor_copy(total[:, :, :].rearrange("p t e -> p (t e)"), p_total))
                dve.wait_ge(shapes_landed, 16)
                step(dve.tensor_copy(psum_b[:, :, :], total[:, :, :]))
                upto = prefix_sums(step, dve, psum_b[:, :, :].rearrange("p t e -> p e t"), psum_a[:, :, :].rearrange("p t e -> p e t"), NT)
                step(dve.tensor_scalar(ntiles[:, :], upto[:, :, NT - 1], 1.0 / SLOTS, 0.5 - 0.5 / SLOTS, ALU.mult, ALU.add))
                step(dve.tensor_scalar(ntiles[:, :], ntiles[:, :], ROUND, None, ALU.add))
                step(dve.tensor_scalar(ntiles[:, :], ntiles[:, :], -ROUND, None, ALU.add))
                step(dve.tensor_copy(ends[:, :], ntiles[:, :]))
                end = prefix_sums(step, dve, ends[:, :], ends_b[:, :], E)
                step(dve.tensor_tensor(passed[:, :, :], seq[0:1, 0:TILES].unsqueeze(2).to_broadcast([1, TILES, E]),
                                       end[0:1, :].unsqueeze(1).to_broadcast([1, TILES, E]), ALU.is_ge))
                step(dve.tensor_reduce(owner_f[:, :], passed[:, :, :], AX.X, ALU.add))
                dve.tensor_copy(owner[:, :], owner_f[:, :])
                step(dve.tensor_tensor(base[:, :], end, ntiles[:, :], ALU.subtract))
                step(dve.tensor_scalar(base[:, :], base[:, :], float(SLOTS), None, ALU.mult))
                step(dve.tensor_tensor(slot[:, :, :], upto.rearrange("p e t -> p t e"), total[:, :, :], ALU.subtract))
                step(dve.tensor_tensor(slot[:, :, :], slot[:, :, :], base[:, :].unsqueeze(1).to_broadcast([P, NT, E]), ALU.add))
                dve.tensor_tensor(slot[:, :, :], p_within.rearrange("p (t e) -> p t e", e=E), slot[:, :, :], ALU.add).then_inc(counts_read, 1)
                dve.wait_ge(counts_read, 1)
                for value, out in ((slot, slot_k), (weight, weight_k)):
                    step(dve.tensor_tensor(product_, picked, value[:, :, :].unsqueeze(1).to_broadcast([P, TOPK, NT, E]), ALU.mult))
                    step(dve.tensor_reduce(out[:, :, :], product_, AX.X, ALU.add))
                step(dve.tensor_scalar(half_k[:, :, :], slot_k[:, :, :], 1.0 / P, 0.5 / P - 0.5, ALU.mult, ALU.add))
                step(dve.tensor_scalar(half_r[:, :, :], half_k[:, :, :], ROUND, None, ALU.add))
                step(dve.tensor_scalar(half_k[:, :, :], half_r[:, :, :], -ROUND, None, ALU.add))
                step(dve.scalar_tensor_tensor(out=place_k[:, :, :], in0=half_k[:, :, :], scalar=-float(P), in1=slot_k[:, :, :],
                                              op0=ALU.mult, op1=ALU.add))
                step(dve.tensor_copy(weight_kh[:, :, :], weight_k[:, :, :]))
                by_entry = entry[:, :, :, :].rearrange("p t k v -> p k t v")
                dve.tensor_copy(by_entry[:, :, :, 0], token1.unsqueeze(1).to_broadcast([P, TOPK, NT]))
                dve.tensor_copy(by_entry[:, :, :, 1], weight_kh[:, :, :].bitcast(F32))
                step(dve.tensor_tensor(by_entry[:, :, :, 2], weight_k[:, :, :], weight_kh[:, :, :].bitcast(F32), ALU.subtract))

            def one_hots(t):
                i = t % 2
                wait(dve, tabled, t - 1)
                dve.tensor_tensor(at_place[i][:, :, :], seq.unsqueeze(1).to_broadcast([P, TOPK, P]),
                                  place_k[:, :, t].unsqueeze(2).to_broadcast([P, TOPK, P]), ALU.is_equal)
                dve.tensor_tensor(in_half[i][:, :, :], seq[:, 0:HALVES].unsqueeze(1).to_broadcast([P, TOPK, HALVES]),
                                  half_k[:, :, t].unsqueeze(2).to_broadcast([P, TOPK, HALVES]), ALU.is_equal).then_inc(onehot, 1)

            def read_tables():
                dve.wait_ge(tabled, NT)
                step(dve.tensor_copy(found[:, :], p_table[:, 0:HALVES]))
                step(dve.tensor_copy(share[:, :], p_table[:, HALVES:2 * HALVES]))
                step(dve.tensor_tensor(share[:, :], p_table[:, 2 * HALVES:], share[:, :], ALU.add))
                step(dve.tensor_scalar(index_f[:, :], found[:, :], -1.0, 0.0, ALU.add, ALU.max))
                step(dve.tensor_copy(source[:, :], index_f[:, :]))
                step(dve.tensor_scalar(spare_rows[:, :], found[:, :], 0.0, spare_row1, ALU.is_equal, ALU.mult))
                step(dve.scalar_tensor_tensor(out=index_f[:, :], in0=found[:, :], scalar=-1.0, in1=spare_rows[:, :], op0=ALU.add, op1=ALU.add))
                dve.tensor_copy(target[:, :], index_f[:, :])

            def gate(c):
                for m in range(MK):
                    dve.wait_ge(hidden, 2 * MK * c + 2 * m + 2)
                    dve.wait_ge(silued, MK * c + m + 1)
                    wait(dve, h_hi, MK * c)
                    wait(dve, h_lo, MK * c)
                    dve.tensor_tensor(hid[:, m], silu[:, m], banks[:, 2 * m + 1], ALU.mult).then_inc(gated, 1)
                for m in range(MK):
                    dve.wait_ge(h_hi, MK * c + m + 1)
                    dve.tensor_tensor(hid_l[c % 2][:, m], hid[:, m], hid_h[c % 2][:, m].bitcast(F32), ALU.subtract).then_inc(h_lo, 1)

            def add_down(c):
                for d in range(TPB * c, TPB * (c + 1)):
                    dve.wait_ge(down, d + 1)
                    dve.tensor_tensor(X[:, d], X[:, d], banks[:, 4 + d % DOWN_BANKS], ALU.add).then_inc(summed, 1)

            choose()
            gate(0)
            place()
            dve.wait_ge(rows_stored, 16)
            for c in range(NBLK):
                for t in range(c * NT // NBLK, (c + 1) * NT // NBLK):
                    one_hots(t)
                if c + 1 < NBLK:
                    gate(c + 1)
                add_down(c)
            read_tables()

        @block.tensor
        def _(pe):
            def product(out, pairs):
                terms = [t for lh, ll, rh, rl in pairs for t in ((lh, rl), (ll, rh), (lh, rh))]
                for i, (a, c) in enumerate(terms):
                    mm = pe.matmul(out, a, c, start=(i == 0), stop=(i == len(terms) - 1))
                return mm

            pe.wait_ge(consts, 4)
            pe.wait_ge(gw_hi, 1)
            pe.wait_ge(gw_lo, 1)
            for c in range(NBLK):
                s = slice(c * W, (c + 1) * W)
                product(banks[0:E, c], [(gw_h[:, k], gw_l[:, k], xh[:, k, s], xl[:, k, s]) for k in range(HK)]).then_inc(routed, 1)
            for t in range(NT):
                pe.wait_ge(lcopied, t * P // W + 1)
                mm = pe.transpose(banks[:, 4, t * E:(t + 1) * E], lcols[:, t * P:(t + 1) * P], ident[0:E, 0:E])
            mm.then_inc(lturned, 1)

            def hidden_block(c):
                s = slice(c * W, (c + 1) * W)
                for m in range(MK):
                    wait(pe, gated, MK * (c - 1) + m + 1)
                    for j in range(2):
                        f = slice(j * FF + m * P, j * FF + (m + 1) * P)
                        product(banks[:, 2 * m + j], [(gu_h[:, k, f], gu_l[:, k, f], xh[:, k, s], xl[:, k, s]) for k in range(HK)]).then_inc(hidden, 1)

            def down_block(c):
                pe.wait_ge(h_hi, MK * c + MK)
                pe.wait_ge(h_lo, MK * c + MK)
                for d in range(TPB * c, TPB * (c + 1)):
                    wait(pe, summed, d - DOWN_BANKS + 1)
                    s = slice(d % TPB * P, (d % TPB + 1) * P)
                    product(banks[:, 4 + d % DOWN_BANKS],
                            [(hid_h[c % 2][:, m, s], hid_l[c % 2][:, m, s], dn_h[:, m], dn_l[:, m]) for m in range(MK)]).then_inc(down, 1)

            def count():
                pe.wait_ge(chosen_ready, 1)
                pe.wait_ge(shapes_landed, 16)
                flags = chosen[:, :, :].rearrange("p t e -> p (t e)")
                pe.matmul(p_within, before, flags, start=True, stop=True)
                pe.matmul(p_total, ones[:, :], flags, start=True, stop=True).then_inc(counted, 1)

            def table(t):
                pe.wait_ge(entered, t + 1)
                i = t % 2
                for k in range(TOPK):
                    mm = pe.matmul(p_table, at_place[i][:, k], valued[i][:, k].rearrange("p v h -> p (v h)"),
                                   start=(t == 0 and k == 0), stop=(t == NT - 1 and k == TOPK - 1))
                mm.then_inc(tabled, 1)

            pe.wait_ge(lcopied, NBLK)
            pe.wait_ge(gu_hi, 1)
            pe.wait_ge(gu_lo, 1)
            hidden_block(0)
            count()
            pe.wait_ge(sigmoided, 1)
            pe.wait_ge(dn_hi, 1)
            pe.wait_ge(dn_lo, 1)
            for c in range(NBLK):
                if c + 1 < NBLK:
                    hidden_block(c + 1)
                if c == 0:
                    pe.wait_ge(counts_read, 1)
                for t in range(c * NT // NBLK, (c + 1) * NT // NBLK):
                    table(t)
                down_block(c)


def routed_experts(nc, X, scratch, w_gu, w_down, x_rows, sums, tables, out):
    source, target, share, owner = tables
    HALF = SLOTS // P
    MK = FF // P
    NBLK = 4
    TPB = NT // NBLK
    with ExitStack() as ctx:
        def sb(name, shape, dt=F32):
            return ctx.enter_context(nc.sbuf_tensor(name, shape, dt))

        def sem(name):
            return ctx.enter_context(nc.semaphore(name))

        flat = scratch[:, :, :].rearrange("p t h -> p (t h)")
        GU, DN = HK * 2 * FF, MK * HID
        gu_raw = [flat[:, i * GU:(i + 1) * GU].rearrange("p (k f) -> p k f", k=HK) for i in range(2)]
        dn_raw = [flat[:, 2 * GU + i * DN:2 * GU + (i + 1) * DN].rearrange("p (k h) -> p k h", k=MK) for i in range(2)]
        gu_h = [sb(f"gu_h{i}", [P, HK, 2 * FF], F32R) for i in range(2)]
        gu_l = [sb(f"gu_l{i}", [P, HK, 2 * FF], F32R) for i in range(2)]
        dn_h = [sb(f"dn_h{i}", [P, MK, HID], F32R) for i in range(2)]
        dn_l = [sb(f"dn_l{i}", [P, MK, HID], F32R) for i in range(2)]
        rows = [sb(f"rows{i}", [P, HALF, HID]) for i in range(2)]
        xt_h = [sb(f"xg_h{i}", [P, HK, SLOTS], F32R) for i in range(2)]
        xt_l = [sb(f"xg_l{i}", [P, HK, SLOTS], F32R) for i in range(2)]
        silu, hid = sb("silu", [P, MK * SLOTS]), sb("hid", [P, MK * SLOTS])
        hid_h = [sb(f"hid_h{i}", [P, MK, SLOTS], F32R) for i in range(2)]
        hid_l = [sb(f"hid_l{i}", [P, MK, SLOTS], F32R) for i in range(2)]
        result = [sb(f"result{i}", [P, HALF, HID]) for i in range(2)]
        from_row = [[sb(f"from_row{i}{u}", [P, 1], U32) for u in range(HALF)] for i in range(2)]
        to_row = [[sb(f"to_row{i}{u}", [P, 1], U32) for u in range(HALF)] for i in range(2)]
        ident = sb("ident6", [P, P])
        stats, mv, std = sb("stats6", [P, NT, 6]), sb("mv6", [P, NT, 2]), sb("std6", [P, NT])
        p_turn = ctx.enter_context(nc.psum_tensor("p_turn", [P, HK, SLOTS], F32))
        p_gate, p_up, *p_down = [ctx.enter_context(nc.psum_tensor(n, [P, HID], F32)) for n in ("p_gate", "p_up", "p_down0", "p_down1")]

        consts = sem("consts6")
        gu_landed, dn_landed = [sem("gu_landed0"), sem("gu_landed1")], [sem("dn_landed0"), sem("dn_landed1")]
        gathered = [sem("gathered0"), sem("gathered1")]
        from_ready, to_ready, scattered = sem("from_ready"), sem("to_ready"), [sem("scattered0"), sem("scattered1")]
        gu_hi, gu_lo, dn_hi, dn_lo = sem("gu_hi"), sem("gu_lo"), sem("dn_hi"), sem("dn_lo")
        x_turned, x_hi, x_lo = sem("xg_turned"), sem("xg_hi"), sem("xg_lo")
        hidden, silued, gated, h_hi, h_lo = (sem(n) for n in ("hidden", "silued", "gated", "h_hi", "h_lo"))
        down, weighed, summed = sem("down"), sem("weighed"), sem("summed")
        sums_landed = [sem(f"sums_landed{c}") for c in range(NBLK)]
        stat, shifted, rooted, inverted, normal, stored = (sem(n) for n in ("stat6", "shifted6", "rooted6", "inverted6", "normal6", "stored"))

        block = ctx.enter_context(nc.Block())

        def tiles(eng, body):
            body(0, 0, False)
            body(1, 1, False)
            with eng.Fori(1, TILES // 2 - 1) as p:
                for i in range(2):
                    body(2 * p + i, i, False)
            for j in range(TILES // 2 * 2 - 2, TILES):
                body(j, j % 2, j == TILES - 1)

        def landed(j, i, each):
            return each * (j // 2 + 1) if isinstance(j, int) else each // 2 * (j - i) + each

        def column(ap, j, u):
            return ap[:, HALF * j + u:HALF * j + u + 1] if isinstance(j, int) else ap[:, bass.ds(HALF * j + u, 1)]

        @block.sync
        def _(sp):
            sp.wait_ge(consts, 2)

            def body(j, i, last):
                number = owner[0:1, j:j + 1] if isinstance(j, int) else owner[0:1, bass.ds(j, 1)]
                e = sp.value_load(number, min_val=0, max_val=E)
                split_before = j - 1 if isinstance(j, int) else sp.to_reg(j - 1)
                sp.wait_ge(consts, 2)
                for s in (gu_hi, gu_lo, dn_hi, dn_lo):
                    wait(sp, s, split_before)
                sp.dma_start(gu_raw[i], w_gu[bass.ds(e, 1)].squeeze(0)).then_inc(gu_landed[i], 16)
                sp.dma_start(dn_raw[i], w_down[bass.ds(e, 1)].squeeze(0)).then_inc(dn_landed[i], 16)

            body(0, 0, False)
            body(1, 1, False)
            with sp.Fori(1, TILES // 2) as p:
                for i in range(2):
                    body(2 * p + i, i, False)
            for j in range(TILES // 2 * 2, TILES):
                body(j, j % 2, True)
            for u in range(HALF):
                sp.wait_ge(scattered[u], 16 * TILES)
            for c in range(NBLK):
                cols = slice(c * TPB, (c + 1) * TPB)
                for u, place in enumerate((X, scratch)):
                    sp.dma_start(place[:, cols], sums[u][0:T].rearrange("(t p) h -> p t h", p=P)[:, cols]).then_inc(sums_landed[c], 16)
            for c in range(NBLK):
                cols = slice(c * TPB, (c + 1) * TPB)
                sp.wait_ge(normal, TPB * (c + 1))
                sp.dma_start(out[:, cols], X[:, cols]).then_inc(stored, 16)
            sp.wait_ge(stored, 16 * NBLK)

        @block.gpsimd
        def _(pool):
            pool.memset(ident[:, :], 0.0).then_inc(consts, 1)
            pool.wait_ge(consts, 1)
            pool.affine_select(out=ident[:, :], in_=ident[:, :], compare_op=ALU.not_equal, fill=1.0,
                               base=0, pattern=[[-1, P]], channel_multiplier=1).then_inc(consts, 1)
            pool.wait_ge(consts, 2)

            def wait_row(sem_, value):
                if isinstance(value, int):
                    wait(pool, sem_, value)
                else:
                    wait_apart(pool, sem_, value, consts, 2)

            def gather(j, i):
                wait_row(x_turned, j - 1)
                for u in range(HALF):
                    ins = pool.tensor_copy(from_row[i][u][:, :], column(source, j, u))
                ins.then_inc(from_ready, 1)
                wait_row(from_ready, j + 1)
                for u in range(HALF):
                    pool.indirect_dma_start(rows[i][:, u], None, x_rows, bass.IndirectOffsetOnAxis(from_row[i][u][:, 0:1], 0)).then_inc(gathered[i], 16)

            def weights_lo(j, i):
                pool.wait_ge(gu_hi, j + 1)
                pool.tensor_tensor(gu_l[i][:, :, :], gu_raw[i], gu_h[i][:, :, :].bitcast(F32), ALU.subtract).then_inc(gu_lo, 1)

            def scatter(j, i):
                for u in range(HALF):
                    wait_row(scattered[u], 16 * j)
                for u in range(HALF):
                    ins = pool.tensor_copy(to_row[i][u][:, :], column(target, j, u))
                ins.then_inc(to_ready, 1)
                wait_row(to_ready, j + 1)
                wait_row(weighed, HALF * j + HALF)
                for u in range(HALF):
                    pool.indirect_dma_start(sums[u], bass.IndirectOffsetOnAxis(to_row[i][u][:, 0:1], 0), result[i][:, u], None,
                                            compute_op=ALU.add).then_inc(scattered[u], 16)

            gather(0, 0)
            weights_lo(0, 0)
            gather(1, 1)

            def body(j, i, last):
                if not isinstance(j, int) or j + 2 < TILES:
                    gather(j + 2, i)
                if not last:
                    weights_lo(j + 1, 1 - i)
                if not isinstance(j, int) or j:
                    scatter(j - 1, 1 - i)

            tiles(pool, body)
            scatter(TILES - 1, (TILES - 1) % 2)

        @block.scalar
        def _(act):
            def gu_split(j, i):
                act.wait_ge(gu_landed[i], landed(j, i, 16))
                wait(act, hidden, j - 1)
                act.copy(gu_h[i][:, :, :], gu_raw[i]).then_inc(gu_hi, 1)

            def dn_split(j, i):
                act.wait_ge(dn_landed[i], landed(j, i, 16))
                wait(act, down, HALF * (j - 1))
                act.copy(dn_h[i][:, :, :], dn_raw[i]).then_inc(dn_hi, 1)

            def x_split(j, i):
                act.wait_ge(x_turned, j + 1)
                wait(act, hidden, j - 1)
                act.copy(xt_h[i][:, :, :], p_turn[:, :, :]).then_inc(x_hi, 1)

            def root(c):
                act.wait_ge(shifted, c + 1)
                cols = slice(c * TPB, (c + 1) * TPB)
                act.sqrt(std[:, cols], std[:, cols]).then_inc(rooted, 1)

            gu_split(0, 0)
            x_split(0, 0)
            dn_split(0, 0)

            def body(j, i, last):
                if not last:
                    gu_split(j + 1, 1 - i)
                act.wait_ge(hidden, j + 1)
                wait(act, gated, j)
                act.activation(silu[:, :], p_gate[:, :], ACT.Silu).then_inc(silued, 1)
                if not last:
                    x_split(j + 1, 1 - i)
                act.wait_ge(gated, j + 1)
                wait(act, down, HALF * (j - 1))
                act.copy(hid_h[i][:, :, :].rearrange("p m s -> p (m s)"), hid[:, :]).then_inc(h_hi, 1)
                if not last:
                    dn_split(j + 1, 1 - i)

            tiles(act, body)
            for c in range(NBLK):
                root(c)

        @block.vector
        def _(dve):
            def dn_split(j, i):
                dve.wait_ge(dn_hi, j + 1)
                dve.tensor_tensor(dn_l[i][:, :, :], dn_raw[i], dn_h[i][:, :, :].bitcast(F32), ALU.subtract).then_inc(dn_lo, 1)

            def x_split(j, i):
                dve.wait_ge(x_hi, j + 1)
                dve.tensor_tensor(xt_l[i][:, :, :], p_turn[:, :, :], xt_h[i][:, :, :].bitcast(F32), ALU.subtract).then_inc(x_lo, 1)

            def weigh(j, i):
                for u in range(HALF):
                    wait(dve, scattered[u], 16 * (j - 1))
                    dve.wait_ge(down, HALF * j + u + 1)
                    dve.tensor_scalar(result[i][:, u], p_down[u][:, :], column(share, j, u), None, ALU.mult).then_inc(weighed, 1)

            def normalise(c):
                block_tiles, cols = range(c * TPB, (c + 1) * TPB), slice(c * TPB, (c + 1) * TPB)
                dve.wait_ge(sums_landed[c], 16 * HALF)
                for t in block_tiles:
                    dve.tensor_tensor(X[:, t], X[:, t], scratch[:, t], ALU.add).then_inc(summed, 1)
                for t in block_tiles:
                    dve.wait_ge(summed, t + 1)
                    dve.bn_stats(stats[:, t], X[:, t]).then_inc(stat, 1)
                dve.wait_ge(stat, TPB * (2 * c + 1))
                for t in block_tiles:
                    dve.bn_aggr(mv[:, t], stats[:, t]).then_inc(stat, 1)
                dve.wait_ge(stat, TPB * (2 * c + 2))
                dve.tensor_scalar(std[:, cols], mv[:, cols, 1], LN_EPS, None, ALU.add).then_inc(shifted, 1)
                dve.wait_ge(rooted, c + 1)
                dve.reciprocal(std[:, cols], std[:, cols]).then_inc(inverted, 1)
                dve.wait_ge(inverted, c + 1)
                for t in block_tiles:
                    dve.tensor_scalar(X[:, t], X[:, t], mv[:, t, 0:1], std[:, t:t + 1], ALU.subtract, ALU.mult).then_inc(normal, 1)

            x_split(0, 0)
            dn_split(0, 0)

            def body(j, i, last):
                dve.wait_ge(silued, j + 1)
                wait(dve, h_hi, j)
                wait(dve, h_lo, j)
                dve.tensor_tensor(hid[:, :], silu[:, :], p_up[:, :], ALU.mult).then_inc(gated, 1)
                if not last:
                    x_split(j + 1, 1 - i)
                dve.wait_ge(h_hi, j + 1)
                dve.tensor_tensor(hid_l[i][:, :, :].rearrange("p m s -> p (m s)"), hid[:, :],
                                  hid_h[i][:, :, :].rearrange("p m s -> p (m s)").bitcast(F32), ALU.subtract).then_inc(h_lo, 1)
                if not isinstance(j, int) or j:
                    weigh(j - 1, 1 - i)
                if not last:
                    dn_split(j + 1, 1 - i)

            tiles(dve, body)
            weigh(TILES - 1, (TILES - 1) % 2)
            for c in range(NBLK):
                normalise(c)

        @block.tensor
        def _(pe):
            def product(out, pairs):
                terms = [t for lh, ll, rh, rl in pairs for t in ((lh, rl), (ll, rh), (lh, rh))]
                for i, (a, c) in enumerate(terms):
                    mm = pe.matmul(out, a, c, start=(i == 0), stop=(i == len(terms) - 1))
                return mm

            def turn(j, i):
                pe.wait_ge(gathered[i], landed(j, i, 16 * HALF))
                wait(pe, x_lo, j)
                for u in range(HALF):
                    for k in range(HK):
                        mm = pe.transpose(p_turn[:, k, u * P:(u + 1) * P], rows[i][:, u, k * P:(k + 1) * P], ident[:, :])
                mm.then_inc(x_turned, 1)

            def hidden_tile(j, i):
                for s in (gu_hi, gu_lo, x_hi, x_lo):
                    pe.wait_ge(s, j + 1)
                wait(pe, gated, j)
                for part, bank in enumerate((p_gate, p_up)):
                    for m in range(MK):
                        f = slice(part * FF + m * P, part * FF + (m + 1) * P)
                        mm = product(bank[:, m * SLOTS:(m + 1) * SLOTS],
                                     [(gu_h[i][:, k, f], gu_l[i][:, k, f], xt_h[i][:, k], xt_l[i][:, k]) for k in range(HK)])
                mm.then_inc(hidden, 1)

            def down_tile(j, i):
                for s in (h_hi, h_lo, dn_hi, dn_lo):
                    pe.wait_ge(s, j + 1)
                wait(pe, weighed, HALF * j)
                for u in range(HALF):
                    s = slice(u * P, (u + 1) * P)
                    product(p_down[u][:, :], [(hid_h[i][:, m, s], hid_l[i][:, m, s], dn_h[i][:, m], dn_l[i][:, m]) for m in range(MK)]).then_inc(down, 1)

            pe.wait_ge(consts, 2)
            turn(0, 0)

            def body(j, i, last):
                hidden_tile(j, i)
                if not last:
                    turn(j + 1, 1 - i)
                if not isinstance(j, int) or j:
                    down_tile(j - 1, 1 - i)

            tiles(pe, body)
            down_tile(TILES - 1, (TILES - 1) % 2)


def decoder_layer(nc, x_cols, x_tok, w_qkv, b_q, b_kv, w_attn_out, ctx_cols, pos, w_q, w_k, w_v, w_out, b_out,
                  gate_cols, expert_bias, w_gu, w_down, shape_consts, x_rows, sums_first, sums_second, out):
    with ExitStack() as ctx:
        def sb(name, shape, dt=F32):
            return ctx.enter_context(nc.sbuf_tensor(name, shape, dt))

        X = sb("X", [P, NT, HID])
        linear_attention(nc, X, x_cols, x_tok, w_qkv, b_q, b_kv, w_attn_out)
        Q = sb("Q", [P, NT, HID])
        with ExitStack() as inner:
            K = inner.enter_context(nc.sbuf_tensor("K", [P, NT, HID], F32))
            V = inner.enter_context(nc.sbuf_tensor("V", [P, NT, XH, XD + 1], F32))
            project_context(nc, X, Q, K, V, ctx_cols, pos, w_q, w_k, w_v)
            softmax_attention(nc, X, Q, K, V, b_out)
        sums = sums_first, sums_second
        HALVES = TILES * SLOTS // P
        tables = sb("source", [P, HALVES], U32), sb("target", [P, HALVES], U32), sb("share", [P, HALVES]), sb("owner", [1, TILES], I32)
        with ExitStack() as inner:
            xh = inner.enter_context(nc.sbuf_tensor("x2h", [P, HK, T], F32R))
            xl = inner.enter_context(nc.sbuf_tensor("x2l", [P, HK, T], F32R))
            project_attention(nc, X, Q, xh, xl, w_out)
            route_and_share(nc, X, Q, xh, xl, gate_cols, expert_bias, w_gu, w_down, shape_consts, x_rows, sums, tables)
        routed_experts(nc, X, Q, w_gu, w_down, x_rows, sums, tables, out)


def kernel(**inputs):
    import concourse.bacc as _bacc
    from concourse.bass_utils import run_bass_kernel_spmd as _run

    a = {name: np.asarray(value) for name, value in inputs.items()}

    def rows(w):
        return w.reshape(-1, P, w.shape[-1]).transpose(1, 0, 2)

    def rotary(w):
        return w.reshape(w.shape[0], XH, 2, XD // 4, 2).transpose(0, 1, 4, 2, 3).reshape(w.shape)

    x = a["x"].reshape(T, HID)
    grouped = [a["L0_attn_Wq"].reshape(KVG, GROUP * DH, HID), a["L0_attn_Wk"].reshape(KVG, DH, HID),
               a["L0_attn_Wv"].reshape(KVG, DH, HID)]
    b_kv = np.concatenate([a["L0_attn_bk"].reshape(KVG, DH), a["L0_attn_bv"].reshape(KVG, DH)], 1)
    w_kv = a["L0_xattn_Wkv"]
    gate = np.concatenate([a["L0_ffn_w_gate"], a["L0_ffn_sw_gate"][None]])
    up = np.concatenate([a["L0_ffn_w_up"], a["L0_ffn_sw_up"][None]])
    down = np.concatenate([a["L0_ffn_w_down"], a["L0_ffn_sw_down"][None]])
    count = np.arange(P, dtype=np.float32)
    shape_consts = np.concatenate([np.tile(count, (P, 1)), (count[:, None] < count).astype(np.float32),
                                   1 + count[:, None] + P * np.arange(NT, dtype=np.float32), T + 1 + count[:, None]], 1)
    laid = {
        "x_cols": rows(x.T),
        "x_tok": rows(x),
        "w_qkv": np.concatenate(grouped, 1).transpose(0, 2, 1).reshape(KVG, HK, P, -1).transpose(0, 2, 1, 3),
        "b_q": a["L0_attn_bq"].reshape(KVG, GROUP, DH).transpose(2, 0, 1),
        "b_kv": b_kv.reshape(-1),
        "w_attn_out": a["L0_attn_Wo"].T.reshape(KVG, GROUP, P, HID).transpose(0, 2, 1, 3),
        "ctx_cols": rows(a["ctx_1024"].reshape(T, CTX).T),
        "pos": rows(a["fside_BxSx2_0"].reshape(T, 2)),
        "w_q": rows(rotary(a["L0_xattn_Wq"])),
        "w_k": rows(rotary(w_kv[:, :HID])),
        "w_v": rows(w_kv[:, HID:]),
        "w_out": rows(a["L0_xattn_Wout"]),
        "b_out": a["L0_xattn_bout"],
        "gate_cols": rows(a["L0_ffn_gate_w"].T),
        "expert_bias": a["L0_ffn_expert_bias"],
        "w_gu": np.concatenate([gate, up], 1).transpose(0, 2, 1).reshape(E + 1, HK, P, 2 * FF).transpose(0, 2, 1, 3),
        "w_down": down.transpose(0, 2, 1).reshape(E + 1, FF // P, P, HID).transpose(0, 2, 1, 3),
        "shape_consts": shape_consts.astype(np.float32),
    }
    nc = _bacc.Bacc("TRN2", target_bir_lowering=False, num_devices=1)
    arrays, args = {}, []
    for name, value in laid.items():
        arrays[f"in_{name}"] = np.ascontiguousarray(value)
        args.append(nc.dram_tensor(f"in_{name}", value.shape, mybir.dt.from_np(value.dtype), kind="ExternalInput").ap())
    args.append(nc.dram_tensor("x_rows", (T, HID), F32, kind="Internal").ap())
    for name in ("sums_first", "sums_second"):
        args.append(nc.dram_tensor(name, (T + P, HID), F32, kind="Internal").ap())
    args.append(nc.dram_tensor("out_x", (P, NT, HID), F32, kind="ExternalOutput").ap())
    decoder_layer(nc, *args)
    got = _run(nc, [arrays], core_ids=[0]).results[0]["out_x"]
    return got.transpose(1, 0, 2).reshape(B, S, HID)
```
